# Optimizing a Trainium2 kernel written in Bass

```python
import numpy as np
import jax
import jax.numpy as jnp

def _softmax(x, axis=-1):
    return jax.nn.softmax(x, axis=axis)

def _gelu(x):
    return jax.nn.gelu(x, approximate=True)

def _silu(x):
    return jax.nn.silu(x)

def _sigmoid(x):
    return jax.nn.sigmoid(x)

def _layernorm(x, axis=-1, eps=1e-05):
    m = jnp.mean(x, axis=axis, keepdims=True)
    v = jnp.var(x, axis=axis, keepdims=True)
    return (x - m) / jnp.sqrt(v + eps)

def _scatter_add(tgt, idx, src, axis=0):
    return tgt.at[idx].add(src)

def _segment_sum(src, seg, n):
    return jax.ops.segment_sum(src, seg, n)
kernel_name = 'mk_xattn_ffn_d1_seqx_r8_701e8e'

def setup_inputs(seed: int=0):
    np.random.seed(seed)
    _w = jnp.asarray

    def _rec_inputs():
        import jax
        import jax.numpy as jnp
        _rk = jax.random.key(seed)
        x = -0.000125 + 0.9999 * jax.random.normal(jax.random.fold_in(_rk, 1), (4, 256, 256), jnp.float32)
        _lenS = 256 - jax.random.randint(jax.random.fold_in(_rk, 7), (4,), 0, max(1, 256 // 4) + 1, jnp.int32)
        _lenS2 = 256 - jax.random.randint(jax.random.fold_in(_rk, 8), (4,), 0, max(1, 256 // 4) + 1, jnp.int32)
        _ctx_2048P = jax.random.normal(jax.random.fold_in(_rk, 11), (4, 16, 256), jnp.float32)
        _ctx_2048c = jax.random.dirichlet(jax.random.fold_in(_rk, 511), 0.3 * jnp.ones((16,), jnp.float32), (4, 256))
        _ctx_2048t = jnp.einsum('bsk,bkd->bsd', _ctx_2048c, _ctx_2048P)
        _ctx_2048t = _ctx_2048t * jax.lax.rsqrt(jnp.mean(jnp.square(_ctx_2048t)) + 1e-12) * 0.953939
        ctx_2048 = -1.52775e-05 + 0.999936 * (_ctx_2048t + 0.3 * jax.random.normal(jax.random.fold_in(_rk, 611), (4, 256, 256), jnp.float32))
        _validS = jnp.arange(256)[None, :] < _lenS[:, None]
        _validS2 = jnp.arange(256)[None, :] < _lenS2[:, None]
        _causal = jnp.tril(jnp.ones((256, 256), dtype=bool))
        mask_BxS2_ff1 = jnp.where(jnp.ones((4, 256), dtype=bool), 1.0, 0.0).astype(jnp.float32)
        return (x, ctx_2048, mask_BxS2_ff1)
    x, ctx_2048, mask_BxS2_ff1 = _rec_inputs()

    def _L0_xattn_setup():
        import jax, jax.numpy as jnp
        import numpy as np
        H = 256
        NH = 16
        HD = H // NH
        FD = 64
        key = jax.random.key(seed)
        ks = jax.random.split(key, 12)
        B, S = (4, 512)
        s = 1.0 / np.sqrt(H)
        sf = 1.0 / np.sqrt(HD)
        return {'query': jax.random.normal(ks[0], (B, S, H), jnp.float32), 'key': jax.random.normal(ks[1], (B, S, H), jnp.float32), 'value': jax.random.normal(ks[2], (B, S, H), jnp.float32), 'attention_mask': jnp.ones((B, S), jnp.float32), 'Wq': jax.random.normal(ks[3], (H, H), jnp.float32) * s, 'bq': jnp.zeros((H,), jnp.float32), 'Wk': jax.random.normal(ks[4], (H, H), jnp.float32) * s, 'bk': jnp.zeros((H,), jnp.float32), 'Wv': jax.random.normal(ks[5], (H, H), jnp.float32) * s, 'bv': jnp.zeros((H,), jnp.float32), 'Wqf': jax.random.normal(ks[6], (FD, HD), jnp.float32) * sf, 'Wkf': jax.random.normal(ks[7], (FD, HD), jnp.float32) * sf, 'Wo': jax.random.normal(ks[8], (H, H), jnp.float32) * s, 'bo': jnp.zeros((H,), jnp.float32)}
    _L0_xattn_all = _L0_xattn_setup()
    _L0_xattn_in = {k: v for k, v in _L0_xattn_all.items() if k in ('Wq', 'bq', 'Wk', 'bk', 'Wv', 'bv', 'Wqf', 'Wkf', 'Wo', 'bo')}
    del _L0_xattn_all

    def _L0_ffn_setup():
        import jax, jax.numpy as jnp
        import numpy as np
        from jax import lax
        DIM = 256
        E = 8
        K = 2
        RANK = 32
        CAP_FACTOR = 1.25

        def gelu(x):
            return jax.nn.gelu(x, approximate=False)

        def _moe_forward(x, gate_w, w1, b1, w2, b2, wd, wu, sw1, sb1, sw2, sb2, swd, swu):
            B, S, D = x.shape
            T = B * S
            cap = max(1, int(T * CAP_FACTOR / E))
            xt = x.reshape(T, D)
            logits = xt @ gate_w
            probs_full = jax.nn.softmax(logits, axis=-1)
            top_p, top_i = lax.top_k(probs_full, K)
            out = jnp.zeros_like(xt)
            for k in range(K):
                e = top_i[:, k]
                w = top_p[:, k]
                onehot = jax.nn.one_hot(e, E, dtype=jnp.int32)
                pos_all = jnp.cumsum(onehot, axis=0) - 1
                pos = jnp.take_along_axis(pos_all, e[:, None], axis=1)[:, 0]
                keep = pos < cap
                pos_c = jnp.where(keep, pos, cap)
                buf = jnp.zeros((E, cap, D), x.dtype).at[e, pos_c].set(xt * keep[:, None].astype(x.dtype), mode='drop')
                h = gelu(jnp.einsum('ecd,edf->ecf', buf, w1) + b1[:, None, :])
                y = jnp.einsum('ecf,efd->ecd', h, w2) + b2[:, None, :]
                a = jnp.einsum('ecr,erd->ecd', gelu(jnp.einsum('ecd,edr->ecr', buf, wd)), wu)
                y = y + a
                tok = y[e, jnp.minimum(pos_c, cap - 1)]
                out = out + tok * keep[:, None].astype(x.dtype) * w[:, None]
            sh = gelu(xt @ sw1 + sb1) @ sw2 + sb2
            sh = sh + gelu(xt @ swd) @ swu
            out = out + 0.2 * sh
            return out.reshape(B, S, D)
        key = jax.random.key(seed)
        ks = jax.random.split(key, 16)
        s = 0.02
        d, h = (DIM, 4 * DIM)
        inp = {'x': jax.random.normal(ks[0], (4, 256, d), dtype=jnp.float32), 'gate_w': jax.random.normal(ks[1], (d, E), dtype=jnp.float32) * s, 'w1': jax.random.normal(ks[2], (E, d, h), dtype=jnp.float32) * s, 'b1': jnp.zeros((E, h), dtype=jnp.float32), 'w2': jax.random.normal(ks[3], (E, h, d), dtype=jnp.float32) * s, 'b2': jnp.zeros((E, d), dtype=jnp.float32), 'wd': jax.random.normal(ks[4], (E, d, RANK), dtype=jnp.float32) * s, 'wu': jax.random.normal(ks[5], (E, RANK, d), dtype=jnp.float32) * s, 'sw1': jax.random.normal(ks[6], (d, h), dtype=jnp.float32) * s, 'sb1': jnp.zeros((h,), dtype=jnp.float32), 'sw2': jax.random.normal(ks[7], (h, d), dtype=jnp.float32) * s, 'sb2': jnp.zeros((d,), dtype=jnp.float32), 'swd': jax.random.normal(ks[8], (d, RANK), dtype=jnp.float32) * s, 'swu': jax.random.normal(ks[9], (RANK, d), dtype=jnp.float32) * s}
        return inp
    _L0_ffn_all = _L0_ffn_setup()
    _L0_ffn_in = {k: v for k, v in _L0_ffn_all.items() if k in ('gate_w', 'w1', 'b1', 'w2', 'b2', 'wd', 'wu', 'sw1', 'sb1', 'sw2', 'sb2', 'swd', 'swu')}
    del _L0_ffn_all
    return {'x': x, 'ctx_2048': ctx_2048, 'mask_BxS2_ff1': mask_BxS2_ff1, 'L0_xattn_Wq': _L0_xattn_in['Wq'], 'L0_xattn_bq': _L0_xattn_in['bq'], 'L0_xattn_Wk': _L0_xattn_in['Wk'], 'L0_xattn_bk': _L0_xattn_in['bk'], 'L0_xattn_Wv': _L0_xattn_in['Wv'], 'L0_xattn_bv': _L0_xattn_in['bv'], 'L0_xattn_Wqf': _L0_xattn_in['Wqf'], 'L0_xattn_Wkf': _L0_xattn_in['Wkf'], 'L0_xattn_Wo': _L0_xattn_in['Wo'], 'L0_xattn_bo': _L0_xattn_in['bo'], 'L0_ffn_gate_w': _L0_ffn_in['gate_w'], 'L0_ffn_w1': _L0_ffn_in['w1'], 'L0_ffn_b1': _L0_ffn_in['b1'], 'L0_ffn_w2': _L0_ffn_in['w2'], 'L0_ffn_b2': _L0_ffn_in['b2'], 'L0_ffn_wd': _L0_ffn_in['wd'], 'L0_ffn_wu': _L0_ffn_in['wu'], 'L0_ffn_sw1': _L0_ffn_in['sw1'], 'L0_ffn_sb1': _L0_ffn_in['sb1'], 'L0_ffn_sw2': _L0_ffn_in['sw2'], 'L0_ffn_sb2': _L0_ffn_in['sb2'], 'L0_ffn_swd': _L0_ffn_in['swd'], 'L0_ffn_swu': _L0_ffn_in['swu']}

def reference(x, ctx_2048, mask_BxS2_ff1, L0_xattn_Wq, L0_xattn_bq, L0_xattn_Wk, L0_xattn_bk, L0_xattn_Wv, L0_xattn_bv, L0_xattn_Wqf, L0_xattn_Wkf, L0_xattn_Wo, L0_xattn_bo, L0_ffn_gate_w, L0_ffn_w1, L0_ffn_b1, L0_ffn_w2, L0_ffn_b2, L0_ffn_wd, L0_ffn_wu, L0_ffn_sw1, L0_ffn_sb1, L0_ffn_sw2, L0_ffn_sb2, L0_ffn_swd, L0_ffn_swu):
    import jax
    import jax.numpy as jnp

    def _L0_xattn_ref(query, key, value, attention_mask, Wq, bq, Wk, bk, Wv, bv, Wqf, Wkf, Wo, bo):
        import jax, jax.numpy as jnp
        import numpy as np
        H = 256
        NH = 16
        HD = H // NH
        FD = 64
        B, Sq, _ = query.shape
        Sk = key.shape[1]

        def heads(x, W, b, S):
            return (x @ W.T + b).reshape(B, S, NH, HD).transpose(0, 2, 1, 3)
        q = heads(query, Wq, bq, Sq)
        k = heads(key, Wk, bk, Sk)
        v = heads(value, Wv, bv, Sk)
        q_prime = jax.nn.relu(jnp.einsum('bhnd,fd->bhnf', q, Wqf))
        k_prime = jax.nn.relu(jnp.einsum('bhnd,fd->bhnf', k, Wkf))
        k_prime = k_prime * attention_mask[:, None, :, None]
        kv = jnp.einsum('bhnf,bhne->bhfe', k_prime, v)
        qkv = jnp.einsum('bhmf,bhfe->bhme', q_prime, kv)
        k_sum = jnp.sum(k_prime, axis=2)
        qk_sum = jnp.einsum('bhmf,bhf->bhm', q_prime, k_sum)[..., None]
        out = qkv / (qk_sum + 1e-08)
        out = out.transpose(0, 2, 1, 3).reshape(B, Sq, H)
        return out @ Wo.T + bo

    def _L0_ffn_ref(x, gate_w, w1, b1, w2, b2, wd, wu, sw1, sb1, sw2, sb2, swd, swu):
        import jax, jax.numpy as jnp
        import numpy as np
        from jax import lax
        DIM = 256
        E = 8
        K = 2
        RANK = 32
        CAP_FACTOR = 1.25

        def gelu(x):
            return jax.nn.gelu(x, approximate=False)

        def _moe_forward(x, gate_w, w1, b1, w2, b2, wd, wu, sw1, sb1, sw2, sb2, swd, swu):
            B, S, D = x.shape
            T = B * S
            cap = max(1, int(T * CAP_FACTOR / E))
            xt = x.reshape(T, D)
            logits = xt @ gate_w
            probs_full = jax.nn.softmax(logits, axis=-1)
            top_p, top_i = lax.top_k(probs_full, K)
            out = jnp.zeros_like(xt)
            for k in range(K):
                e = top_i[:, k]
                w = top_p[:, k]
                onehot = jax.nn.one_hot(e, E, dtype=jnp.int32)
                pos_all = jnp.cumsum(onehot, axis=0) - 1
                pos = jnp.take_along_axis(pos_all, e[:, None], axis=1)[:, 0]
                keep = pos < cap
                pos_c = jnp.where(keep, pos, cap)
                buf = jnp.zeros((E, cap, D), x.dtype).at[e, pos_c].set(xt * keep[:, None].astype(x.dtype), mode='drop')
                h = gelu(jnp.einsum('ecd,edf->ecf', buf, w1) + b1[:, None, :])
                y = jnp.einsum('ecf,efd->ecd', h, w2) + b2[:, None, :]
                a = jnp.einsum('ecr,erd->ecd', gelu(jnp.einsum('ecd,edr->ecr', buf, wd)), wu)
                y = y + a
                tok = y[e, jnp.minimum(pos_c, cap - 1)]
                out = out + tok * keep[:, None].astype(x.dtype) * w[:, None]
            sh = gelu(xt @ sw1 + sb1) @ sw2 + sb2
            sh = sh + gelu(xt @ swd) @ swu
            out = out + 0.2 * sh
            return out.reshape(B, S, D)
        return _moe_forward(x, gate_w, w1, b1, w2, b2, wd, wu, sw1, sb1, sw2, sb2, swd, swu)
    x = x + _L0_xattn_ref(_layernorm(x, axis=-1), ctx_2048, ctx_2048, mask_BxS2_ff1, L0_xattn_Wq, L0_xattn_bq, L0_xattn_Wk, L0_xattn_bk, L0_xattn_Wv, L0_xattn_bv, L0_xattn_Wqf, L0_xattn_Wkf, L0_xattn_Wo, L0_xattn_bo)
    x = x + _L0_ffn_ref(_layernorm(x, axis=-1), L0_ffn_gate_w, L0_ffn_w1, L0_ffn_b1, L0_ffn_w2, L0_ffn_b2, L0_ffn_wd, L0_ffn_wu, L0_ffn_sw1, L0_ffn_sb1, L0_ffn_sw2, L0_ffn_sb2, L0_ffn_swd, L0_ffn_swu)
    return x

_drawn_inputs = setup_inputs


def setup_inputs(seed=0):
    import zlib

    import numpy as np

    out = dict(_drawn_inputs(seed))
    spreads = {'L0_xattn_bq': (0.0, 0.8),
     'L0_xattn_bk': (0.0, 0.8),
     'L0_xattn_bv': (0.0, 0.1),
     'L0_xattn_bo': (0.0, 0.1),
     'L0_ffn_b1': (0.0, 0.8),
     'L0_ffn_b2': (0.0, 0.38),
     'L0_ffn_sb1': (0.0, 0.8),
     'L0_ffn_sb2': (0.0, 0.424)}
    factors = {'L0_ffn_wd': 8.0,
     'L0_ffn_wu': 8.0,
     'L0_ffn_sw1': 2.961,
     'L0_ffn_sw2': 2.724,
     'L0_ffn_swd': 8.0,
     'L0_ffn_swu': 8.0}
    for name, (base, spread) in spreads.items():
        noise = np.random.default_rng([zlib.crc32(name.encode()), seed]).standard_normal(out[name].shape)
        drawn = base * np.exp(spread * noise) if base else spread * noise
        out[name] = jnp.asarray(drawn.astype(out[name].dtype))
    for name, factor in factors.items():
        out[name] = (out[name] * factor).astype(out[name].dtype)
    return out
```

```python
from contextlib import ExitStack

import numpy as np

import concourse.bass as bass
from concourse import mybir

ACT = mybir.ActivationFunctionType
ALU = mybir.AluOpType
AX_X = mybir.AxisListType.X
F32 = mybir.dt.float32
F32R = mybir.dt.float32r
BF16 = mybir.dt.bfloat16
I32 = mybir.dt.int32

P = 128
B, S, D = 4, 256, 256
T = B * S
TT = S // P
NT = T // P
KD = D // P
NH, HD, FD = 16, 16, 64
E = 8
CAP = int(T * 1.25 / E)
SLOTS = 2 * CAP
ST = 4
SP = SLOTS // ST
FH = 1024
MH = FH // P
RANK = 32
LN_EPS = 1e-5
DEN_EPS = 1e-8
META = 4
ROW = D + META
NOWHERE = 1 << 20
CH = 1024
AD = KD * RANK + D
AP3 = 3 * RANK
NB = 10
BQ, BK, MK = NB, NB + 2, NB + 4
BCOLS = MK + NT
C_ID, C_MASK, C_TRI, C_ONE, C_RANK, C_BASE = 0, 128, 384, 512, 640, 704
CCOLS = C_BASE + 2 * NT
NG = MH + 1
FIRST, LAST = 3, 11


def attention_groups():
    inputs = lambda b: [("tc", b, 0), ("tx", b, 0), ("k", b, 0), ("v", b, 0), ("q", b, 0)]
    order = inputs(0)
    for b in range(B):
        order += [("kf", b, j) for j in range(4)]
        if b:
            order += [("wo", b - 1, 0)]
        order += [("qf", b, j) for j in range(4)]
        if b:
            order += [("t2", b - 1, 0)]
        order += [("kv", b, j) for j in range(2)] + [("tkv", b, j) for j in range(2)]
        if b + 1 < B:
            order += inputs(b + 1)
        order += [("qkv", b, j) for j in range(2)]
    order += [("wo", B - 1, 0)]
    bank = [n % 8 for n in range(len(order))]
    order += [("t2", B - 1, 0), ("lg", 0, 0), ("lg", 1, 0), ("tlg", 0, 0), ("pos", 0, 0)]
    bank += [5, 6, 7, 5, 6]
    return order, bank


def build_program(nc, x, ctx, attw, wch, adw, gw, bcol_d, bexp_d, brow_d, cst_d, dest_d, pre_d, xbuf, ybuf, out):
    ORDER, BANK = attention_groups()
    AT = {g: n for n, g in enumerate(ORDER)}

    with ExitStack() as stack:
        def sb(name, shape, dt, on=stack):
            return on.enter_context(nc.sbuf_tensor(name, shape, dt))

        def sem(name):
            return stack.enter_context(nc.semaphore(name))

        ps = [stack.enter_context(nc.psum_tensor(f"bank{i}", [P, 512], F32)) for i in range(8)]

        cst = sb("cst", [P, CCOLS], F32)
        ident = cst[:, C_ID:C_ID + P]
        tri_ones = sb("tri_ones", [P, 2 * P], BF16)
        ones = sb("ones", [P, FD], F32)
        bcol = sb("bcol", [P, BCOLS], F32)
        brow = sb("brow", [P, 3, D], F32)
        dest = sb("dest", [P, NT, 2], I32)
        gate_raw = sb("gate_raw", [P, KD, P], F32)
        gate_hi = sb("gate_hi", [P, KD, P], F32R)
        gate_lo = sb("gate_lo", [P, KD, P], F32R)
        res = sb("res", [P, NT, D], F32)
        rows = sb("rows", [P, NT, ROW], F32)
        xt_hi = sb("xt_hi", [P, KD, T], F32R)
        xt_lo = sb("xt_lo", [P, KD, T], F32R)
        raw = [sb(f"raw{q}", [P, CH], F32) for q in range(4)]
        raw_ad = sb("raw_ad", [P, AD], F32)
        sw_hi = [sb(f"sw_hi{q}", [P, CH], F32R) for q in range(4)]
        sw_lo = [sb(f"sw_lo{q}", [P, CH], F32R) for q in range(4)]
        sdn_hi = sb("sdn_hi", [P, KD, 3, RANK], F32R)
        sdn_lo = sb("sdn_lo", [P, KD, 3, RANK], F32R)
        sup = sb("sup", [AP3, D], F32R)
        lg = sb("lg", [P, NT, E], F32)
        z = sb("z", [P, NT, E], F32)
        hot = sb("hot", [P, NT, 2, E], F32)
        hot_bf = sb("hot_bf", [P, NT, 2, E], BF16)
        tmp16 = sb("tmp16", [P, NT, 2, E], F32)
        top = sb("top", [P, 2, NT], F32)
        rank = sb("rank", [P, NT, 2], F32)
        place = sb("place", [P, NT, 2], F32)
        slot = sb("slot", [P, NT, 2], F32)
        slot_i = sb("slot_i", [P, NT, 2], I32)
        pre = sb("pre", [P, ROW], F32)
        tmp_exp = sb("tmp_exp", [P, NT, E], F32)
        esum = sb("esum", [P, 3, NT], F32)
        stats2 = sb("stats2", [P, TT, 6], F32)
        mv2 = sb("mv2", [P, TT, 2], F32)
        sd2 = sb("sd2", [P, TT], F32)
        rstd2 = sb("rstd2", [P, TT], F32)
        nmr2 = sb("nmr2", [P, TT], F32)

        att = ExitStack()
        aw_hi = [sb(f"aw_hi{i}", [P, CH], F32R, att) for i in range(3)]
        aw_lo = [sb(f"aw_lo{i}", [P, CH], F32R, att) for i in range(3)]
        ctx_sb = [sb(f"ctx{i}", [P, TT, D], F32, att) for i in range(2)]
        xn = sb("xn", [P, TT, D], F32, att)
        stats = sb("stats", [P, TT, 6], F32, att)
        mv = sb("mv", [P, TT, 2], F32, att)
        sd = sb("sd", [P, TT], F32, att)
        rstd = sb("rstd", [P, TT], F32, att)
        nmr = sb("nmr", [P, TT], F32, att)
        mask_hi = sb("mask_hi", [P, NT], F32R, att)
        mask_lo = sb("mask_lo", [P, NT], F32, att)
        ct_hi, ct_lo = sb("ct_hi", [P, KD, S], F32R, att), sb("ct_lo", [P, KD, S], F32R, att)
        nt_hi, nt_lo = sb("nt_hi", [P, KD, S], F32R, att), sb("nt_lo", [P, KD, S], F32R, att)
        k_hi, k_lo = sb("k_hi", [P, KD, S], F32R, att), sb("k_lo", [P, KD, S], F32R, att)
        q_hi, q_lo = sb("q_hi", [P, KD, S], F32R, att), sb("q_lo", [P, KD, S], F32R, att)
        v32 = sb("v32", [P, TT, D], F32, att)
        v_hi = sb("v_hi", [P, TT, 4, P], F32R, att)
        v_lo = sb("v_lo", [P, TT, 4, P], F32R, att)
        kf_hi, kf_lo = sb("kf_hi", [P, TT, 2, 512], F32R, att), sb("kf_lo", [P, TT, 2, 512], F32R, att)
        qf_hi, qf_lo = sb("qf_hi", [P, 8, S], F32R, att), sb("qf_lo", [P, 8, S], F32R, att)
        kvm = sb("kvm", [P, 4, S], F32, att)
        kvt_hi, kvt_lo = sb("kvt_hi", [P, 8, P], F32R, att), sb("kvt_lo", [P, 8, P], F32R, att)
        den = sb("den", [FD, 2 * S], F32, att)
        rden = sb("rden", [FD, 2 * S], F32, att)
        o32 = sb("o32", [P, KD, S], F32, att)
        o_hi, o_lo = sb("o_hi", [P, KD, S], F32R, att), sb("o_lo", [P, KD, S], F32R, att)
        att.close()

        ffn = ExitStack()
        h_hi, h_lo = sb("h_hi", [P, MH, SLOTS], F32R, ffn), sb("h_lo", [P, MH, SLOTS], F32R, ffn)
        h32 = [sb(f"h32_{i}", [P, SLOTS], F32, ffn) for i in range(3)]
        a_st = sb("a_st", [AP3, SLOTS], F32R, ffn)
        ew_hi = [sb(f"ew_hi{q}", [P, CH], F32R, ffn) for q in range(4)]
        ew_lo = [sb(f"ew_lo{q}", [P, CH], F32R, ffn) for q in range(4)]
        dn_hi = sb("dn_hi", [P, KD, 3, RANK], F32R, ffn)
        dn_lo = sb("dn_lo", [P, KD, 3, RANK], F32R, ffn)
        up = sb("up", [AP3, D], F32R, ffn)
        bexp = [sb(f"bexp{i}", [P, NB], F32, ffn) for i in range(2)]
        xg = [sb(f"xg{i}", [SP, ST, D], F32, ffn) for i in range(2)]
        meta = [sb(f"meta{i}", [SP, ST, META], F32, ffn) for i in range(2)]
        xe_hi, xe_lo = sb("xe_hi", [P, KD, SLOTS], F32R, ffn), sb("xe_lo", [P, KD, SLOTS], F32R, ffn)
        ye = sb("ye", [P, KD, SLOTS], F32, ffn)
        yw = [sb(f"yw{i}", [SP, ST, D], F32, ffn) for i in range(2)]
        yk = sb("yk", [P, 2, NT, D], F32, ffn)
        lgt = sb("lgt", [E, T], F32, ffn)
        ffn.close()

        cst_ld, bcol_ld, brow_ld = sem("cst_ld"), sem("bcol_ld"), sem("brow_ld")
        misc_ld = sem("misc_ld")
        pre_ld = sem("pre_ld")
        x_in = [sem(f"x_in{b}") for b in range(B)]
        ctx_in = [sem(f"ctx_in{b}") for b in range(B)]
        aw_ld = [sem(f"aw_ld{i}") for i in range(3)]
        aw_hi_done, aw_lo_done = sem("aw_hi_done"), sem("aw_lo_done")
        prefilled = sem("prefilled")
        const_ready = sem("const_ready")
        gate_hi_done = sem("gate_hi_done")
        mask_hi_done = sem("mask_hi_done")
        pool_const = sem("pool_const")
        sb2_scaled = sem("sb2_scaled")
        att_full, att_evac, att_hi = sem("att_full"), sem("att_evac"), sem("att_hi")
        ln1_mv, ln1_sd, ln1_rs, ln1_out = sem("ln1_mv"), sem("ln1_sd"), sem("ln1_rs"), sem("ln1_out")
        ln2_mv, ln2_sd, ln2_rs, ln2_out = sem("ln2_mv"), sem("ln2_sd"), sem("ln2_rs"), sem("ln2_out")
        vmask = sem("vmask")
        bo_added, sb2_added = sem("bo_added"), sem("sb2_added")
        den_ready, den_read = sem("den_ready"), sem("den_read")
        step = sem("step")
        z_ready, exp_done = sem("z_ready"), sem("exp_done")
        meta_ids = sem("meta_ids")
        hot_ready = sem("hot_ready")
        slots_ready = sem("slots_ready")
        dispatched = sem("dispatched")
        w_ld = [sem(f"w_ld{q}") for q in range(4)]
        w_hi = [sem(f"w_hi{q}") for q in range(4)]
        w_lo = [sem(f"w_lo{q}") for q in range(4)]
        ad_ld, ad_hi, ad_lo = sem("ad_ld"), sem("ad_hi"), sem("ad_lo")
        bias_ld = [sem(f"bias_ld{i}") for i in range(2)]
        g1_full, gelu_done, h_hi_done, h_split = sem("g1_full"), sem("gelu_done"), sem("h_hi_done"), sem("h_split")
        sh_full, sh_evac = sem("sh_full"), sem("sh_evac")
        y_full, y_evac = sem("y_full"), sem("y_evac")
        xg_ld = [sem(f"xg_ld{i}") for i in range(2)]
        meta_ld = [sem(f"meta_ld{i}") for i in range(2)]
        tin_full, tin_hi, tin_evac = sem("tin_full"), sem("tin_hi"), sem("tin_evac")
        tout_full, tout_evac = sem("tout_full"), sem("tout_evac")
        y_sent = [sem(f"y_sent{i}") for i in range(2)]
        yk_ld = [sem(f"yk_ld{i}") for i in range(2)]
        early_out = sem("early_out")
        stored = sem("stored")

        LAST_ATT = AT[("wo", B - 1, 0)] + 1

        def split3(w_h, w_l, m_h, m_l):
            return ((w_h, m_h), (w_h, m_l), (w_l, m_h))

        def xtok(b):
            return x[b].rearrange("(t p) d -> p t d", p=P)

        block = stack.enter_context(nc.Block())

        @block.sync
        def _(eng):
            def load_raw(u, q):
                eng.dma_start(raw[q][:, :], wch[u, q]).then_inc(w_ld[q], 16)

            def load_adapter(u):
                eng.dma_start(raw_ad[:, :], adw[u]).then_inc(ad_ld, 16)

            def load_rows(e, par):
                eng.dma_start(xg[par][:, :, :],
                              xbuf[bass.ds(e * SLOTS, SLOTS), 0:D].rearrange("(j p) c -> p j c", p=SP)
                              ).then_inc(xg_ld[par], 16)

            def load_meta(e, par):
                eng.dma_start(meta[par][:, :, :],
                              xbuf[bass.ds(e * SLOTS, SLOTS), D:ROW].rearrange("(j p) c -> p j c", p=SP)
                              ).then_inc(meta_ld[par], 16)

            eng.dma_start(res[:, 0:TT, :], xtok(0)).then_inc(x_in[0], 16)
            eng.dma_start(cst[:, :], cst_d).then_inc(cst_ld, 16)
            eng.dma_start(raw[1][:, :], attw[0]).then_inc(aw_ld[0], 16)
            eng.dma_start(raw[2][:, :], attw[1]).then_inc(aw_ld[1], 16)
            eng.dma_start(raw[3][:, :], attw[2]).then_inc(aw_ld[2], 16)
            for b in range(1, B):
                eng.dma_start(res[:, TT * b:TT * b + TT, :], xtok(b)).then_inc(x_in[b], 16)
            load_raw(0, 0)
            load_adapter(0)
            for q in range(1, 4):
                eng.wait_ge(aw_lo_done, q)
                load_raw(0, q)
            for b in range(2, B):
                eng.wait_ge(att_full, AT[("tc", b - 2, 0)] + 1)
                eng.dma_start(ctx_sb[b % 2][:, :, :],
                              ctx[b].rearrange("(t p) d -> p t d", p=P)).then_inc(ctx_in[b], 16)
            eng.wait_ge(pre_ld, 16)
            eng.dma_start(xbuf.rearrange("(a p) c -> p a c", p=P),
                          pre[:, :].unsqueeze(1).to_broadcast([P, E * SLOTS // P, ROW])).then_inc(prefilled, 16)
            eng.dma_start(ybuf.rearrange("(a p) c -> p a c", p=P),
                          pre[:, 0:D].unsqueeze(1).to_broadcast([P, 2 * NT, D])).then_inc(prefilled, 16)

            def load_expert_weights(e):
                for q in range(4):
                    eng.wait_ge(w_lo[q], e + 1)
                    load_raw(e + 1, q)
                    if q == 1:
                        eng.wait_ge(ad_lo, 2 * e + 2)
                        load_adapter(e + 1)

            load_expert_weights(0)
            eng.wait_ge(dispatched, 16 * 2 * NT)
            load_rows(0, 0)
            load_meta(0, 0)

            def load_bias(e, par):
                eng.dma_start(bexp[par][:, :], bexp_d[e]).then_inc(bias_ld[par], 16)

            def step_loads(e, par, wait_sent, wait_rows):
                if wait_rows:
                    eng.wait_ge(tin_full, 2 * e)
                load_rows(e + 1, par)
                load_expert_weights(e + 1)
                if wait_rows:
                    eng.wait_ge(y_evac, 2 * e)
                load_bias(e + 1, par)
                if wait_sent is not None:
                    eng.wait_ge(y_sent[par], wait_sent)
                load_meta(e + 1, par)

            load_bias(0, 0)
            step_loads(0, 1, None, False)
            with eng.Fori(0, 3) as i:
                step_loads(2 * i + 1, 0, 64 * i + 64, True)
                step_loads(2 * i + 2, 1, 64 * i + 64, True)

            for i in range(2):
                eng.wait_ge(y_sent[i], 64 * (E // 2))
            yview = ybuf.rearrange("(k t p) d -> p k t d", k=2, p=P)
            for k in range(2):
                eng.dma_start(yk[:, k, 0:NT - TT, :], yview[:, k, 0:NT - TT]).then_inc(yk_ld[0], 16)
            for k in range(2):
                eng.dma_start(yk[:, k, NT - TT:NT, :], yview[:, k, NT - TT:NT]).then_inc(yk_ld[1], 16)
            oview = out.rearrange("b (t p) d -> p (b t) d", p=P)
            eng.wait_ge(early_out, 1)
            eng.dma_start(oview[:, 0:NT - TT], res[:, 0:NT - TT, :]).then_inc(stored, 16)
            eng.wait_ge(early_out, 2)
            eng.dma_start(oview[:, NT - TT:NT], res[:, NT - TT:NT, :]).then_inc(stored, 16)
            eng.wait_ge(stored, 32)

        @block.gpsimd
        def _(eng):
            g = nc.gpsimd
            last_slot, last_row = eng.to_reg(E * SLOTS - 1), eng.to_reg(2 * T - 1)
            g.memset(ones[:, :], 1.0).then_inc(pool_const, 1)
            eng.wait_ge(brow_ld, 16)
            g.tensor_scalar(brow[:, 2, :], brow[:, 2, :], 0.2, None, ALU.mult).then_inc(sb2_scaled, 1)

            def mask_columns(b):
                if b:
                    eng.wait_ge(att_full, AT[("kv", b - 1, 1)] + 1)
                for tt in range(TT):
                    for dst, m in ((v_hi, bcol[:, MK + TT * b + tt:MK + TT * b + tt + 1]),
                                   (v_lo, mask_lo[:, TT * b + tt:TT * b + tt + 1])):
                        g.tensor_scalar(dst[:, tt, :, FD:P], ones[:, :].unsqueeze(1).to_broadcast([P, 4, FD]),
                                        m, None, ALU.mult).then_inc(vmask, 1)

            def add_row(b, i, done):
                tok = res[:, TT * b:TT * b + TT, :]
                g.tensor_tensor(tok, tok, brow[:, i, :].unsqueeze(1).to_broadcast([P, TT, D]),
                                ALU.add).then_inc(done, 1)

            def low_half(dst, src, hi):
                return g.tensor_tensor(dst[:, :], src[:, :], hi[:, :], ALU.subtract)

            eng.wait_ge(pool_const, 1)
            eng.wait_ge(const_ready, 1)
            mask_columns(0)
            eng.wait_ge(misc_ld, 32)
            for k in range(2):
                g.tensor_copy(rows[:, :, D + 1 + 2 * k].bitcast(I32), dest[:, :, k]).then_inc(meta_ids, 1)
            for b in range(B):
                eng.wait_ge(ln1_out, TT * b + TT)
                add_row(b, 1, bo_added)
                eng.wait_ge(w_hi[b], 1)
                low_half(sw_lo[b], raw[b], sw_hi[b]).then_inc(w_lo[b], 1)
                if b + 1 < B:
                    mask_columns(b + 1)
                if b:
                    if b == 1:
                        eng.wait_ge(sb2_scaled, 1)
                    eng.wait_ge(ln2_out, TT * b)
                    add_row(b - 1, 2, sb2_added)
            eng.wait_ge(ln2_out, TT * B)
            add_row(B - 1, 2, sb2_added)

            def expert_low(e, q):
                eng.wait_ge(w_hi[q], e + 2)
                low_half(ew_lo[q], raw[q], ew_hi[q]).then_inc(w_lo[q], 1)

            expert_low(0, 0)
            eng.wait_ge(prefilled, 32)
            eng.wait_ge(slots_ready, 1)
            eng.wait_ge(meta_ids, 2)
            for t in range(NT):
                for k in range(2):
                    g.indirect_dma_start(out=xbuf, out_offset=bass.IndirectOffsetOnAxis(ap=slot_i[:, t, k:k + 1], axis=0),
                                         in_=rows[:, t, :], in_offset=None,
                                         bounds_check=last_slot, oob_is_err=False).then_inc(dispatched, 16)
            expert_low(0, 1)
            expert_low(0, 2)

            def send_rows(par):
                for j in range(ST):
                    choice = j // (ST // 2)
                    idx = meta[par][:, j, 1 + 2 * choice:2 + 2 * choice].bitcast(I32)
                    g.indirect_dma_start(out=ybuf, out_offset=bass.IndirectOffsetOnAxis(ap=idx, axis=0),
                                         in_=yw[par][:, j, :], in_offset=None,
                                         bounds_check=last_row, oob_is_err=False).then_inc(y_sent[par], 16)

            def expert(e, par):
                expert_low(e + 1, 0)
                eng.wait_ge(tout_evac, 2 * e)
                expert_low(e + 1, 1)
                send_rows(1 - par)
                expert_low(e + 1, 2)

            for q in range(3):
                expert_low(1, q)
            with eng.Fori(0, 3) as i:
                expert(2 * i + 1, 1)
                expert(2 * i + 2, 0)
            eng.wait_ge(tout_evac, 2 * E - 2)
            send_rows(0)
            eng.wait_ge(tout_evac, 2 * E)
            send_rows(1)

        @block.scalar
        def _(eng):
            a = nc.scalar
            eng.dma_start(ctx_sb[0][:, :, :], ctx[0].rearrange("(t p) d -> p t d", p=P)).then_inc(ctx_in[0], 16)
            eng.dma_start(bcol[:, :], bcol_d).then_inc(bcol_ld, 16)
            eng.dma_start(brow[:, :, :], brow_d.partition_broadcast(P)).then_inc(brow_ld, 16)
            eng.dma_start(ctx_sb[1][:, :, :], ctx[1].rearrange("(t p) d -> p t d", p=P)).then_inc(ctx_in[1], 16)
            eng.dma_start(dest[:, :, :], dest_d).then_inc(misc_ld, 16)
            eng.dma_start(gate_raw[:, :, :], gw).then_inc(misc_ld, 16)
            eng.dma_start(pre[:, :], pre_d).then_inc(pre_ld, 16)

            def full(stage, b, j=0):
                eng.wait_ge(att_full, AT[(stage, b, j)] + 1)

            def hi_done(ins):
                ins.then_inc(att_hi, 1)

            def chunk_hi(i):
                eng.wait_ge(aw_ld[i], 16)
                a.activation(aw_hi[i][:, :], raw[i + 1][:, :], ACT.Copy).then_inc(aw_hi_done, 1)

            def ln_sqrt(mvt, sdt, s_mv, s_sd, b):
                eng.wait_ge(s_mv, TT * b + TT)
                a.activation(sdt[:, :], mvt[:, :, 1], ACT.Sqrt, bias=LN_EPS).then_inc(s_sd, 1)

            def ln_apply(dst, rs, nm, s_rs, s_out, b):
                eng.wait_ge(s_rs, 2 * b + 2)
                for tt in range(TT):
                    a.activation(dst(tt), res[:, TT * b + tt, :], ACT.Identity,
                                 scale=rs[:, tt:tt + 1], bias=nm[:, tt:tt + 1]).then_inc(s_out, 1)

            def ln1_apply(b):
                if b:
                    full("tx", b - 1)
                ln_apply(lambda tt: xn[:, tt, :], rstd, nmr, ln1_rs, ln1_out, b)

            def ln2_apply(b):
                ln_apply(lambda tt: rows[:, TT * b + tt, 0:D], rstd2, nmr2, ln2_rs, ln2_out, b)

            def inputs(b):
                full("tc", b)
                hi_done(a.activation(ct_hi[:, :, :], ps[BANK[AT[("tc", b, 0)]]][:, :], ACT.Copy))
                full("tx", b)
                hi_done(a.activation(nt_hi[:, :, :], ps[BANK[AT[("tx", b, 0)]]][:, :], ACT.Copy))
                for stage, dst, c in (("k", k_hi, BK), ("q", q_hi, BQ)):
                    full(stage, b)
                    bank = ps[BANK[AT[(stage, b, 0)]]]
                    for m in range(KD):
                        hi_done(a.activation(dst[:, m, :], bank[:, S * m:S * m + S], ACT.Identity,
                                             bias=bcol[:, c + m:c + m + 1]))

            chunk_hi(0)
            ln_sqrt(mv, sd, ln1_mv, ln1_sd, 0)
            ln1_apply(0)
            chunk_hi(1)
            chunk_hi(2)
            eng.wait_ge(bcol_ld, 16)
            a.activation(mask_hi[:, :], bcol[:, MK:MK + NT], ACT.Copy).then_inc(mask_hi_done, 1)
            inputs(0)
            eng.wait_ge(misc_ld, 32)
            a.activation(gate_hi[:, :, :], gate_raw[:, :, :], ACT.Copy).then_inc(gate_hi_done, 1)

            for b in range(B):
                if b + 1 < B:
                    ln_sqrt(mv, sd, ln1_mv, ln1_sd, b + 1)
                for j in range(4):
                    full("kf", b, j)
                    hi_done(a.activation(kf_hi[:, j // 2, j % 2, :], ps[BANK[AT[("kf", b, j)]]][:, :], ACT.Relu))
                if b + 1 < B:
                    ln1_apply(b + 1)
                for j in range(4):
                    if b and j == 2:
                        ln_sqrt(mv2, sd2, ln2_mv, ln2_sd, b - 1)
                    full("qf", b, j)
                    hi_done(a.activation(qf_hi[:, 2 * j:2 * j + 2, :], ps[BANK[AT[("qf", b, j)]]][:, :], ACT.Relu))
                if b:
                    ln2_apply(b - 1)
                    full("t2", b - 1)
                    hi_done(a.activation(xt_hi[:, :, S * (b - 1):S * b],
                                         ps[BANK[AT[("t2", b - 1, 0)]]][:, :].rearrange("p (k n) -> p k n", k=KD), ACT.Copy))
                for j in range(2):
                    full("tkv", b, j)
                    hi_done(a.activation(kvt_hi[:, 4 * j:4 * j + 4, :], ps[BANK[AT[("tkv", b, j)]]][:, :], ACT.Copy))
                eng.wait_ge(w_ld[b], 16)
                a.activation(sw_hi[b][:, :], raw[b][:, :], ACT.Copy).then_inc(w_hi[b], 1)
                if b == 1:
                    eng.wait_ge(ad_ld, 16)
                    a.activation(sdn_hi[:, :, :, :], raw_ad[:, 0:KD * RANK].rearrange("p (k r) -> p k r", k=KD).unsqueeze(2).to_broadcast([P, KD, 3, RANK]), ACT.Copy).then_inc(ad_hi, 1)
                    a.activation(sup[:, :], raw_ad[0:AP3, KD * RANK:AD], ACT.Copy).then_inc(ad_hi, 1)
                if b + 1 < B:
                    inputs(b + 1)
                for j in range(2):
                    full("qkv", b, j)
                    n = 2 * b + j
                    if n:
                        eng.wait_ge(den_read, n)
                    a.activation(den[:, :], ps[BANK[AT[("qkv", b, j)]]][FD:P, :], ACT.Identity,
                                 bias=DEN_EPS).then_inc(den_ready, 1)

            def gelu_groups(body, ms, n, bias):
                for m in ms:
                    g0 = body * NG + m
                    eng.wait_ge(g1_full, g0 + 1)
                    if not isinstance(body, int) or g0 >= 3:
                        eng.wait_ge(h_split, g0 - 2)
                    if m < MH:
                        a.activation(h32[m % 3][:, 0:n], ps[m % 3][:, 0:n], ACT.Gelu,
                                     bias=bias[:, m:m + 1]).then_inc(gelu_done, 1)
                    else:
                        a.activation(h32[m % 3][0:AP3, 0:n], ps[m % 3][0:AP3, 0:n], ACT.Gelu).then_inc(gelu_done, 1)

            shared_bias = bcol[:, 0:NB]

            def expert_hi(e, q):
                if isinstance(e, int) and e == 0:
                    eng.wait_ge(att_full, LAST_ATT)
                elif q < 2:
                    eng.wait_ge(g1_full, (e - 1 + FIRST) * NG + 4 * q + 4)
                else:
                    eng.wait_ge(y_full, 2 * e)
                eng.wait_ge(w_ld[q], 16 * e + 32)
                a.activation(ew_hi[q][:, :], raw[q][:, :], ACT.Copy).then_inc(w_hi[q], 1)

            def adapter_hi(e):
                eng.wait_ge(ad_ld, 16 * e + 32)
                a.activation(dn_hi[:, :, :, :], raw_ad[:, 0:KD * RANK].rearrange("p (k r) -> p k r", k=KD).unsqueeze(2).to_broadcast([P, KD, 3, RANK]), ACT.Copy).then_inc(ad_hi, 1)
                a.activation(up[:, :], raw_ad[0:AP3, KD * RANK:AD], ACT.Copy).then_inc(ad_hi, 1)

            def rows_hi(e, par):
                for k in range(KD):
                    eng.wait_ge(tin_full, 2 * e + 1 + k)
                    a.activation(xe_hi[:, k, :], ps[5 + k][:, 0:SLOTS], ACT.Copy).then_inc(tin_hi, 1)

            ln_sqrt(mv2, sd2, ln2_mv, ln2_sd, B - 1)
            ln2_apply(B - 1)
            gelu_groups(0, range(NG), S, shared_bias)
            full("t2", B - 1)
            hi_done(a.activation(xt_hi[:, :, S * (B - 1):T],
                                 ps[BANK[AT[("t2", B - 1, 0)]]][:, :].rearrange("p (k n) -> p k n", k=KD), ACT.Copy))
            expert_hi(0, 0)
            eng.wait_ge(z_ready, 1)
            a.activation(tmp_exp[:, :, :], z[:, :, :], ACT.Exp).then_inc(exp_done, 1)
            eng.wait_ge(z_ready, 2)
            a.activation(esum[:, 1, :], top[:, 1, :], ACT.Exp).then_inc(exp_done, 1)
            expert_hi(0, 1)
            gelu_groups(1, range(NG), S, shared_bias)
            expert_hi(0, 2)
            expert_hi(0, 3)
            adapter_hi(0)
            gelu_groups(2, range(NG), S, shared_bias)
            rows_hi(0, 0)

            def expert(e, par, bias_seen, last=False):
                body = e + FIRST
                eng.wait_ge(bias_ld[par], bias_seen)
                gelu_groups(body, range(4), SLOTS, bexp[par])
                if not last:
                    expert_hi(e + 1, 0)
                gelu_groups(body, range(4, NG), SLOTS, bexp[par])
                if not last:
                    rows_hi(e + 1, 1 - par)
                    expert_hi(e + 1, 1)
                for d in range(KD):
                    eng.wait_ge(y_full, 2 * e + 1 + d)
                    a.activation(ye[:, d, :], ps[3 + d][:, 0:SLOTS], ACT.Identity,
                                 bias=bexp[par][:, MH + d:MH + d + 1]).then_inc(y_evac, 1)
                if not last:
                    expert_hi(e + 1, 2)
                    expert_hi(e + 1, 3)
                    adapter_hi(e + 1)

            expert(0, 0, 16)
            with eng.Fori(0, 3) as i:
                expert(2 * i + 1, 1, 16 * i + 16)
                expert(2 * i + 2, 0, 16 * i + 32)
            expert(E - 1, 1, 64, last=True)
            gelu_groups(LAST, range(NG), S, shared_bias)

        @block.tensor
        def _(eng):
            pe = nc.tensor

            def mm(dst, pairs, last_inc=None, start=True, stop=True):
                for n, (w, m) in enumerate(pairs):
                    ins = pe.matmul(dst, w, m, start=start and n == 0, stop=stop and n == len(pairs) - 1)
                return ins

            def bank_of(g):
                n = AT[g]
                before = [i for i in range(n) if BANK[i] == BANK[n]]
                if before:
                    eng.wait_ge(att_evac, before[-1] + 1)
                return ps[BANK[n]]

            def done(stage, b, j=0):
                eng.wait_ge(att_evac, AT[(stage, b, j)] + 1)

            def full(ins):
                ins.then_inc(att_full, 1)

            def turn(g, src):
                bank = bank_of(g)
                for k in range(KD):
                    for tt in range(TT):
                        ins = pe.transpose(bank[:, k * S + tt * P:k * S + tt * P + P],
                                           src(tt)[:, k * P:k * P + P], ident)
                full(ins)

            def aw(i, c, n):
                return aw_hi[i][:, c:c + n], aw_lo[i][:, c:c + n]

            def project(stage, b, c, src_hi, src_lo):
                bank = bank_of((stage, b, 0))
                for m in range(KD):
                    pairs = []
                    for k in range(KD):
                        wh, wl = aw(0, c + k * D + m * P, P)
                        pairs += split3(wh, wl, src_hi[:, k, :], src_lo[:, k, :])
                    ins = mm(bank[:, m * S:m * S + S], pairs)
                full(ins)

            def project_rows(g, i, c, src_hi, src_lo):
                bank = bank_of(g)
                for tt in range(TT):
                    pairs = []
                    for k in range(KD):
                        mh, ml = aw(i, c + k * D, D)
                        pairs += split3(src_hi[:, k, tt * P:tt * P + P], src_lo[:, k, tt * P:tt * P + P], mh, ml)
                    ins = mm(bank[:, tt * D:tt * D + D], pairs)
                full(ins)

            def inputs(b):
                eng.wait_ge(ctx_in[b], 16)
                if b == 0:
                    eng.wait_ge(cst_ld, 16)
                turn(("tc", b, 0), lambda tt: ctx_sb[b % 2][:, tt, :])
                eng.wait_ge(ln1_out, TT * b + TT)
                turn(("tx", b, 0), lambda tt: xn[:, tt, :])
                if b == 0:
                    eng.wait_ge(aw_lo_done, 1)
                done("tc", b)
                project("k", b, 0, ct_hi, ct_lo)
                if b == 0:
                    eng.wait_ge(aw_lo_done, 2)
                project_rows(("v", b, 0), 1, 0, ct_hi, ct_lo)
                done("tx", b)
                project("q", b, KD * D, nt_hi, nt_lo)

            def key_features(b):
                done("k", b)
                if b == 0:
                    eng.wait_ge(aw_lo_done, 3)
                for j in range(4):
                    tt, k = j // 2, j % 2
                    bank = bank_of(("kf", b, j))
                    full(mm(bank[:, :], split3(k_hi[:, k, tt * P:tt * P + P], k_lo[:, k, tt * P:tt * P + P], *aw(2, 0, 512))))

            def query_features(b):
                done("q", b)
                for j in range(4):
                    bank = bank_of(("qf", b, j))
                    for i in range(2):
                        m = 2 * j + i
                        wh, wl = aw(2, 512 + (m % 4) * P, P)
                        ins = mm(bank[:, i * S:i * S + S], split3(wh, wl, q_hi[:, m // 4, :], q_lo[:, m // 4, :]))
                    full(ins)

            def attention_out(b):
                done("qkv", b, 1)
                project_rows(("wo", b, 0), 1, KD * D, o_hi, o_lo)

            def turn_normed(b):
                eng.wait_ge(ln2_out, TT * b + TT)
                turn(("t2", b, 0), lambda tt: rows[:, TT * b + tt, 0:D])

            def key_values(b):
                done("v", b)
                eng.wait_ge(vmask, 4 * b + 4)
                for j in range(2):
                    bank = bank_of(("kv", b, j))
                    for i in range(2):
                        g = 2 * j + i
                        pairs = []
                        for tt in range(TT):
                            done("kf", b, 2 * tt + g // 2)
                            c = (g % 2) * S
                            pairs += split3(v_hi[:, tt, g, :], v_lo[:, tt, g, :],
                                            kf_hi[:, tt, g // 2, c:c + S], kf_lo[:, tt, g // 2, c:c + S])
                        ins = mm(bank[:, i * S:i * S + S], pairs)
                    full(ins)
                for j in range(2):
                    done("kv", b, j)
                    bank = bank_of(("tkv", b, j))
                    for i in range(2):
                        for c in range(2):
                            ins = pe.transpose(bank[:, (2 * i + c) * P:(2 * i + c + 1) * P],
                                               kvm[:, 2 * j + i, c * P:c * P + P], ident)
                    full(ins)

            def attend(b):
                for j in range(2):
                    done("tkv", b, j)
                    bank = bank_of(("qkv", b, j))
                    for i in range(2):
                        g = 2 * j + i
                        done("qf", b, g)
                        pairs = []
                        for c in range(2):
                            pairs += split3(kvt_hi[:, 2 * g + c, :], kvt_lo[:, 2 * g + c, :],
                                            qf_hi[:, 2 * g + c, :], qf_lo[:, 2 * g + c, :])
                        ins = mm(bank[:, i * S:i * S + S], pairs)
                    full(ins)

            inputs(0)
            for b in range(B):
                key_features(b)
                if b:
                    attention_out(b - 1)
                query_features(b)
                if b:
                    turn_normed(b - 1)
                key_values(b)
                if b + 1 < B:
                    inputs(b + 1)
                attend(b)
            attention_out(B - 1)

            def hidden(body, ms, n, wh, wl, dh, dl, mh, ml):
                for m in ms:
                    g0 = body * NG + m
                    if isinstance(body, int) and g0 < 3:
                        eng.wait_ge(att_evac, max(i for i in range(LAST_ATT) if BANK[i] == m) + 1)
                    else:
                        eng.wait_ge(gelu_done, g0 - 2)
                    pairs = []
                    for k in range(KD):
                        if m < MH:
                            c = k * 512 + (m % 4) * P
                            st = (wh[m // 4][:, c:c + P], wl[m // 4][:, c:c + P])
                        else:
                            st = (dh[:, k, :, :].rearrange("p a r -> p (a r)"), dl[:, k, :, :].rearrange("p a r -> p (a r)"))
                        pairs += split3(*st, mh(k), ml(k))
                    rowsn = P if m < MH else AP3
                    mm(ps[m % 3][0:rowsn, 0:n], pairs).then_inc(g1_full, 1)

            def shared_hidden(body, c, ms):
                hidden(body, ms, S, sw_hi, sw_lo, sdn_hi, sdn_lo,
                       lambda k: xt_hi[:, k, S * c:S * c + S], lambda k: xt_lo[:, k, S * c:S * c + S])

            def shared_out(body, n, tts):
                for tt in tts:
                    if n:
                        eng.wait_ge(sh_evac, TT * (n - 1) + tt + 1)
                    elif tt == 0:
                        for bank in (3, 4):
                            eng.wait_ge(att_evac, max(i for i in range(LAST_ATT) if BANK[i] == bank) + 1)
                    if body == LAST:
                        eng.wait_ge(y_evac, 2 * E)
                    tok = slice(tt * P, tt * P + P)
                    for m in range(MH):
                        if tt == tts[0]:
                            eng.wait_ge(h_split, body * NG + m + 1)
                        c = (m % 4) * D
                        mm(ps[3 + tt][:, 0:D], split3(h_hi[:, m, tok], h_lo[:, m, tok],
                                                      sw_hi[2 + m // 4][:, c:c + D], sw_lo[2 + m // 4][:, c:c + D]),
                           start=m == 0, stop=False)
                    eng.wait_ge(h_split, body * NG + NG)
                    pe.matmul(ps[3 + tt][:, 0:D], a_st[:, tok], sup[:, :], start=False, stop=True).then_inc(sh_full, 1)

            for q in range(2):
                eng.wait_ge(w_lo[q], 1)
            eng.wait_ge(ad_lo, 2)
            done("t2", 0)
            shared_hidden(0, 0, range(NG))
            turn_normed(B - 1)
            done("t2", B - 1)
            eng.wait_ge(const_ready, 3)
            for half in range(2):
                bank = bank_of(("lg", half, 0))
                pairs = []
                for k in range(KD):
                    c = half * 512
                    pairs += split3(gate_hi[:, k, :], gate_lo[:, k, :], xt_hi[:, k, c:c + 512], xt_lo[:, k, c:c + 512])
                full(mm(bank[:, :], pairs))
            for q in range(2, 4):
                eng.wait_ge(w_lo[q], 1)
            shared_out(0, 0, [0])
            done("lg", 1)
            bank = bank_of(("tlg", 0, 0))
            for t in range(NT):
                ins = pe.transpose(bank[:, E * t:E * t + E], lgt[:, P * t:P * t + P], ident[0:E, 0:E])
            full(ins)
            shared_out(0, 0, [1])
            shared_hidden(1, 1, range(0, 4))
            eng.wait_ge(hot_ready, 1)
            bank = bank_of(("pos", 0, 0))
            tri, one = tri_ones[:, 0:P], tri_ones[:, P:2 * P]
            width = 2 * E
            pe.matmul(bank[:, 0:NT * width], tri, hot_bf[:, :, :, :], start=True, stop=False)
            for t in range(NT - 1):
                ins = pe.matmul(bank[:, (t + 1) * width:NT * width], one,
                                hot_bf[:, t, :, :].rearrange("p k e -> p (k e)").unsqueeze(1).to_broadcast([P, NT - 1 - t, width]),
                                start=False, stop=t == NT - 2)
            full(ins)
            shared_hidden(1, 1, range(4, NG))
            shared_out(1, 1, [0, 1])
            shared_hidden(2, 2, range(NG))

            def rows_in(e, par, seen):
                eng.wait_ge(xg_ld[par], seen)
                if not (isinstance(e, int) and e <= 1):
                    eng.wait_ge(tout_evac, 2 * e - 2)
                elif e == 0:
                    done("pos", 0)
                for k in range(KD):
                    for j in range(ST):
                        ins = pe.transpose(ps[5 + k][:, j * SP:j * SP + SP],
                                           xg[par][:, j, k * P:k * P + P], ident[0:SP, 0:SP])
                    ins.then_inc(tin_full, 1)

            def rows_out(e):
                eng.wait_ge(y_evac, 2 * e + 2)
                if not (isinstance(e, int) and e == 0):
                    eng.wait_ge(tout_evac, 2 * e)
                for j in range(ST):
                    bank = ps[7] if j < 2 else ps[5]
                    for d in range(KD):
                        c = (j % 2) * D + d * P
                        ins = pe.transpose(bank[0:SP, c:c + P], ye[:, d, j * SP:j * SP + SP], ident)
                    if j % 2:
                        ins.then_inc(tout_full, 1)

            rows_in(0, 0, 16)
            shared_out(2, 2, [0, 1])

            def expert(e, par, seen, first=False, last=False):
                body = e + FIRST
                half = lambda ms: hidden(body, ms, SLOTS, ew_hi, ew_lo, dn_hi, dn_lo,
                                         lambda k: xe_hi[:, k, :], lambda k: xe_lo[:, k, :])
                eng.wait_ge(tin_evac, 2 * e + 2)
                eng.wait_ge(w_lo[0], e + 2)
                half(range(4))
                if not first:
                    rows_out(e - 1)
                eng.wait_ge(w_lo[1], e + 2)
                half(range(4, MH))
                eng.wait_ge(ad_lo, 2 * e + 4)
                half([MH])
                if not last:
                    rows_in(e + 1, 1 - par, seen)
                if first:
                    eng.wait_ge(sh_evac, 3 * TT)
                else:
                    eng.wait_ge(y_evac, 2 * e)
                for m in range(MH):
                    eng.wait_ge(h_split, body * NG + m + 1)
                    if m % 4 == 0:
                        eng.wait_ge(w_lo[2 + m // 4], e + 2)
                    for d in range(KD):
                        c = (m % 4) * D + d * P
                        ins = mm(ps[3 + d][:, 0:SLOTS], split3(ew_hi[2 + m // 4][:, c:c + P], ew_lo[2 + m // 4][:, c:c + P],
                                                               h_hi[:, m, :], h_lo[:, m, :]), start=m == 0, stop=False)
                eng.wait_ge(h_split, body * NG + NG)
                for d in range(KD):
                    pe.matmul(ps[3 + d][:, 0:SLOTS], up[:, d * P:d * P + P], a_st[:, :],
                              start=False, stop=True).then_inc(y_full, 1)

            expert(0, 0, 16, first=True)
            with eng.Fori(0, 3) as i:
                expert(2 * i + 1, 1, 16 * i + 32)
                expert(2 * i + 2, 0, 16 * i + 32)
            expert(E - 1, 1, None, last=True)
            shared_hidden(LAST, B - 1, range(2))
            rows_out(E - 1)
            shared_hidden(LAST, B - 1, range(2, NG))
            shared_out(LAST, 3, [0, 1])

        @block.vector
        def _(eng):
            v = nc.vector
            steps = [0]

            def own(ins):
                steps[0] += 1
                ins.then_inc(step, 1)
                eng.wait_ge(step, steps[0])

            def full(stage, b, j=0):
                eng.wait_ge(att_full, AT[(stage, b, j)] + 1)
                return ps[BANK[AT[(stage, b, j)]]]

            def evac(ins):
                ins.then_inc(att_evac, 1)

            hi_seen = [0]

            def after_hi(n=1):
                hi_seen[0] += n
                eng.wait_ge(att_hi, hi_seen[0])

            def low(dst, src, hi):
                return v.tensor_tensor(dst, src, hi, ALU.subtract)

            def statistics(b, st, mvt, s_mv):
                for tt in range(TT):
                    ins = v.bn_stats(st[:, tt, :], res[:, TT * b + tt, :])
                own(ins)
                for tt in range(TT):
                    v.bn_aggr(mvt[:, tt, :], st[:, tt, :]).then_inc(s_mv, 1)

            def factors(b, mvt, sdt, rs, nm, s_sd, s_rs):
                eng.wait_ge(s_sd, b + 1)
                v.reciprocal(rs[:, :], sdt[:, :]).then_inc(s_rs, 1)
                eng.wait_ge(s_rs, 2 * b + 1)
                v.scalar_tensor_tensor(nm[:, :], mvt[:, :, 0], -1.0, rs[:, :], ALU.mult, ALU.mult).then_inc(s_rs, 1)

            def inputs(b):
                bank = full("tc", b)
                after_hi()
                evac(low(ct_lo[:, :, :], bank[:, :], ct_hi[:, :, :]))
                bank = full("tx", b)
                after_hi()
                evac(low(nt_lo[:, :, :], bank[:, :], nt_hi[:, :, :]))
                for stage, hi, lo, c in (("k", k_hi, k_lo, BK), ("v", 0, 0, 0), ("q", q_hi, q_lo, BQ)):
                    bank = full(stage, b)
                    if stage == "v":
                        own(v.tensor_tensor(v32[:, :, :], bank[:, :].rearrange("p (t d) -> p t d", t=TT),
                                            brow[:, 0, :].unsqueeze(1).to_broadcast([P, TT, D]), ALU.add))
                        masks = [bcol[:, MK + TT * b + tt:MK + TT * b + tt + 1] for tt in range(TT)]
                        vh = [v_hi[:, tt, :, 0:FD] for tt in range(TT)]
                        vs = [v32[:, tt, :].rearrange("p (g c) -> p g c", g=4) for tt in range(TT)]
                        for tt in range(TT):
                            ins = v.tensor_scalar(vh[tt], vs[tt], masks[tt], None, ALU.mult)
                        own(ins)
                        for tt in range(TT):
                            ins = v.scalar_tensor_tensor(v_lo[:, tt, :, 0:FD], vs[tt], masks[tt], vh[tt], ALU.mult, ALU.subtract)
                        evac(ins)
                        continue
                    after_hi(KD)
                    for m in range(KD):
                        ins = v.scalar_tensor_tensor(lo[:, m, :], bank[:, S * m:S * m + S], bcol[:, c + m:c + m + 1],
                                                     hi[:, m, :], ALU.add, ALU.subtract)
                    evac(ins)

            def relu_low(dst, bank, hi):
                return v.scalar_tensor_tensor(dst, bank[:, :], 0.0, hi, ALU.max, ALU.subtract)

            eng.wait_ge(x_in[0], 16)
            statistics(0, stats, mv, ln1_mv)
            factors(0, mv, sd, rstd, nmr, ln1_sd, ln1_rs)
            eng.wait_ge(mask_hi_done, 1)
            v.tensor_tensor(mask_lo[:, :], bcol[:, MK:MK + NT], mask_hi[:, :], ALU.subtract).then_inc(const_ready, 1)
            for i in range(3):
                eng.wait_ge(aw_hi_done, i + 1)
                low(aw_lo[i][:, :], raw[i + 1][:, :], aw_hi[i][:, :]).then_inc(aw_lo_done, 1)
            eng.wait_ge(brow_ld, 16)
            inputs(0)
            eng.wait_ge(cst_ld, 16)
            v.tensor_copy(tri_ones[:, :], cst[:, C_TRI:C_TRI + 2 * P]).then_inc(const_ready, 1)
            eng.wait_ge(gate_hi_done, 1)
            low(gate_lo[:, :, :], gate_raw[:, :, :], gate_hi[:, :, :]).then_inc(const_ready, 1)

            def attention_sum(b):
                bank = full("wo", b)
                eng.wait_ge(bo_added, b + 1)
                tok = res[:, TT * b:TT * b + TT, :]
                evac(v.tensor_tensor(tok, bank[:, :].rearrange("p (t d) -> p t d", t=TT), tok, ALU.add))
                eng.wait_ge(att_evac, AT[("wo", b, 0)] + 1)
                statistics(b, stats2, mv2, ln2_mv)

            for b in range(B):
                if b + 1 < B:
                    eng.wait_ge(x_in[b + 1], 16)
                    statistics(b + 1, stats, mv, ln1_mv)
                for j in range(4):
                    bank = full("kf", b, j)
                    after_hi()
                    evac(relu_low(kf_lo[:, j // 2, j % 2, :], bank, kf_hi[:, j // 2, j % 2, :]))
                    if j == 1 and b + 1 < B:
                        factors(b + 1, mv, sd, rstd, nmr, ln1_sd, ln1_rs)
                if b:
                    attention_sum(b - 1)
                for j in range(4):
                    bank = full("qf", b, j)
                    after_hi()
                    evac(relu_low(qf_lo[:, 2 * j:2 * j + 2, :], bank, qf_hi[:, 2 * j:2 * j + 2, :]))
                    if b and j == 2:
                        factors(b - 1, mv2, sd2, rstd2, nmr2, ln2_sd, ln2_rs)
                if b:
                    bank = full("t2", b - 1)
                    after_hi()
                    evac(low(xt_lo[:, :, S * (b - 1):S * b], bank[:, :].rearrange("p (k n) -> p k n", k=KD),
                             xt_hi[:, :, S * (b - 1):S * b]))
                for j in range(2):
                    bank = full("kv", b, j)
                    evac(v.tensor_tensor(kvm[:, 2 * j:2 * j + 2, :], bank[:, :].rearrange("p (g n) -> p g n", g=2),
                                         cst[:, C_MASK:C_MASK + S].unsqueeze(1).to_broadcast([P, 2, S]), ALU.mult))
                for j in range(2):
                    bank = full("tkv", b, j)
                    after_hi()
                    evac(low(kvt_lo[:, 4 * j:4 * j + 4, :], bank[:, :], kvt_hi[:, 4 * j:4 * j + 4, :]))
                if b == 1:
                    eng.wait_ge(ad_hi, 2)
                    v.tensor_tensor(sdn_lo[:, :, :, :], raw_ad[:, 0:KD * RANK].rearrange("p (k r) -> p k r", k=KD).unsqueeze(2).to_broadcast([P, KD, 3, RANK]),
                                    sdn_hi[:, :, :, :], ALU.subtract).then_inc(ad_lo, 1)
                    v.tensor_tensor(sup[2 * RANK:AP3, :], raw_ad[2 * RANK:AP3, KD * RANK:AD], sup[2 * RANK:AP3, :],
                                    ALU.subtract).then_inc(ad_lo, 1)
                if b + 1 < B:
                    inputs(b + 1)
                for j in range(2):
                    bank = full("qkv", b, j)
                    eng.wait_ge(den_ready, 2 * b + j + 1)
                    v.reciprocal(rden[:, :], den[:, :]).then_inc(den_read, 1)
                    eng.wait_ge(den_read, 2 * b + j + 1)
                    for i in range(2):
                        ins = v.tensor_tensor(o32[FD * i:FD * i + FD, j, :], bank[0:FD, S * i:S * i + S],
                                              rden[:, S * i:S * i + S], ALU.mult)
                    own(ins)
                    own(v.tensor_copy(o_hi[:, j, :], o32[:, j, :]))
                    evac(low(o_lo[:, j, :], o32[:, j, :], o_hi[:, j, :]))

            attention_sum(B - 1)
            factors(B - 1, mv2, sd2, rstd2, nmr2, ln2_sd, ln2_rs)

            def split_groups(body, ms, n):
                for m in ms:
                    g0 = body * NG + m
                    eng.wait_ge(gelu_done, g0 + 1)
                    src = h32[m % 3]
                    if m < MH:
                        v.tensor_copy(h_hi[:, m, 0:n], src[:, 0:n]).then_inc(h_hi_done, 1)
                        eng.wait_ge(h_hi_done, g0 + 1)
                        low(h_lo[:, m, 0:n], src[:, 0:n], h_hi[:, m, 0:n]).then_inc(h_split, 1)
                    else:
                        v.tensor_copy(a_st[:, 0:n], src[0:AP3, 0:n]).then_inc(h_hi_done, 1)
                        eng.wait_ge(h_hi_done, g0 + 1)
                        mid = slice(RANK, 2 * RANK)
                        low(a_st[mid, 0:n], src[mid, 0:n], a_st[mid, 0:n]).then_inc(h_split, 1)

            def add_shared(c, n):
                for tt in range(TT):
                    eng.wait_ge(sh_full, TT * n + tt + 1)
                    if tt == 0:
                        eng.wait_ge(sb2_added, c + 1)
                    tok = res[:, TT * c + tt, :]
                    v.scalar_tensor_tensor(tok, ps[3 + tt][:, 0:D], 0.2, tok, ALU.mult, ALU.add).then_inc(sh_evac, 1)

            split_groups(0, range(NG), S)
            bank = full("t2", B - 1)
            after_hi()
            evac(low(xt_lo[:, :, S * (B - 1):T], bank[:, :].rearrange("p (k n) -> p k n", k=KD),
                     xt_hi[:, :, S * (B - 1):T]))
            for half in range(2):
                bank = full("lg", half)
                evac(v.tensor_copy(lgt[:, 512 * half:512 * half + 512], bank[0:E, :]))

            bank = full("tlg", 0)
            evac(v.tensor_copy(lg[:, :, :], bank[:, 0:NT * E].rearrange("p (t e) -> p t e", e=E)))
            eng.wait_ge(att_evac, AT[("tlg", 0, 0)] + 1)

            def over_experts(col):
                return col.unsqueeze(2).to_broadcast([P, NT, E])

            ranks = cst[:, C_RANK:C_RANK + NT * E].rearrange("p (t e) -> p t e", e=E)
            own(v.tensor_reduce(top[:, 0, :], lg[:, :, :], AX_X, ALU.max))
            v.tensor_tensor(z[:, :, :], lg[:, :, :], over_experts(top[:, 0, :]), ALU.subtract).then_inc(z_ready, 1)
            eng.wait_ge(z_ready, 1)
            tmp = tmp16[:, :, 0, :]
            own(v.scalar_tensor_tensor(tmp, z[:, :, :], 0.0, ranks, ALU.is_equal, ALU.mult))
            own(v.tensor_reduce(rank[:, :, 0], tmp, AX_X, ALU.max))
            own(v.tensor_tensor(hot[:, :, 0, :], ranks, over_experts(rank[:, :, 0]), ALU.is_equal))
            own(v.scalar_tensor_tensor(lg[:, :, :], hot[:, :, 0, :], -1e30, z[:, :, :], ALU.mult, ALU.add))
            v.tensor_reduce(top[:, 1, :], lg[:, :, :], AX_X, ALU.max).then_inc(z_ready, 1)
            eng.wait_ge(z_ready, 2)
            own(v.tensor_tensor(tmp, lg[:, :, :], over_experts(top[:, 1, :]), ALU.is_equal))
            own(v.tensor_tensor(tmp, tmp, ranks, ALU.mult))
            own(v.tensor_reduce(rank[:, :, 1], tmp, AX_X, ALU.max))
            own(v.tensor_tensor(hot[:, :, 1, :], ranks, over_experts(rank[:, :, 1]), ALU.is_equal))
            v.tensor_copy(hot_bf[:, :, :, :], hot[:, :, :, :]).then_inc(hot_ready, 1)
            eng.wait_ge(exp_done, 2)
            own(v.tensor_reduce(esum[:, 0, :], tmp_exp[:, :, :], AX_X, ALU.add))
            own(v.reciprocal(esum[:, 2, :], esum[:, 0, :]))
            v.tensor_copy(rows[:, :, D], esum[:, 2, :])
            v.tensor_tensor(rows[:, :, D + 2], esum[:, 1, :], esum[:, 2, :], ALU.mult)
            own(v.scalar_tensor_tensor(slot[:, :, :], rank[:, :, :], -float(SLOTS),
                                       cst[:, C_BASE:C_BASE + 2 * NT].rearrange("p (t k) -> p t k", k=2), ALU.mult, ALU.add))
            add_shared(0, 0)
            split_groups(1, range(0, 4), S)
            bank = full("pos", 0)
            evac(v.tensor_tensor(tmp16[:, :, :, :], hot[:, :, :, :],
                                 bank[:, 0:NT * 2 * E].rearrange("p (t k e) -> p t k e", t=NT, k=2), ALU.mult))
            eng.wait_ge(att_evac, AT[("pos", 0, 0)] + 1)
            own(v.tensor_reduce(place[:, :, :], tmp16[:, :, :, :], AX_X, ALU.add))
            own(v.tensor_tensor(slot[:, :, :], slot[:, :, :], place[:, :, :], ALU.add))
            own(v.tensor_scalar(place[:, :, :], place[:, :, :], float(CAP), float(NOWHERE), ALU.is_ge, ALU.mult))
            own(v.tensor_tensor(slot[:, :, :], slot[:, :, :], place[:, :, :], ALU.add))
            v.tensor_copy(slot_i[:, :, :], slot[:, :, :]).then_inc(slots_ready, 1)
            split_groups(1, range(4, NG), S)
            add_shared(1, 1)
            split_groups(2, range(NG), S)

            def rows_low(e):
                for k in range(KD):
                    eng.wait_ge(tin_hi, 2 * e + 1 + k)
                    low(xe_lo[:, k, :], ps[5 + k][:, 0:SLOTS], xe_hi[:, k, :]).then_inc(tin_evac, 1)

            def weighted(e, par, seen, sent):
                eng.wait_ge(meta_ld[par], seen)
                if sent is not None:
                    eng.wait_ge(y_sent[par], sent)
                for j in range(ST):
                    if j % 2 == 0:
                        eng.wait_ge(tout_full, 2 * e + 1 + j // 2)
                    bank = ps[7] if j < 2 else ps[5]
                    ins = v.tensor_scalar(yw[par][:, j, :], bank[0:SP, (j % 2) * D:(j % 2) * D + D],
                                          meta[par][:, j, 2 * (j // 2):2 * (j // 2) + 1], None, ALU.mult)
                    if j % 2:
                        ins.then_inc(tout_evac, 1)

            def expert_low(e):
                eng.wait_ge(w_hi[3], e + 2)
                low(ew_lo[3][:, :], raw[3][:, :], ew_hi[3][:, :]).then_inc(w_lo[3], 1)
                eng.wait_ge(ad_hi, 2 * e + 4)
                v.tensor_tensor(dn_lo[:, :, :, :], raw_ad[:, 0:KD * RANK].rearrange("p (k r) -> p k r", k=KD).unsqueeze(2).to_broadcast([P, KD, 3, RANK]),
                                dn_hi[:, :, :, :], ALU.subtract).then_inc(ad_lo, 1)
                v.tensor_tensor(up[2 * RANK:AP3, :], raw_ad[2 * RANK:AP3, KD * RANK:AD], up[2 * RANK:AP3, :],
                                ALU.subtract).then_inc(ad_lo, 1)

            rows_low(0)
            add_shared(2, 2)

            def expert(e, par, seen=None, sent=None, first=False, last=False):
                body = e + FIRST
                split_groups(body, range(2), SLOTS)
                expert_low(e)
                split_groups(body, range(2, 4), SLOTS)
                if not first:
                    weighted(e - 1, 1 - par, seen, sent)
                split_groups(body, range(4, NG), SLOTS)
                if not last:
                    rows_low(e + 1)

            expert(0, 0, first=True)
            expert(1, 1, seen=16)
            expert(2, 0, seen=16)
            with eng.Fori(1, 3) as i:
                expert(2 * i + 1, 1, seen=16 * i + 16, sent=64 * i)
                expert(2 * i + 2, 0, seen=16 * i + 16, sent=64 * i)
            expert(E - 1, 1, seen=64, sent=64 * 3, last=True)
            split_groups(LAST, range(2), S)
            weighted(E - 1, 1, 64, 64 * 3)
            split_groups(LAST, range(2, NG), S)

            add_shared(B - 1, 3)
            early, late = slice(0, NT - TT), slice(NT - TT, NT)
            eng.wait_ge(yk_ld[0], 32)
            own(v.tensor_tensor(res[:, early, :], res[:, early, :], yk[:, 0, early, :], ALU.add))
            v.tensor_tensor(res[:, early, :], res[:, early, :], yk[:, 1, early, :], ALU.add).then_inc(early_out, 1)
            eng.wait_ge(yk_ld[1], 32)
            eng.wait_ge(sh_evac, 4 * TT)
            own(v.tensor_tensor(res[:, late, :], res[:, late, :], yk[:, 0, late, :], ALU.add))
            v.tensor_tensor(res[:, late, :], res[:, late, :], yk[:, 1, late, :], ALU.add).then_inc(early_out, 1)


def kernel(x, ctx_2048, mask_BxS2_ff1, **w):
    import concourse.bacc as bacc
    from concourse.bass_utils import run_bass_kernel_spmd

    def f(name):
        return np.asarray(w[name])

    def tiles(m):
        return np.asarray(m).reshape(-1, P, m.shape[-1]).transpose(1, 0, 2)

    def cols(m):
        return tiles(m).reshape(P, -1)

    feat = np.zeros((P, 2, 8 * FD), np.float32)
    for h in range(8):
        for i, name in enumerate(("L0_xattn_Wkf", "L0_xattn_Wqf")):
            feat[HD * h:HD * h + HD, i, FD * h:FD * h + FD] = f(name).T
    attw = np.stack([np.concatenate([cols(f("L0_xattn_Wk").T), cols(f("L0_xattn_Wq").T)], 1),
                     np.concatenate([cols(f("L0_xattn_Wv").T), cols(f("L0_xattn_Wo").T)], 1),
                     feat.reshape(P, CH)])

    def chunks(w1, w2):
        one, two = tiles(w1), tiles(w2)
        return np.stack([one[:, :, 0:512].reshape(P, CH), one[:, :, 512:1024].reshape(P, CH),
                         two[:, 0:4].reshape(P, CH), two[:, 4:8].reshape(P, CH)])

    def adapter(wd, wu):
        side = np.zeros((P, D), np.float32)
        side[0:AP3] = np.concatenate([wu, wu, wu], 0)
        return np.concatenate([cols(wd), side], 1)

    w1, w2, wd, wu = (f("L0_ffn_" + n) for n in ("w1", "w2", "wd", "wu"))
    wch = np.stack([chunks(f("L0_ffn_sw1"), f("L0_ffn_sw2"))] + [chunks(w1[e], w2[e]) for e in range(E)])
    adw = np.stack([adapter(f("L0_ffn_swd"), f("L0_ffn_swu"))] + [adapter(wd[e], wu[e]) for e in range(E)])
    gate = np.zeros((D, P), np.float32)
    gate[:, 0:E] = f("L0_ffn_gate_w")
    vec = lambda m: np.asarray(m).reshape(-1, P).T
    bexp = np.stack([np.concatenate([vec(f("L0_ffn_b1")[e]), vec(f("L0_ffn_b2")[e])], 1) for e in range(E)])
    bias = [vec(f("L0_ffn_sb1")), np.zeros((P, 2), np.float32), vec(f("L0_xattn_bq")), vec(f("L0_xattn_bk")), vec(mask_BxS2_ff1)]
    bcol = np.concatenate(bias, 1)
    brow = np.stack([f("L0_xattn_bv"), f("L0_xattn_bo"), f("L0_ffn_sb2")])

    r, c = np.arange(P), np.arange(256)
    cst = np.zeros((P, CCOLS), np.float32)
    cst[:, C_ID:C_ID + P] = np.eye(P)
    cst[:, C_MASK:C_MASK + 256] = ((r[:, None] % FD) // HD) == (c[None, :] // FD)
    cst[:, C_TRI:C_TRI + P] = r[:, None] < r[None, :]
    cst[:, C_ONE:C_ONE + P] = 1.0
    cst[:, C_RANK:C_RANK + NT * E] = np.tile(E - np.arange(E), NT)
    cst[:, C_BASE:C_BASE + 2 * NT] = np.tile([E * SLOTS, E * SLOTS + CAP], NT)
    dest = (np.arange(NT)[None, :, None] * P + r[:, None, None] + T * np.arange(2)[None, None, :]).astype(np.int32)
    pre = np.zeros((P, ROW), np.int32)
    pre[:, D + 1::2] = NOWHERE + r[:, None]

    nc = bacc.Bacc("TRN2", target_bir_lowering=False, num_devices=1)
    arrays, args = {}, []
    for name, arr in (("x", x), ("ctx", ctx_2048), ("attw", attw), ("wch", wch), ("adw", adw), ("gate", tiles(gate)),
                      ("bcol", bcol), ("bexp", bexp), ("brow", brow), ("cst", cst), ("dest", dest), ("pre", pre.view(np.float32))):
        arrays["in_" + name] = np.ascontiguousarray(arr)
        args.append(nc.dram_tensor("in_" + name, arr.shape, mybir.dt.from_np(arrays["in_" + name].dtype),
                                   kind="ExternalInput").ap())
    args.append(nc.dram_tensor("xbuf", (E * SLOTS, ROW), F32, kind="Internal").ap())
    args.append(nc.dram_tensor("ybuf", (2 * T, D), F32, kind="Internal").ap())
    args.append(nc.dram_tensor("out", (B, S, D), F32, kind="ExternalOutput").ap())
    build_program(nc, *args)
    r = run_bass_kernel_spmd(nc, [arrays], core_ids=[0])
    return r.results[0]["out"]
```

```python
from contextlib import ExitStack

import numpy as np

import concourse.bass as bass
from concourse import mybir

ACT = mybir.ActivationFunctionType
ALU = mybir.AluOpType
AX_X = mybir.AxisListType.X
F32 = mybir.dt.float32
F32R = mybir.dt.float32r
BF16 = mybir.dt.bfloat16
I32 = mybir.dt.int32

P = 128
B, S, D = 4, 256, 256
T = B * S
TT = S // P
NT = T // P
KD = D // P
NH, HD, FD = 16, 16, 64
E = 8
CAP = int(T * 1.25 / E)
SLOTS = 2 * CAP
ST = 4
SP = SLOTS // ST
FH = 1024
MH = FH // P
RANK = 32
LN_EPS = 1e-5
DEN_EPS = 1e-8
META = 4
ROW = D + META
NOWHERE = 1 << 20
CH = 1024
AD = KD * RANK + D
AP3 = 3 * RANK
NB = 10
BQ, BK, MK = NB, NB + 2, NB + 4
BCOLS = MK + NT
C_ID, C_TRI, C_ONE, C_RANK, C_BASE = 0, P, 2 * P, 3 * P, 3 * P + NT * E
CCOLS = C_BASE + 2 * NT
NG = MH + 1
FIRST, LAST = 3, 11


def attention_groups():
    order = [("tc", 0, 0), ("tx", 0, 0), ("k", 0, 0), ("v", 0, 0), ("q", 0, 0)]
    for b in range(B):
        order += [("kf", b, j) for j in range(4)]
        order += [("qf", b, j) for j in range(4)]
        order += [("kv", b, j) for j in range(2)]
        if b + 1 < B:
            order += [("tc", b + 1, 0)]
        if b:
            order += [("wo", b - 1, 0)]
        order += [("tkv", b, j) for j in range(2)]
        if b + 1 < B:
            order += [("tx", b + 1, 0), ("k", b + 1, 0), ("v", b + 1, 0)]
        if b:
            order += [("t2", b - 1, 0)]
        if b + 1 < B:
            order += [("q", b + 1, 0)]
        order += [("qkv", b, j) for j in range(2)]
    order += [("wo", B - 1, 0)]
    bank = [n % 8 for n in range(len(order))]
    order += [("t2", B - 1, 0), ("lg", 0, 0), ("lg", 1, 0), ("tlg", 0, 0), ("pos", 0, 0)]
    bank += [5, 6, 7, 5, 6]
    return order, bank


def build_program(nc, x, ctx, attw, wch, adw, gw, bcol_d, bexp_d, brow_d, cst_d, dest_d, pre_d, xbuf, ybuf, out):
    ORDER, BANK = attention_groups()
    AT = {g: n for n, g in enumerate(ORDER)}

    with ExitStack() as stack:
        def sb(name, shape, dt, on=stack):
            return on.enter_context(nc.sbuf_tensor(name, shape, dt))

        def sem(name):
            return stack.enter_context(nc.semaphore(name))

        ps = [stack.enter_context(nc.psum_tensor(f"bank{i}", [P, 512], F32)) for i in range(8)]

        cst = sb("cst", [P, CCOLS], F32)
        ident = cst[:, C_ID:C_ID + P]
        tri_ones = sb("tri_ones", [P, 2 * P], BF16)
        ones = sb("ones", [P, FD], F32)
        bcol = sb("bcol", [P, BCOLS], F32)
        brow = sb("brow", [P, 3, D], F32)
        dest = sb("dest", [P, NT, 2], I32)
        gate_raw = sb("gate_raw", [P, KD, P], F32)
        gate_hi = sb("gate_hi", [P, KD, P], F32R)
        gate_lo = sb("gate_lo", [P, KD, P], F32R)
        res = sb("res", [P, NT, D], F32)
        rows = sb("rows", [P, NT, ROW], F32)
        xt_hi = sb("xt_hi", [P, KD, T], F32R)
        xt_lo = sb("xt_lo", [P, KD, T], F32R)
        raw = [sb(f"raw{q}", [P, CH], F32) for q in range(4)]
        raw_ad = sb("raw_ad", [P, AD], F32)
        sw_hi = [sb(f"sw_hi{q}", [P, CH], F32R) for q in range(4)]
        sw_lo = [sb(f"sw_lo{q}", [P, CH], F32R) for q in range(4)]
        sdn_hi = sb("sdn_hi", [P, KD, 3, RANK], F32R)
        sdn_lo = sb("sdn_lo", [P, KD, 3, RANK], F32R)
        sup = sb("sup", [AP3, D], F32R)
        lg = sb("lg", [P, NT, E], F32)
        z = sb("z", [P, NT, E], F32)
        hot = sb("hot", [P, NT, 2, E], F32)
        hot_bf = sb("hot_bf", [P, NT, 2, E], BF16)
        tmp16 = sb("tmp16", [P, NT, 2, E], F32)
        top = sb("top", [P, 2, NT], F32)
        rank = sb("rank", [P, NT, 2], F32)
        place = sb("place", [P, NT, 2], F32)
        slot = sb("slot", [P, NT, 2], F32)
        slot_i = sb("slot_i", [P, NT, 2], I32)
        pre = sb("pre", [P, ROW], F32)
        tmp_exp = sb("tmp_exp", [P, NT, E], F32)
        esum = sb("esum", [P, 3, NT], F32)
        stats2 = sb("stats2", [P, TT, 6], F32)
        mv2 = sb("mv2", [P, TT, 2], F32)
        sd2 = sb("sd2", [P, TT], F32)
        rstd2 = sb("rstd2", [P, TT], F32)
        nmr2 = sb("nmr2", [P, TT], F32)

        att = ExitStack()
        num = [sb(f"num{j}", [P, S], F32, att) for j in range(2)]
        den = [sb(f"den{j}", [P, S], F32, att) for j in range(2)]
        rden = [sb(f"rden{j}", [P, S], F32, att) for j in range(2)]
        o32 = sb("o32", [P, KD, S], F32, att)
        o_hi, o_lo = sb("o_hi", [P, KD, S], F32R, att), sb("o_lo", [P, KD, S], F32R, att)
        aw_hi = {i: sb(f"aw_hi{i}", [P, CH // 2], F32R, att) for i in (5, 0, 1, 2, 3, 4)}
        aw_lo = {i: sb(f"aw_lo{i}", [P, CH // 2], F32R, att) for i in (5, 0, 1, 2, 3, 4)}
        ctx_sb = sb("ctx_sb", [P, TT, D], F32, att)
        xn = sb("xn", [P, TT, D], F32, att)
        stats = sb("stats", [P, TT, 6], F32, att)
        mv = [sb(f"mv{i}", [P, TT, 2], F32, att) for i in range(2)]
        sd = [sb(f"sd{i}", [P, TT], F32, att) for i in range(2)]
        rstd = [sb(f"rstd{i}", [P, TT], F32, att) for i in range(2)]
        nmr = [sb(f"nmr{i}", [P, TT], F32, att) for i in range(2)]
        mask_hi = sb("mask_hi", [P, NT], F32R, att)
        mask_lo = sb("mask_lo", [P, NT], F32, att)
        ct_hi, ct_lo = sb("ct_hi", [P, KD, S], F32R, att), sb("ct_lo", [P, KD, S], F32R, att)
        nt_hi, nt_lo = sb("nt_hi", [P, KD, S], F32R, att), sb("nt_lo", [P, KD, S], F32R, att)
        k_hi, k_lo = sb("k_hi", [P, KD, S], F32R, att), sb("k_lo", [P, KD, S], F32R, att)
        q_hi, q_lo = sb("q_hi", [P, KD, S], F32R, att), sb("q_lo", [P, KD, S], F32R, att)
        v32 = sb("v32", [P, TT, D], F32, att)
        v_hi = sb("v_hi", [P, TT, 4, P], F32R, att)
        v_lo = sb("v_lo", [P, TT, 4, P], F32R, att)
        kf_hi, kf_lo = sb("kf_hi", [P, TT, 2, 512], F32R, att), sb("kf_lo", [P, TT, 2, 512], F32R, att)
        qf_hi, qf_lo = sb("qf_hi", [P, 8, S], F32R, att), sb("qf_lo", [P, 8, S], F32R, att)
        kvm = sb("kvm", [P, 4, S], F32, att)
        kvt_hi, kvt_lo = sb("kvt_hi", [P, 8, P], F32R, att), sb("kvt_lo", [P, 8, P], F32R, att)
        att.close()

        ffn = ExitStack()
        yk = sb("yk", [P, 2, NT, D], F32, ffn)
        yw = [sb(f"yw{i}", [SP, ST, D], F32, ffn) for i in range(2)]
        h_hi, h_lo = sb("h_hi", [P, MH, SLOTS], F32R, ffn), sb("h_lo", [P, MH, SLOTS], F32R, ffn)
        h32 = [sb(f"h32_{i}", [P, SLOTS], F32, ffn) for i in range(3)]
        a_st = sb("a_st", [AP3, SLOTS], F32R, ffn)
        ew_hi = [sb(f"ew_hi{q}", [P, CH], F32R, ffn) for q in range(4)]
        ew_lo = [sb(f"ew_lo{q}", [P, CH], F32R, ffn) for q in range(4)]
        dn_hi = sb("dn_hi", [P, KD, 3, RANK], F32R, ffn)
        dn_lo = sb("dn_lo", [P, KD, 3, RANK], F32R, ffn)
        up = sb("up", [AP3, D], F32R, ffn)
        bexp = [sb(f"bexp{i}", [P, NB], F32, ffn) for i in range(2)]
        xg = [sb(f"xg{i}", [SP, ST, D], F32, ffn) for i in range(2)]
        meta = [sb(f"meta{i}", [SP, ST, META], F32, ffn) for i in range(2)]
        xe_hi, xe_lo = sb("xe_hi", [P, KD, SLOTS], F32R, ffn), sb("xe_lo", [P, KD, SLOTS], F32R, ffn)
        ye = sb("ye", [P, KD, SLOTS], F32, ffn)
        lgt = sb("lgt", [E, T], F32, ffn)
        ffn.close()

        ident_ld, cst_ld, bcol_ld, brow_ld = sem("ident_ld"), sem("cst_ld"), sem("bcol_ld"), sem("brow_ld")
        misc_ld = sem("misc_ld")
        pre_ld = sem("pre_ld")
        x_in = [sem(f"x_in{b}") for b in range(B)]
        ctx_in = [sem(f"ctx_in{b}") for b in range(B)]
        aw_ld = [sem(f"aw_ld{i}") for i in range(6)]
        aw_hi_done, aw_lo_done = sem("aw_hi_done"), sem("aw_lo_done")
        prefilled = sem("prefilled")
        const_ready = sem("const_ready")
        gate_hi_done = sem("gate_hi_done")
        mask_hi_done = sem("mask_hi_done")
        pool_const, kvt_zeroed = sem("pool_const"), sem("kvt_zeroed")
        sb2_scaled = sem("sb2_scaled")
        att_full, att_evac, att_hi = sem("att_full"), sem("att_evac"), sem("att_hi")
        ln1_mv, ln1_sd, ln1_rs, ln1_out = sem("ln1_mv"), sem("ln1_sd"), sem("ln1_rs"), sem("ln1_out")
        ln2_mv, ln2_sd, ln2_rs, ln2_out = sem("ln2_mv"), sem("ln2_sd"), sem("ln2_rs"), sem("ln2_out")
        vmask = sem("vmask")
        bo_added, sb2_added = sem("bo_added"), sem("sb2_added")
        qkv_copied = sem("qkv_copied")
        inverted, divided, o_high, o_split = sem("inverted"), sem("divided"), sem("o_high"), sem("o_split")
        v_high, v_masked, v_split = sem("v_high"), sem("v_masked"), sem("v_split")
        kv_copied = sem("kv_copied")
        step = sem("step")
        z_ready, exp_done = sem("z_ready"), sem("exp_done")
        meta_ids = sem("meta_ids")
        hot_ready = sem("hot_ready")
        slots_ready = sem("slots_ready")
        dispatched = sem("dispatched")
        w_ld = [sem(f"w_ld{q}") for q in range(4)]
        w_hi = [sem(f"w_hi{q}") for q in range(4)]
        w_lo = [sem(f"w_lo{q}") for q in range(4)]
        ad_ld, ad_hi, ad_lo = sem("ad_ld"), sem("ad_hi"), sem("ad_lo")
        bias_ld = [sem(f"bias_ld{i}") for i in range(2)]
        g1_full, gelu_done, h_hi_done, h_split = sem("g1_full"), sem("gelu_done"), sem("h_hi_done"), sem("h_split")
        sh_full, sh_evac = sem("sh_full"), sem("sh_evac")
        y_full, y_evac = sem("y_full"), sem("y_evac")
        xg_ld = [sem(f"xg_ld{i}") for i in range(2)]
        meta_ld = [sem(f"meta_ld{i}") for i in range(2)]
        tin_full, tin_hi, tin_evac = sem("tin_full"), sem("tin_hi"), sem("tin_evac")
        tout_full, tout_evac = sem("tout_full"), sem("tout_evac")
        y_sent = [sem(f"y_sent{i}") for i in range(2)]
        yk_ld = [sem(f"yk_ld{i}") for i in range(2)]
        early_out = sem("early_out")
        stored = sem("stored")

        LAST_ATT = AT[("wo", B - 1, 0)] + 1

        def split3(w_h, w_l, m_h, m_l):
            return ((w_h, m_h), (w_h, m_l), (w_l, m_h))

        def kv_blocks(dst, b, j, i):
            c = HD * (2 * j + i)
            half = slice(FD * i, FD * i + FD)
            kept = lambda ap: ap.rearrange("p g (s x) -> p g s x", s=2)[:, :, :, c:c + HD]
            return (kept(dst[half, j::2, :]),
                    kept(ps[BANK[AT[("tkv", b, j)]]][half, :].rearrange("p (g x) -> p g x", g=4)))

        def raw_aw(i):
            return raw[1 + i // 2][:, (i % 2) * (CH // 2):(i % 2 + 1) * (CH // 2)]

        def xtok(b):
            return x[b].rearrange("(t p) d -> p t d", p=P)

        EVAC = {g: sum(other[0] not in ("kv", "qkv") for other in ORDER[:n + 1]) for g, n in AT.items()}

        def wait_finished(eng, group):
            if group[0] == "kv":
                eng.wait_ge(kv_copied, 2 * group[1] + group[2] + 1)
            elif group[0] == "qkv":
                eng.wait_ge(qkv_copied, 4 * (2 * group[1] + group[2] + 1))
            else:
                eng.wait_ge(att_evac, EVAC[group])

        def wait_bank(eng, bank):
            wait_finished(eng, [ORDER[n] for n in range(LAST_ATT) if BANK[n] == bank][-1])

        block = stack.enter_context(nc.Block())

        @block.sync
        def _(eng):
            def load_raw(u, q):
                eng.dma_start(raw[q][:, :], wch[u, q]).then_inc(w_ld[q], 16)

            def load_adapter(u):
                eng.dma_start(raw_ad[:, :], adw[u]).then_inc(ad_ld, 16)

            def load_rows(e, par):
                eng.dma_start(xg[par][:, :, :],
                              xbuf[bass.ds(e * SLOTS, SLOTS), 0:D].rearrange("(j p) c -> p j c", p=SP)
                              ).then_inc(xg_ld[par], 16)

            def load_meta(e, par):
                eng.dma_start(meta[par][:, :, :],
                              xbuf[bass.ds(e * SLOTS, SLOTS), D:ROW].rearrange("(j p) c -> p j c", p=SP)
                              ).then_inc(meta_ld[par], 16)

            eng.dma_start(res[:, 0:TT, :], xtok(0)).then_inc(x_in[0], 16)
            eng.dma_start(cst[:, 0:P], cst_d[:, 0:P]).then_inc(ident_ld, 16)
            for i in range(3):
                eng.dma_start(raw_aw(i), attw[i]).then_inc(aw_ld[i], 16)
            eng.dma_start(brow[:, :, :], brow_d.partition_broadcast(P)).then_inc(brow_ld, 16)
            for i in range(3, 6):
                eng.dma_start(raw_aw(i), attw[i]).then_inc(aw_ld[i], 16)
            eng.dma_start(res[:, TT:2 * TT, :], xtok(1)).then_inc(x_in[1], 16)
            eng.dma_start(cst[:, P:CCOLS], cst_d[:, P:CCOLS]).then_inc(cst_ld, 16)
            for b in range(2, B):
                eng.dma_start(res[:, TT * b:TT * b + TT, :], xtok(b)).then_inc(x_in[b], 16)
            eng.dma_start(dest[:, :, :], dest_d).then_inc(misc_ld, 16)
            eng.dma_start(gate_raw[:, :, :], gw).then_inc(misc_ld, 16)
            eng.dma_start(pre[:, :], pre_d).then_inc(pre_ld, 16)
            load_raw(0, 0)
            load_adapter(0)
            for q in range(1, 4):
                eng.wait_ge(aw_lo_done, 2 * q)
                load_raw(0, q)
            for b in range(1, B):
                eng.wait_ge(att_full, AT[("tc", b - 1, 0)] + 1)
                eng.dma_start(ctx_sb[:, :, :],
                              ctx[b].rearrange("(t p) d -> p t d", p=P)).then_inc(ctx_in[b], 16)
            eng.wait_ge(pre_ld, 16)
            eng.dma_start(xbuf.rearrange("(a p) c -> p a c", p=P),
                          pre[:, :].unsqueeze(1).to_broadcast([P, E * SLOTS // P, ROW])).then_inc(prefilled, 16)
            eng.dma_start(ybuf.rearrange("(a p) c -> p a c", p=P),
                          pre[:, 0:D].unsqueeze(1).to_broadcast([P, 2 * NT, D])).then_inc(prefilled, 16)

            def load_expert_weights(e):
                for q in range(4):
                    eng.wait_ge(w_lo[q], e + 1)
                    load_raw(e + 1, q)
                    if q == 1:
                        eng.wait_ge(ad_lo, 2 * e + 2)
                        load_adapter(e + 1)

            load_expert_weights(0)
            eng.wait_ge(dispatched, 16 * 2 * NT)
            load_rows(0, 0)

            def load_bias(e, par):
                eng.dma_start(bexp[par][:, :], bexp_d[e]).then_inc(bias_ld[par], 16)

            def step_loads(e, par, sent=None):
                if sent is not None:
                    eng.wait_ge(tin_full, 2 * e)
                load_rows(e + 1, 1 - par)
                load_expert_weights(e + 1)
                if sent is not None:
                    eng.wait_ge(y_evac, 2 * e)
                load_bias(e + 1, 1 - par)
                if sent is not None and not (isinstance(e, int) and e == 1):
                    eng.wait_ge(y_sent[par], sent)
                load_meta(e, par)

            load_bias(0, 0)
            step_loads(0, 0)
            step_loads(1, 1, 0)
            step_loads(2, 0, 64)
            with eng.Fori(1, 3) as i:
                step_loads(2 * i + 1, 1, 64 * i)
                step_loads(2 * i + 2, 0, 64 * i + 64)
            eng.wait_ge(y_sent[1], 64 * (E // 2 - 1))
            load_meta(E - 1, 1)

            for i in range(2):
                eng.wait_ge(y_sent[i], 64 * (E // 2))
            yview = ybuf.rearrange("(k t p) d -> p k t d", k=2, p=P)
            for k in range(2):
                eng.dma_start(yk[:, k, 0:NT - TT, :], yview[:, k, 0:NT - TT]).then_inc(yk_ld[0], 16)
            for k in range(2):
                eng.dma_start(yk[:, k, NT - TT:NT, :], yview[:, k, NT - TT:NT]).then_inc(yk_ld[1], 16)
            oview = out.rearrange("b (t p) d -> p (b t) d", p=P)
            eng.wait_ge(early_out, 1)
            eng.dma_start(oview[:, 0:NT - TT], res[:, 0:NT - TT, :]).then_inc(stored, 16)
            eng.wait_ge(early_out, 2)
            eng.dma_start(oview[:, NT - TT:NT], res[:, NT - TT:NT, :]).then_inc(stored, 16)
            eng.wait_ge(stored, 32)

        @block.gpsimd
        def _(eng):
            g = nc.gpsimd
            last_slot, last_row = eng.to_reg(E * SLOTS - 1), eng.to_reg(2 * T - 1)
            g.memset(ones[:, :], 1.0).then_inc(pool_const, 1)
            def mask_columns(b):
                if b:
                    eng.wait_ge(att_full, AT[("kv", b - 1, 1)] + 1)
                for tt in range(TT):
                    for dst, m in ((v_hi, bcol[:, MK + TT * b + tt:MK + TT * b + tt + 1]),
                                   (v_lo, mask_lo[:, TT * b + tt:TT * b + tt + 1])):
                        g.tensor_scalar(dst[:, tt, :, FD:P], ones[:, :].unsqueeze(1).to_broadcast([P, 4, FD]),
                                        m, None, ALU.mult).then_inc(vmask, 1)

            def add_row(b, i, done):
                tok = res[:, TT * b:TT * b + TT, :]
                g.tensor_tensor(tok, tok, brow[:, i, :].unsqueeze(1).to_broadcast([P, TT, D]),
                                ALU.add).then_inc(done, 1)

            def values_low(b):
                eng.wait_ge(v_high, TT * b + TT)
                for tt in range(TT):
                    m = bcol[:, MK + TT * b + tt:MK + TT * b + tt + 1]
                    g.tensor_scalar(v32[:, tt, :], v32[:, tt, :], m, None, ALU.mult).then_inc(v_masked, 1)
                eng.wait_ge(v_masked, TT * b + TT)
                for tt in range(TT):
                    g.tensor_tensor(v_lo[:, tt, :, 0:FD], v32[:, tt, :].rearrange("p (g c) -> p g c", g=4),
                                    v_hi[:, tt, :, 0:FD], ALU.subtract).then_inc(v_split, 1)

            def low_half(dst, src, hi):
                return g.tensor_tensor(dst[:, :], src[:, :], hi[:, :], ALU.subtract)

            for t in (kvt_hi, kvt_lo):
                g.memset(t[:, :, :].bitcast(F32), 0.0).then_inc(kvt_zeroed, 1)
            eng.wait_ge(pool_const, 1)
            eng.wait_ge(const_ready, 1)
            mask_columns(0)
            values_low(0)
            eng.wait_ge(brow_ld, 16)
            g.tensor_scalar(brow[:, 2, :], brow[:, 2, :], 0.2, None, ALU.mult).then_inc(sb2_scaled, 1)
            eng.wait_ge(misc_ld, 32)
            for k in range(2):
                g.tensor_copy(rows[:, :, D + 1 + 2 * k].bitcast(I32), dest[:, :, k]).then_inc(meta_ids, 1)
            def divide(b):
                for j in range(2):
                    n = 2 * b + j
                    eng.wait_ge(qkv_copied, 4 * n + 4)
                    eng.wait_ge(inverted, n + 1)
                    g.tensor_tensor(o32[:, j, :], num[j][:, :], rden[j][:, :], ALU.mult).then_inc(divided, 1)
                    eng.wait_ge(o_high, n + 1)
                    g.tensor_tensor(o_lo[:, j, :], o32[:, j, :], o_hi[:, j, :], ALU.subtract).then_inc(o_split, 1)

            def add_sb2(b):
                eng.wait_ge(ln2_out, TT * b + TT)
                add_row(b, 2, sb2_added)

            eng.wait_ge(sb2_scaled, 1)
            for b in range(B):
                if b:
                    divide(b - 1)
                eng.wait_ge(ln1_out, TT * b + TT)
                add_row(b, 1, bo_added)
                if b > 1:
                    add_sb2(b - 2)
                if b + 1 < B:
                    mask_columns(b + 1)
                    values_low(b + 1)
                eng.wait_ge(w_hi[b], 1)
                low_half(sw_lo[b], raw[b], sw_hi[b]).then_inc(w_lo[b], 1)
            divide(B - 1)
            for b in range(B - 2, B):
                add_sb2(b)

            def expert_low(e, q):
                eng.wait_ge(w_hi[q], e + 2)
                low_half(ew_lo[q], raw[q], ew_hi[q]).then_inc(w_lo[q], 1)

            expert_low(0, 0)
            eng.wait_ge(prefilled, 32)
            eng.wait_ge(slots_ready, 1)
            eng.wait_ge(meta_ids, 2)
            for t in range(NT):
                for k in range(2):
                    g.indirect_dma_start(out=xbuf, out_offset=bass.IndirectOffsetOnAxis(ap=slot_i[:, t, k:k + 1], axis=0),
                                         in_=rows[:, t, :], in_offset=None,
                                         bounds_check=last_slot, oob_is_err=False).then_inc(dispatched, 16)
            expert_low(0, 1)

            def send_rows(par):
                for j in range(ST):
                    choice = j // (ST // 2)
                    idx = meta[par][:, j, 1 + 2 * choice:2 + 2 * choice].bitcast(I32)
                    g.indirect_dma_start(out=ybuf, out_offset=bass.IndirectOffsetOnAxis(ap=idx, axis=0),
                                         in_=yw[par][:, j, :], in_offset=None,
                                         bounds_check=last_row, oob_is_err=False).then_inc(y_sent[par], 16)

            def expert(e, par):
                expert_low(e, 2)
                expert_low(e, 3)
                eng.wait_ge(tout_evac, 2 * e)
                expert_low(e + 1, 1)
                send_rows(1 - par)

            expert_low(0, 2)
            expert_low(0, 3)
            expert_low(1, 1)
            with eng.Fori(0, 3) as i:
                expert(2 * i + 1, 1)
                expert(2 * i + 2, 0)
            expert_low(E - 1, 2)
            expert_low(E - 1, 3)
            eng.wait_ge(tout_evac, 2 * E - 2)
            send_rows(0)
            eng.wait_ge(tout_evac, 2 * E)
            send_rows(1)

        @block.scalar
        def _(eng):
            a = nc.scalar
            eng.dma_start(ctx_sb[:, :, :], ctx[0].rearrange("(t p) d -> p t d", p=P)).then_inc(ctx_in[0], 16)
            eng.dma_start(bcol[:, :], bcol_d).then_inc(bcol_ld, 16)

            def full(stage, b, j=0):
                eng.wait_ge(att_full, AT[(stage, b, j)] + 1)

            def hi_done(ins):
                ins.then_inc(att_hi, 1)

            def chunk_hi(i):
                eng.wait_ge(aw_ld[i], 16)
                a.activation(aw_hi[i][:, :], raw_aw(i), ACT.Copy).then_inc(aw_hi_done, 1)

            def ln_sqrt(mvt, sdt, s_mv, s_sd, b):
                eng.wait_ge(s_mv, TT * b + TT)
                a.activation(sdt[:, :], mvt[:, :, 1], ACT.Sqrt, bias=LN_EPS).then_inc(s_sd, 1)

            def ln_apply(dst, rs, nm, s_rs, s_out, b):
                eng.wait_ge(s_rs, 2 * b + 2)
                for tt in range(TT):
                    a.activation(dst(tt), res[:, TT * b + tt, :], ACT.Identity,
                                 scale=rs[:, tt:tt + 1], bias=nm[:, tt:tt + 1]).then_inc(s_out, 1)

            def ln1_sqrt(b):
                ln_sqrt(mv[b % 2], sd[b % 2], ln1_mv, ln1_sd, b)

            def ln1_apply(b):
                if b:
                    full("tx", b - 1)
                ln_apply(lambda tt: xn[:, tt, :], rstd[b % 2], nmr[b % 2], ln1_rs, ln1_out, b)

            def ln2_apply(b):
                ln_apply(lambda tt: rows[:, TT * b + tt, 0:D], rstd2, nmr2, ln2_rs, ln2_out, b)

            def turned_hi(stage, dst, b):
                full(stage, b)
                hi_done(a.activation(dst[:, :, :], ps[BANK[AT[(stage, b, 0)]]][:, :], ACT.Copy))

            def biased_hi(stage, dst, c, b):
                full(stage, b)
                bank = ps[BANK[AT[(stage, b, 0)]]]
                for m in range(KD):
                    hi_done(a.activation(dst[:, m, :], bank[:, S * m:S * m + S], ACT.Identity,
                                         bias=bcol[:, c + m:c + m + 1]))

            def values_hi(b):
                wait_finished(eng, ("v", b, 0))
                for tt in range(TT):
                    a.activation(v_hi[:, tt, :, 0:FD], v32[:, tt, :].rearrange("p (g c) -> p g c", g=4), ACT.Copy,
                                 scale=bcol[:, MK + TT * b + tt:MK + TT * b + tt + 1]).then_inc(v_high, 1)

            def features_hi(stage, dst, b, js):
                for j in js:
                    full(stage, b, j)
                    hi_done(a.activation(dst(j), ps[BANK[AT[(stage, b, j)]]][:, :], ACT.Relu))

            def shared_weights_hi(q):
                eng.wait_ge(w_ld[q], 16)
                a.activation(sw_hi[q][:, :], raw[q][:, :], ACT.Copy).then_inc(w_hi[q], 1)

            def normed_hi(b):
                full("t2", b)
                hi_done(a.activation(xt_hi[:, :, S * b:S * b + S],
                                     ps[BANK[AT[("t2", b, 0)]]][:, :].rearrange("p (k n) -> p k n", k=KD), ACT.Copy))

            ln1_sqrt(0)
            chunk_hi(0)
            ln1_apply(0)
            turned_hi("tc", ct_hi, 0)
            chunk_hi(1)
            turned_hi("tx", nt_hi, 0)
            chunk_hi(2)
            chunk_hi(3)
            eng.wait_ge(bcol_ld, 16)
            a.activation(mask_hi[:, :], bcol[:, MK:MK + NT], ACT.Copy).then_inc(mask_hi_done, 1)
            biased_hi("k", k_hi, BK, 0)
            values_hi(0)
            biased_hi("q", q_hi, BQ, 0)
            chunk_hi(4)
            chunk_hi(5)
            ln1_sqrt(1)
            eng.wait_ge(misc_ld, 32)
            a.activation(gate_hi[:, :, :], gate_raw[:, :, :], ACT.Copy).then_inc(gate_hi_done, 1)

            def quotients(b):
                for j in range(2):
                    full("qkv", b, j)
                    bank = ps[BANK[AT[("qkv", b, j)]]]
                    for i in range(2):
                        a.activation(den[j][FD * i:FD * i + FD, :], bank[FD:P, S * i:S * i + S], ACT.Identity,
                                     bias=DEN_EPS).then_inc(qkv_copied, 1)
                    for i in range(2):
                        a.activation(num[j][FD * i:FD * i + FD, :], bank[0:FD, S * i:S * i + S], ACT.Copy).then_inc(qkv_copied, 1)

            def quotients_hi(b, j):
                eng.wait_ge(divided, 2 * b + j + 1)
                a.activation(o_hi[:, j, :], o32[:, j, :], ACT.Copy).then_inc(o_high, 1)

            queries = lambda j: qf_hi[:, 2 * j:2 * j + 2, :]
            for b in range(B):
                features_hi("kf", lambda j: kf_hi[:, j // 2, j % 2, :], b, range(4))
                if b + 1 < B:
                    ln1_apply(b + 1)
                features_hi("qf", queries, b, range(2))
                if b:
                    quotients_hi(b - 1, 0)
                features_hi("qf", queries, b, range(2, 4))
                if b:
                    quotients_hi(b - 1, 1)
                for j in range(2):
                    full("kv", b, j)
                    a.activation(kvm[:, 2 * j:2 * j + 2, :], ps[BANK[AT[("kv", b, j)]]][:, :], ACT.Copy).then_inc(kv_copied, 1)
                if b + 2 < B:
                    ln1_sqrt(b + 2)
                if b + 1 < B:
                    turned_hi("tc", ct_hi, b + 1)
                for j in range(2):
                    full("tkv", b, j)
                    for i in range(2):
                        dst, src = kv_blocks(kvt_hi, b, j, i)
                        hi_done(a.activation(dst, src, ACT.Copy))
                if b:
                    ln_sqrt(mv2, sd2, ln2_mv, ln2_sd, b - 1)
                if b + 1 < B:
                    turned_hi("tx", nt_hi, b + 1)
                    biased_hi("k", k_hi, BK, b + 1)
                if b:
                    ln2_apply(b - 1)
                shared_weights_hi(b)
                if b + 1 < B:
                    values_hi(b + 1)
                if b:
                    normed_hi(b - 1)
                if b + 1 < B:
                    biased_hi("q", q_hi, BQ, b + 1)
                if b == 1:
                    eng.wait_ge(ad_ld, 16)
                    a.activation(sdn_hi[:, :, :, :], raw_ad[:, 0:KD * RANK].rearrange("p (k r) -> p k r", k=KD).unsqueeze(2).to_broadcast([P, KD, 3, RANK]), ACT.Copy).then_inc(ad_hi, 1)
                    a.activation(sup[:, :], raw_ad[0:AP3, KD * RANK:AD], ACT.Copy).then_inc(ad_hi, 1)
                quotients(b)
            for j in range(2):
                quotients_hi(B - 1, j)

            def gelu_groups(body, ms, n, bias):
                for m in ms:
                    g0 = body * NG + m
                    eng.wait_ge(g1_full, g0 + 1)
                    if not isinstance(body, int) or g0 >= 3:
                        eng.wait_ge(h_split, g0 - 2)
                    if m < MH:
                        a.activation(h32[m % 3][:, 0:n], ps[m % 3][:, 0:n], ACT.Gelu,
                                     bias=bias[:, m:m + 1]).then_inc(gelu_done, 1)
                    else:
                        a.activation(h32[m % 3][0:AP3, 0:n], ps[m % 3][0:AP3, 0:n], ACT.Gelu).then_inc(gelu_done, 1)

            shared_bias = bcol[:, 0:NB]

            def expert_hi(e, q):
                if isinstance(e, int) and e == 0:
                    eng.wait_ge(att_full, LAST_ATT)
                elif q < 2:
                    eng.wait_ge(g1_full, (e - 1 + FIRST) * NG + 4 * q + 4)
                else:
                    eng.wait_ge(y_full, 2 * e)
                eng.wait_ge(w_ld[q], 16 * e + 32)
                a.activation(ew_hi[q][:, :], raw[q][:, :], ACT.Copy).then_inc(w_hi[q], 1)

            def down_hi(e):
                if not (isinstance(e, int) and e == 0):
                    eng.wait_ge(g1_full, (e - 1 + FIRST) * NG + NG)
                eng.wait_ge(ad_ld, 16 * e + 32)
                a.activation(dn_hi[:, :, :, :], raw_ad[:, 0:KD * RANK].rearrange("p (k r) -> p k r", k=KD).unsqueeze(2).to_broadcast([P, KD, 3, RANK]), ACT.Copy).then_inc(ad_hi, 1)

            def up_hi(e):
                a.activation(up[:, :], raw_ad[0:AP3, KD * RANK:AD], ACT.Copy).then_inc(ad_hi, 1)

            def rows_hi(e, par):
                for k in range(KD):
                    eng.wait_ge(tin_full, 2 * e + 1 + k)
                    a.activation(xe_hi[:, k, :], ps[5 + k][:, 0:SLOTS], ACT.Copy).then_inc(tin_hi, 1)

            ln_sqrt(mv2, sd2, ln2_mv, ln2_sd, B - 1)
            ln2_apply(B - 1)
            gelu_groups(0, range(NG), S, shared_bias)
            normed_hi(B - 1)
            expert_hi(0, 0)
            eng.wait_ge(z_ready, 1)
            a.activation(tmp_exp[:, :, :], z[:, :, :], ACT.Exp).then_inc(exp_done, 1)
            eng.wait_ge(z_ready, 2)
            a.activation(esum[:, 1, :], top[:, 1, :], ACT.Exp).then_inc(exp_done, 1)
            expert_hi(0, 1)
            gelu_groups(1, range(NG), S, shared_bias)
            down_hi(0)
            gelu_groups(2, range(NG), S, shared_bias)
            rows_hi(0, 0)

            def expert(e, par, bias_seen, last=False):
                body = e + FIRST
                eng.wait_ge(bias_ld[par], bias_seen)
                gelu_groups(body, range(2), SLOTS, bexp[par])
                expert_hi(e, 2)
                gelu_groups(body, range(2, 4), SLOTS, bexp[par])
                expert_hi(e, 3)
                gelu_groups(body, range(4, 6), SLOTS, bexp[par])
                up_hi(e)
                gelu_groups(body, range(6, NG), SLOTS, bexp[par])
                if not last:
                    expert_hi(e + 1, 0)
                    expert_hi(e + 1, 1)
                    down_hi(e + 1)
                    rows_hi(e + 1, 1 - par)
                for d in range(KD):
                    eng.wait_ge(y_full, 2 * e + 1 + d)
                    a.activation(ye[:, d, :], ps[3 + d][:, 0:SLOTS], ACT.Identity,
                                 bias=bexp[par][:, MH + d:MH + d + 1]).then_inc(y_evac, 1)

            expert(0, 0, 16)
            with eng.Fori(0, 3) as i:
                expert(2 * i + 1, 1, 16 * i + 16)
                expert(2 * i + 2, 0, 16 * i + 32)
            expert(E - 1, 1, 64, last=True)
            gelu_groups(LAST, range(NG), S, shared_bias)

        @block.tensor
        def _(eng):
            pe = nc.tensor

            def mm(dst, pairs, last_inc=None, start=True, stop=True):
                for n, (w, m) in enumerate(pairs):
                    ins = pe.matmul(dst, w, m, start=start and n == 0, stop=stop and n == len(pairs) - 1)
                return ins

            def bank_of(g):
                n = AT[g]
                before = [ORDER[i] for i in range(n) if BANK[i] == BANK[n]]
                if before:
                    wait_finished(eng, before[-1])
                return ps[BANK[n]]

            def done(stage, b, j=0):
                wait_finished(eng, (stage, b, j))

            def full(ins):
                ins.then_inc(att_full, 1)

            def turn(g, src):
                bank = bank_of(g)
                for k in range(KD):
                    for tt in range(TT):
                        ins = pe.transpose(bank[:, k * S + tt * P:k * S + tt * P + P],
                                           src(tt)[:, k * P:k * P + P], ident)
                full(ins)

            def aw(i, c, n):
                return aw_hi[i][:, c:c + n], aw_lo[i][:, c:c + n]

            def project(stage, b, i, src_hi, src_lo):
                bank = bank_of((stage, b, 0))
                for m in range(KD):
                    pairs = []
                    for k in range(KD):
                        wh, wl = aw(i, k * D + m * P, P)
                        pairs += split3(wh, wl, src_hi[:, k, :], src_lo[:, k, :])
                    ins = mm(bank[:, m * S:m * S + S], pairs)
                full(ins)

            def project_rows(g, i, src_hi, src_lo):
                bank = bank_of(g)
                for tt in range(TT):
                    pairs = []
                    for k in range(KD):
                        mh, ml = aw(i, k * D, D)
                        pairs += split3(src_hi[:, k, tt * P:tt * P + P], src_lo[:, k, tt * P:tt * P + P], mh, ml)
                    ins = mm(bank[:, tt * D:tt * D + D], pairs)
                full(ins)

            def turn_context(b):
                eng.wait_ge(ctx_in[b], 16)
                turn(("tc", b, 0), lambda tt: ctx_sb[:, tt, :])

            def turn_queries(b):
                eng.wait_ge(ln1_out, TT * b + TT)
                turn(("tx", b, 0), lambda tt: xn[:, tt, :])

            def project_keys(b):
                if b == 0:
                    eng.wait_ge(aw_lo_done, 1)
                done("tc", b)
                project("k", b, 0, ct_hi, ct_lo)

            def project_values(b):
                if b == 0:
                    eng.wait_ge(aw_lo_done, 2)
                project_rows(("v", b, 0), 1, ct_hi, ct_lo)

            def project_queries(b):
                if b == 0:
                    eng.wait_ge(aw_lo_done, 3)
                done("tx", b)
                project("q", b, 2, nt_hi, nt_lo)

            def key_features(b):
                done("k", b)
                if b == 0:
                    eng.wait_ge(aw_lo_done, 4)
                for j in range(4):
                    tt, k = j // 2, j % 2
                    bank = bank_of(("kf", b, j))
                    full(mm(bank[:, :], split3(k_hi[:, k, tt * P:tt * P + P], k_lo[:, k, tt * P:tt * P + P], *aw(3, 0, 512))))

            def query_features(b):
                done("q", b)
                if b == 0:
                    eng.wait_ge(aw_lo_done, 5)
                for j in range(4):
                    bank = bank_of(("qf", b, j))
                    for i in range(2):
                        m = 2 * j + i
                        wh, wl = aw(4, (m % 4) * P, P)
                        ins = mm(bank[:, i * S:i * S + S], split3(wh, wl, q_hi[:, m // 4, :], q_lo[:, m // 4, :]))
                    full(ins)

            def attention_out(b):
                eng.wait_ge(o_split, 2 * b + 2)
                if b == 0:
                    eng.wait_ge(aw_lo_done, 6)
                project_rows(("wo", b, 0), 5, o_hi, o_lo)

            def turn_normed(b):
                eng.wait_ge(ln2_out, TT * b + TT)
                turn(("t2", b, 0), lambda tt: rows[:, TT * b + tt, 0:D])

            def key_values(b):
                eng.wait_ge(v_split, TT * b + TT)
                eng.wait_ge(vmask, 4 * b + 4)
                for j in range(2):
                    bank = bank_of(("kv", b, j))
                    for i in range(2):
                        g = 2 * j + i
                        pairs = []
                        for tt in range(TT):
                            done("kf", b, 2 * tt + g // 2)
                            c = (g % 2) * S
                            pairs += split3(v_hi[:, tt, g, :], v_lo[:, tt, g, :],
                                            kf_hi[:, tt, g // 2, c:c + S], kf_lo[:, tt, g // 2, c:c + S])
                        ins = mm(bank[:, i * S:i * S + S], pairs)
                    full(ins)

            def turn_key_values(b):
                done("kv", b, 1)
                for j in range(2):
                    bank = bank_of(("tkv", b, j))
                    for g in range(4):
                        ins = pe.transpose(bank[:, g * P:g * P + P], kvm[:, g, j * P:j * P + P], ident)
                    full(ins)

            def attend(b):
                done("tkv", b, 1)
                if b == 0:
                    eng.wait_ge(kvt_zeroed, 2)
                for j in range(2):
                    bank = bank_of(("qkv", b, j))
                    for i in range(2):
                        g = 2 * j + i
                        done("qf", b, g)
                        pairs = []
                        for c in range(2):
                            pairs += split3(kvt_hi[:, 2 * g + c, :], kvt_lo[:, 2 * g + c, :],
                                            qf_hi[:, 2 * g + c, :], qf_lo[:, 2 * g + c, :])
                        ins = mm(bank[:, i * S:i * S + S], pairs)
                    full(ins)

            eng.wait_ge(ident_ld, 16)
            turn_context(0)
            turn_queries(0)
            project_keys(0)
            project_values(0)
            project_queries(0)
            for b in range(B):
                key_features(b)
                query_features(b)
                key_values(b)
                if b + 1 < B:
                    turn_context(b + 1)
                if b:
                    attention_out(b - 1)
                turn_key_values(b)
                if b + 1 < B:
                    turn_queries(b + 1)
                    project_keys(b + 1)
                    project_values(b + 1)
                if b:
                    turn_normed(b - 1)
                if b + 1 < B:
                    project_queries(b + 1)
                attend(b)
            attention_out(B - 1)

            def hidden(body, ms, n, wh, wl, dh, dl, mh, ml):
                for m in ms:
                    g0 = body * NG + m
                    if isinstance(body, int) and g0 < 3:
                        wait_bank(eng, m)
                    else:
                        eng.wait_ge(gelu_done, g0 - 2)
                    pairs = []
                    for k in range(KD):
                        if m < MH:
                            c = k * 512 + (m % 4) * P
                            st = (wh[m // 4][:, c:c + P], wl[m // 4][:, c:c + P])
                        else:
                            st = (dh[:, k, :, :].rearrange("p a r -> p (a r)"), dl[:, k, :, :].rearrange("p a r -> p (a r)"))
                        pairs += split3(*st, mh(k), ml(k))
                    rowsn = P if m < MH else AP3
                    mm(ps[m % 3][0:rowsn, 0:n], pairs).then_inc(g1_full, 1)

            def shared_hidden(body, c, ms):
                hidden(body, ms, S, sw_hi, sw_lo, sdn_hi, sdn_lo,
                       lambda k: xt_hi[:, k, S * c:S * c + S], lambda k: xt_lo[:, k, S * c:S * c + S])

            def shared_out(body, n, tts):
                for tt in tts:
                    if n:
                        eng.wait_ge(sh_evac, TT * (n - 1) + tt + 1)
                    elif tt == 0:
                        for bank in (3, 4):
                            wait_bank(eng, bank)
                    if body == LAST:
                        eng.wait_ge(y_evac, 2 * E)
                    tok = slice(tt * P, tt * P + P)
                    for m in range(MH):
                        if tt == tts[0]:
                            eng.wait_ge(h_split, body * NG + m + 1)
                        c = (m % 4) * D
                        mm(ps[3 + tt][:, 0:D], split3(h_hi[:, m, tok], h_lo[:, m, tok],
                                                      sw_hi[2 + m // 4][:, c:c + D], sw_lo[2 + m // 4][:, c:c + D]),
                           start=m == 0, stop=False)
                    eng.wait_ge(h_split, body * NG + NG)
                    pe.matmul(ps[3 + tt][:, 0:D], a_st[:, tok], sup[:, :], start=False, stop=True).then_inc(sh_full, 1)

            for q in range(2):
                eng.wait_ge(w_lo[q], 1)
            eng.wait_ge(ad_lo, 2)
            done("t2", 0)
            shared_hidden(0, 0, range(NG))
            turn_normed(B - 1)
            done("t2", B - 1)
            eng.wait_ge(const_ready, 3)
            for half in range(2):
                bank = bank_of(("lg", half, 0))
                pairs = []
                for k in range(KD):
                    c = half * 512
                    pairs += split3(gate_hi[:, k, :], gate_lo[:, k, :], xt_hi[:, k, c:c + 512], xt_lo[:, k, c:c + 512])
                full(mm(bank[:, :], pairs))
            for q in range(2, 4):
                eng.wait_ge(w_lo[q], 1)
            shared_out(0, 0, [0])
            done("lg", 1)
            bank = bank_of(("tlg", 0, 0))
            for t in range(NT):
                ins = pe.transpose(bank[:, E * t:E * t + E], lgt[:, P * t:P * t + P], ident[0:E, 0:E])
            full(ins)
            shared_out(0, 0, [1])
            shared_hidden(1, 1, range(0, 4))
            eng.wait_ge(hot_ready, 1)
            bank = bank_of(("pos", 0, 0))
            tri, one = tri_ones[:, 0:P], tri_ones[:, P:2 * P]
            width = 2 * E
            pe.matmul(bank[:, 0:NT * width], tri, hot_bf[:, :, :, :], start=True, stop=False)
            for t in range(NT - 1):
                ins = pe.matmul(bank[:, (t + 1) * width:NT * width], one,
                                hot_bf[:, t, :, :].rearrange("p k e -> p (k e)").unsqueeze(1).to_broadcast([P, NT - 1 - t, width]),
                                start=False, stop=t == NT - 2)
            full(ins)
            shared_hidden(1, 1, range(4, NG))
            shared_out(1, 1, [0, 1])
            shared_hidden(2, 2, range(NG))

            def rows_in(e, par, seen):
                eng.wait_ge(xg_ld[par], seen)
                if isinstance(e, int) and e == 0:
                    done("pos", 0)
                elif not (isinstance(e, int) and e == 1):
                    eng.wait_ge(tout_evac, 2 * e - 2)
                for k in range(KD):
                    for j in range(ST):
                        ins = pe.transpose(ps[5 + k][:, j * SP:j * SP + SP],
                                           xg[par][:, j, k * P:k * P + P], ident[0:SP, 0:SP])
                    ins.then_inc(tin_full, 1)

            def rows_out(e):
                eng.wait_ge(y_evac, 2 * e + 2)
                if not (isinstance(e, int) and e == 0):
                    eng.wait_ge(tout_evac, 2 * e)
                for j in range(ST):
                    bank = ps[7] if j < 2 else ps[5]
                    for d in range(KD):
                        c = (j % 2) * D + d * P
                        ins = pe.transpose(bank[0:SP, c:c + P], ye[:, d, j * SP:j * SP + SP], ident)
                    if j % 2:
                        ins.then_inc(tout_full, 1)

            rows_in(0, 0, 16)
            shared_out(2, 2, [0, 1])

            def expert(e, par, seen, first=False, last=False):
                body = e + FIRST
                half = lambda ms: hidden(body, ms, SLOTS, ew_hi, ew_lo, dn_hi, dn_lo,
                                         lambda k: xe_hi[:, k, :], lambda k: xe_lo[:, k, :])
                eng.wait_ge(tin_evac, 2 * e + 2)
                eng.wait_ge(w_lo[0], e + 2)
                half(range(4))
                eng.wait_ge(w_lo[1], e + 2)
                half(range(4, MH))
                eng.wait_ge(ad_lo, 2 * e + 3)
                half([MH])
                if not first:
                    rows_out(e - 1)
                if first:
                    eng.wait_ge(sh_evac, 3 * TT)
                else:
                    eng.wait_ge(y_evac, 2 * e)
                for m in range(MH):
                    eng.wait_ge(h_split, body * NG + m + 1)
                    if m % 4 == 0:
                        eng.wait_ge(w_lo[2 + m // 4], e + 2)
                    if m == 4 and not last:
                        rows_in(e + 1, 1 - par, seen)
                    for d in range(KD):
                        c = (m % 4) * D + d * P
                        ins = mm(ps[3 + d][:, 0:SLOTS], split3(ew_hi[2 + m // 4][:, c:c + P], ew_lo[2 + m // 4][:, c:c + P],
                                                               h_hi[:, m, :], h_lo[:, m, :]), start=m == 0, stop=False)
                eng.wait_ge(h_split, body * NG + NG)
                eng.wait_ge(ad_lo, 2 * e + 4)
                for d in range(KD):
                    pe.matmul(ps[3 + d][:, 0:SLOTS], up[:, d * P:d * P + P], a_st[:, :],
                              start=False, stop=True).then_inc(y_full, 1)

            expert(0, 0, 16, first=True)
            with eng.Fori(0, 3) as i:
                expert(2 * i + 1, 1, 16 * i + 32)
                expert(2 * i + 2, 0, 16 * i + 32)
            expert(E - 1, 1, None, last=True)
            shared_hidden(LAST, B - 1, range(2))
            rows_out(E - 1)
            shared_hidden(LAST, B - 1, range(2, NG))
            shared_out(LAST, 3, [0, 1])

        @block.vector
        def _(eng):
            v = nc.vector
            steps = [0]

            def own(ins):
                steps[0] += 1
                ins.then_inc(step, 1)
                eng.wait_ge(step, steps[0])

            def full(stage, b, j=0):
                eng.wait_ge(att_full, AT[(stage, b, j)] + 1)
                return ps[BANK[AT[(stage, b, j)]]]

            def evac(ins):
                ins.then_inc(att_evac, 1)

            hi_seen = [0]

            def after_hi(n=1):
                hi_seen[0] += n
                eng.wait_ge(att_hi, hi_seen[0])

            def low(dst, src, hi):
                return v.tensor_tensor(dst, src, hi, ALU.subtract)

            def statistics(b, st, mvt, s_mv):
                for tt in range(TT):
                    ins = v.bn_stats(st[:, tt, :], res[:, TT * b + tt, :])
                own(ins)
                for tt in range(TT):
                    v.bn_aggr(mvt[:, tt, :], st[:, tt, :]).then_inc(s_mv, 1)

            def factors(b, mvt, sdt, rs, nm, s_sd, s_rs):
                eng.wait_ge(s_sd, b + 1)
                v.reciprocal(rs[:, :], sdt[:, :]).then_inc(s_rs, 1)
                eng.wait_ge(s_rs, 2 * b + 1)
                v.scalar_tensor_tensor(nm[:, :], mvt[:, :, 0], -1.0, rs[:, :], ALU.mult, ALU.mult).then_inc(s_rs, 1)

            def turned_low(stage, lo, hi, b):
                bank = full(stage, b)
                after_hi()
                evac(low(lo[:, :, :], bank[:, :], hi[:, :, :]))

            def biased_low(stage, lo, hi, c, b):
                bank = full(stage, b)
                after_hi(KD)
                for m in range(KD):
                    ins = v.scalar_tensor_tensor(lo[:, m, :], bank[:, S * m:S * m + S], bcol[:, c + m:c + m + 1],
                                                 hi[:, m, :], ALU.add, ALU.subtract)
                evac(ins)

            def values(b):
                bank = full("v", b)
                evac(v.tensor_tensor(v32[:, :, :], bank[:, :].rearrange("p (t d) -> p t d", t=TT),
                                     brow[:, 0, :].unsqueeze(1).to_broadcast([P, TT, D]), ALU.add))

            def relu_low(dst, bank, hi):
                return v.scalar_tensor_tensor(dst, bank[:, :], 0.0, hi, ALU.max, ALU.subtract)

            def ln1_factors(b):
                factors(b, mv[b % 2], sd[b % 2], rstd[b % 2], nmr[b % 2], ln1_sd, ln1_rs)

            def chunk_low(i):
                eng.wait_ge(aw_hi_done, i + 1)
                low(aw_lo[i][:, :], raw_aw(i), aw_hi[i][:, :]).then_inc(aw_lo_done, 1)

            eng.wait_ge(x_in[0], 16)
            statistics(0, stats, mv[0], ln1_mv)
            ln1_factors(0)
            chunk_low(0)
            turned_low("tc", ct_lo, ct_hi, 0)
            chunk_low(1)
            turned_low("tx", nt_lo, nt_hi, 0)
            chunk_low(2)
            chunk_low(3)
            eng.wait_ge(mask_hi_done, 1)
            v.tensor_tensor(mask_lo[:, :], bcol[:, MK:MK + NT], mask_hi[:, :], ALU.subtract).then_inc(const_ready, 1)
            biased_low("k", k_lo, k_hi, BK, 0)
            eng.wait_ge(brow_ld, 16)
            values(0)
            biased_low("q", q_lo, q_hi, BQ, 0)
            chunk_low(4)
            eng.wait_ge(x_in[1], 16)
            statistics(1, stats, mv[1], ln1_mv)
            chunk_low(5)
            ln1_factors(1)
            eng.wait_ge(cst_ld, 16)
            v.tensor_copy(tri_ones[:, :], cst[:, C_TRI:C_TRI + 2 * P]).then_inc(const_ready, 1)
            eng.wait_ge(gate_hi_done, 1)
            low(gate_lo[:, :, :], gate_raw[:, :, :], gate_hi[:, :, :]).then_inc(const_ready, 1)

            def attention_sum(b):
                bank = full("wo", b)
                eng.wait_ge(bo_added, b + 1)
                tok = res[:, TT * b:TT * b + TT, :]
                evac(v.tensor_tensor(tok, bank[:, :].rearrange("p (t d) -> p t d", t=TT), tok, ALU.add))
                wait_finished(eng, ("wo", b, 0))
                statistics(b, stats2, mv2, ln2_mv)

            def keys_low(b, j):
                bank = full("kf", b, j)
                after_hi()
                evac(relu_low(kf_lo[:, j // 2, j % 2, :], bank, kf_hi[:, j // 2, j % 2, :]))

            def queries_low(b, j):
                bank = full("qf", b, j)
                after_hi()
                evac(relu_low(qf_lo[:, 2 * j:2 * j + 2, :], bank, qf_hi[:, 2 * j:2 * j + 2, :]))

            def normed_low(b):
                bank = full("t2", b)
                after_hi()
                evac(low(xt_lo[:, :, S * b:S * b + S], bank[:, :].rearrange("p (k n) -> p k n", k=KD),
                         xt_hi[:, :, S * b:S * b + S]))

            def invert(b, j):
                eng.wait_ge(qkv_copied, 4 * (2 * b + j) + 2)
                v.reciprocal(rden[j][:, :], den[j][:, :]).then_inc(inverted, 1)

            for b in range(B):
                if b:
                    invert(b - 1, 0)
                for j in range(4):
                    keys_low(b, j)
                if b:
                    invert(b - 1, 1)
                for j in range(4):
                    queries_low(b, j)
                if b + 2 < B:
                    eng.wait_ge(x_in[b + 2], 16)
                    statistics(b + 2, stats, mv[b % 2], ln1_mv)
                if b + 1 < B:
                    turned_low("tc", ct_lo, ct_hi, b + 1)
                if b:
                    attention_sum(b - 1)
                for j in range(2):
                    full("tkv", b, j)
                    after_hi(2)
                    for i in range(2):
                        dst, src = kv_blocks(kvt_lo, b, j, i)
                        ins = low(dst, src, kv_blocks(kvt_hi, b, j, i)[0])
                    evac(ins)
                if b + 2 < B:
                    ln1_factors(b + 2)
                if b:
                    factors(b - 1, mv2, sd2, rstd2, nmr2, ln2_sd, ln2_rs)
                if b + 1 < B:
                    turned_low("tx", nt_lo, nt_hi, b + 1)
                    biased_low("k", k_lo, k_hi, BK, b + 1)
                    values(b + 1)
                if b:
                    normed_low(b - 1)
                if b + 1 < B:
                    biased_low("q", q_lo, q_hi, BQ, b + 1)
                if b == 1:
                    eng.wait_ge(ad_hi, 2)
                    v.tensor_tensor(sdn_lo[:, :, :, :], raw_ad[:, 0:KD * RANK].rearrange("p (k r) -> p k r", k=KD).unsqueeze(2).to_broadcast([P, KD, 3, RANK]),
                                    sdn_hi[:, :, :, :], ALU.subtract).then_inc(ad_lo, 1)
                    v.tensor_tensor(sup[2 * RANK:AP3, :], raw_ad[2 * RANK:AP3, KD * RANK:AD], sup[2 * RANK:AP3, :],
                                    ALU.subtract).then_inc(ad_lo, 1)
            for j in range(2):
                invert(B - 1, j)

            attention_sum(B - 1)
            factors(B - 1, mv2, sd2, rstd2, nmr2, ln2_sd, ln2_rs)

            def split_groups(body, ms, n):
                for m in ms:
                    g0 = body * NG + m
                    eng.wait_ge(gelu_done, g0 + 1)
                    src = h32[m % 3]
                    if m < MH:
                        v.tensor_copy(h_hi[:, m, 0:n], src[:, 0:n]).then_inc(h_hi_done, 1)
                        eng.wait_ge(h_hi_done, g0 + 1)
                        low(h_lo[:, m, 0:n], src[:, 0:n], h_hi[:, m, 0:n]).then_inc(h_split, 1)
                    else:
                        v.tensor_copy(a_st[:, 0:n], src[0:AP3, 0:n]).then_inc(h_hi_done, 1)
                        eng.wait_ge(h_hi_done, g0 + 1)
                        mid = slice(RANK, 2 * RANK)
                        low(a_st[mid, 0:n], src[mid, 0:n], a_st[mid, 0:n]).then_inc(h_split, 1)

            def add_shared(c, n):
                for tt in range(TT):
                    eng.wait_ge(sh_full, TT * n + tt + 1)
                    if tt == 0:
                        eng.wait_ge(sb2_added, c + 1)
                    tok = res[:, TT * c + tt, :]
                    v.scalar_tensor_tensor(tok, ps[3 + tt][:, 0:D], 0.2, tok, ALU.mult, ALU.add).then_inc(sh_evac, 1)

            split_groups(0, range(NG), S)
            normed_low(B - 1)
            for half in range(2):
                bank = full("lg", half)
                evac(v.tensor_copy(lgt[:, 512 * half:512 * half + 512], bank[0:E, :]))

            bank = full("tlg", 0)
            evac(v.tensor_copy(lg[:, :, :], bank[:, 0:NT * E].rearrange("p (t e) -> p t e", e=E)))
            wait_finished(eng, ("tlg", 0, 0))

            def over_experts(col):
                return col.unsqueeze(2).to_broadcast([P, NT, E])

            ranks = cst[:, C_RANK:C_RANK + NT * E].rearrange("p (t e) -> p t e", e=E)
            own(v.tensor_reduce(top[:, 0, :], lg[:, :, :], AX_X, ALU.max))
            v.tensor_tensor(z[:, :, :], lg[:, :, :], over_experts(top[:, 0, :]), ALU.subtract).then_inc(z_ready, 1)
            eng.wait_ge(z_ready, 1)
            tmp = tmp16[:, :, 0, :]
            own(v.scalar_tensor_tensor(tmp, z[:, :, :], 0.0, ranks, ALU.is_equal, ALU.mult))
            own(v.tensor_reduce(rank[:, :, 0], tmp, AX_X, ALU.max))
            own(v.tensor_tensor(hot[:, :, 0, :], ranks, over_experts(rank[:, :, 0]), ALU.is_equal))
            own(v.scalar_tensor_tensor(lg[:, :, :], hot[:, :, 0, :], -1e30, z[:, :, :], ALU.mult, ALU.add))
            v.tensor_reduce(top[:, 1, :], lg[:, :, :], AX_X, ALU.max).then_inc(z_ready, 1)
            eng.wait_ge(z_ready, 2)
            own(v.tensor_tensor(tmp, lg[:, :, :], over_experts(top[:, 1, :]), ALU.is_equal))
            own(v.tensor_tensor(tmp, tmp, ranks, ALU.mult))
            own(v.tensor_reduce(rank[:, :, 1], tmp, AX_X, ALU.max))
            own(v.tensor_tensor(hot[:, :, 1, :], ranks, over_experts(rank[:, :, 1]), ALU.is_equal))
            v.tensor_copy(hot_bf[:, :, :, :], hot[:, :, :, :]).then_inc(hot_ready, 1)
            eng.wait_ge(exp_done, 2)
            own(v.tensor_reduce(esum[:, 0, :], tmp_exp[:, :, :], AX_X, ALU.add))
            own(v.reciprocal(esum[:, 2, :], esum[:, 0, :]))
            v.tensor_copy(rows[:, :, D], esum[:, 2, :])
            v.tensor_tensor(rows[:, :, D + 2], esum[:, 1, :], esum[:, 2, :], ALU.mult)
            own(v.scalar_tensor_tensor(slot[:, :, :], rank[:, :, :], -float(SLOTS),
                                       cst[:, C_BASE:C_BASE + 2 * NT].rearrange("p (t k) -> p t k", k=2), ALU.mult, ALU.add))
            add_shared(0, 0)
            split_groups(1, range(0, 4), S)
            bank = full("pos", 0)
            evac(v.tensor_tensor(tmp16[:, :, :, :], hot[:, :, :, :],
                                 bank[:, 0:NT * 2 * E].rearrange("p (t k e) -> p t k e", t=NT, k=2), ALU.mult))
            wait_finished(eng, ("pos", 0, 0))
            own(v.tensor_reduce(place[:, :, :], tmp16[:, :, :, :], AX_X, ALU.add))
            own(v.tensor_tensor(slot[:, :, :], slot[:, :, :], place[:, :, :], ALU.add))
            own(v.tensor_scalar(place[:, :, :], place[:, :, :], float(CAP), float(NOWHERE), ALU.is_ge, ALU.mult))
            own(v.tensor_tensor(slot[:, :, :], slot[:, :, :], place[:, :, :], ALU.add))
            v.tensor_copy(slot_i[:, :, :], slot[:, :, :]).then_inc(slots_ready, 1)
            split_groups(1, range(4, NG), S)
            add_shared(1, 1)
            split_groups(2, range(NG), S)

            def rows_low(e):
                for k in range(KD):
                    eng.wait_ge(tin_hi, 2 * e + 1 + k)
                    low(xe_lo[:, k, :], ps[5 + k][:, 0:SLOTS], xe_hi[:, k, :]).then_inc(tin_evac, 1)

            def weighted(e, par, seen, sent):
                eng.wait_ge(meta_ld[par], seen)
                if sent is not None:
                    eng.wait_ge(y_sent[par], sent)
                for j in range(ST):
                    if j % 2 == 0:
                        eng.wait_ge(tout_full, 2 * e + 1 + j // 2)
                    bank = ps[7] if j < 2 else ps[5]
                    ins = v.tensor_scalar(yw[par][:, j, :], bank[0:SP, (j % 2) * D:(j % 2) * D + D],
                                          meta[par][:, j, 2 * (j // 2):2 * (j // 2) + 1], None, ALU.mult)
                    if j % 2:
                        ins.then_inc(tout_evac, 1)

            def first_low(e):
                eng.wait_ge(w_hi[0], e + 2)
                low(ew_lo[0][:, :], raw[0][:, :], ew_hi[0][:, :]).then_inc(w_lo[0], 1)

            def down_low(e):
                eng.wait_ge(ad_hi, 2 * e + 3)
                v.tensor_tensor(dn_lo[:, :, :, :], raw_ad[:, 0:KD * RANK].rearrange("p (k r) -> p k r", k=KD).unsqueeze(2).to_broadcast([P, KD, 3, RANK]),
                                dn_hi[:, :, :, :], ALU.subtract).then_inc(ad_lo, 1)

            def up_low(e):
                eng.wait_ge(ad_hi, 2 * e + 4)
                v.tensor_tensor(up[2 * RANK:AP3, :], raw_ad[2 * RANK:AP3, KD * RANK:AD], up[2 * RANK:AP3, :],
                                ALU.subtract).then_inc(ad_lo, 1)

            down_low(0)
            rows_low(0)
            add_shared(2, 2)

            def expert(e, par, seen=None, sent=None, first=False, last=False):
                body = e + FIRST
                split_groups(body, range(6), SLOTS)
                up_low(e)
                split_groups(body, range(6, NG), SLOTS)
                if not last:
                    first_low(e + 1)
                    down_low(e + 1)
                if not first:
                    weighted(e - 1, 1 - par, seen, sent)
                if not last:
                    rows_low(e + 1)

            expert(0, 0, first=True)
            expert(1, 1, seen=16)
            expert(2, 0, seen=16)
            with eng.Fori(1, 3) as i:
                expert(2 * i + 1, 1, seen=16 * i + 16, sent=64 * i)
                expert(2 * i + 2, 0, seen=16 * i + 16, sent=64 * i)
            expert(E - 1, 1, seen=64, sent=64 * 3, last=True)
            split_groups(LAST, range(2), S)
            weighted(E - 1, 1, 64, 64 * 3)
            split_groups(LAST, range(2, NG), S)

            add_shared(B - 1, 3)
            early, late = slice(0, NT - TT), slice(NT - TT, NT)
            eng.wait_ge(yk_ld[0], 32)
            own(v.tensor_tensor(res[:, early, :], res[:, early, :], yk[:, 0, early, :], ALU.add))
            v.tensor_tensor(res[:, early, :], res[:, early, :], yk[:, 1, early, :], ALU.add).then_inc(early_out, 1)
            eng.wait_ge(yk_ld[1], 32)
            eng.wait_ge(sh_evac, 4 * TT)
            own(v.tensor_tensor(res[:, late, :], res[:, late, :], yk[:, 0, late, :], ALU.add))
            v.tensor_tensor(res[:, late, :], res[:, late, :], yk[:, 1, late, :], ALU.add).then_inc(early_out, 1)


def kernel(x, ctx_2048, mask_BxS2_ff1, **w):
    import concourse.bacc as bacc
    from concourse.bass_utils import run_bass_kernel_spmd

    def f(name):
        return np.asarray(w[name])

    def tiles(m):
        return np.asarray(m).reshape(-1, P, m.shape[-1]).transpose(1, 0, 2)

    def cols(m):
        return tiles(m).reshape(P, -1)

    feat = np.zeros((P, 2, 8 * FD), np.float32)
    for h in range(8):
        for i, name in enumerate(("L0_xattn_Wkf", "L0_xattn_Wqf")):
            feat[HD * h:HD * h + HD, i, FD * h:FD * h + FD] = f(name).T
    attw = np.stack([cols(f("L0_xattn_Wk").T), cols(f("L0_xattn_Wv").T), cols(f("L0_xattn_Wq").T),
                     feat[:, 0], feat[:, 1], cols(f("L0_xattn_Wo").T)])

    def chunks(w1, w2):
        one, two = tiles(w1), tiles(w2)
        return np.stack([one[:, :, 0:512].reshape(P, CH), one[:, :, 512:1024].reshape(P, CH),
                         two[:, 0:4].reshape(P, CH), two[:, 4:8].reshape(P, CH)])

    def adapter(wd, wu):
        side = np.zeros((P, D), np.float32)
        side[0:AP3] = np.concatenate([wu, wu, wu], 0)
        return np.concatenate([cols(wd), side], 1)

    w1, w2, wd, wu = (f("L0_ffn_" + n) for n in ("w1", "w2", "wd", "wu"))
    wch = np.stack([chunks(f("L0_ffn_sw1"), f("L0_ffn_sw2"))] + [chunks(w1[e], w2[e]) for e in range(E)])
    adw = np.stack([adapter(f("L0_ffn_swd"), f("L0_ffn_swu"))] + [adapter(wd[e], wu[e]) for e in range(E)])
    gate = np.zeros((D, P), np.float32)
    gate[:, 0:E] = f("L0_ffn_gate_w")
    vec = lambda m: np.asarray(m).reshape(-1, P).T
    bexp = np.stack([np.concatenate([vec(f("L0_ffn_b1")[e]), vec(f("L0_ffn_b2")[e])], 1) for e in range(E)])
    bias = [vec(f("L0_ffn_sb1")), np.zeros((P, 2), np.float32), vec(f("L0_xattn_bq")), vec(f("L0_xattn_bk")), vec(mask_BxS2_ff1)]
    bcol = np.concatenate(bias, 1)
    brow = np.stack([f("L0_xattn_bv"), f("L0_xattn_bo"), f("L0_ffn_sb2")])

    r = np.arange(P)
    cst = np.zeros((P, CCOLS), np.float32)
    cst[:, C_ID:C_ID + P] = np.eye(P)
    cst[:, C_TRI:C_TRI + P] = r[:, None] < r[None, :]
    cst[:, C_ONE:C_ONE + P] = 1.0
    cst[:, C_RANK:C_RANK + NT * E] = np.tile(E - np.arange(E), NT)
    cst[:, C_BASE:C_BASE + 2 * NT] = np.tile([E * SLOTS, E * SLOTS + CAP], NT)
    dest = (np.arange(NT)[None, :, None] * P + r[:, None, None] + T * np.arange(2)[None, None, :]).astype(np.int32)
    pre = np.zeros((P, ROW), np.int32)
    pre[:, D + 1::2] = NOWHERE + r[:, None]

    nc = bacc.Bacc("TRN2", target_bir_lowering=False, num_devices=1)
    arrays, args = {}, []
    for name, arr in (("x", x), ("ctx", ctx_2048), ("attw", attw), ("wch", wch), ("adw", adw), ("gate", tiles(gate)),
                      ("bcol", bcol), ("bexp", bexp), ("brow", brow), ("cst", cst), ("dest", dest), ("pre", pre.view(np.float32))):
        arrays["in_" + name] = np.ascontiguousarray(arr)
        args.append(nc.dram_tensor("in_" + name, arr.shape, mybir.dt.from_np(arrays["in_" + name].dtype),
                                   kind="ExternalInput").ap())
    args.append(nc.dram_tensor("xbuf", (E * SLOTS, ROW), F32, kind="Internal").ap())
    args.append(nc.dram_tensor("ybuf", (2 * T, D), F32, kind="Internal").ap())
    args.append(nc.dram_tensor("out", (B, S, D), F32, kind="ExternalOutput").ap())
    build_program(nc, *args)
    r = run_bass_kernel_spmd(nc, [arrays], core_ids=[0])
    return r.results[0]["out"]
```

```python
from contextlib import ExitStack

import numpy as np

import concourse.bass as bass
from concourse import mybir

ACT = mybir.ActivationFunctionType
ALU = mybir.AluOpType
AX_X = mybir.AxisListType.X
F32 = mybir.dt.float32
F32R = mybir.dt.float32r
BF16 = mybir.dt.bfloat16
I32 = mybir.dt.int32

P = 128
B, S, D = 4, 256, 256
T = B * S
TT = S // P
NT = T // P
KD = D // P
NH, HD, FD = 16, 16, 64
E = 8
CAP = int(T * 1.25 / E)
SLOTS = 2 * CAP
ST = 4
SP = SLOTS // ST
FH = 1024
MH = FH // P
RANK = 32
LN_EPS = 1e-5
DEN_EPS = 1e-8
GP = 32
META = 2
ROW = D + META
NOWHERE = 1 << 20
CH = 1024
AD = KD * RANK + D
AP3 = 3 * RANK
NB = 10
BQ, BK, MK = NB, NB + 2, NB + 4
BCOLS = MK + NT
C_ID, C_TRI, C_ONE, C_EXP, C_BASE = 0, P, 2 * P, 3 * P, 3 * P + E
CCOLS = C_BASE + 2 * NT
NG = MH + 1
FIRST = 2
TAIL = FIRST + E
ROUNDS = ((0, 4), (4, 6), (6, 8))


def attention_groups():
    order = [("tc", 0, 0), ("tx", 0, 0), ("k", 0, 0), ("v", 0, 0), ("q", 0, 0)]
    for b in range(B - 1):
        order += [("kf", b, j) for j in range(4)]
        order += [("qf", b, j) for j in range(4)]
        order += [("tc", b + 1, 0)]
        order += [("kv", b, j) for j in range(2)]
        if b:
            order += [("wo", b - 1, 0)]
        order += [("tkv", b, j) for j in range(2)]
        order += [("tx", b + 1, 0), ("k", b + 1, 0), ("v", b + 1, 0)]
        order += [("q", b + 1, 0)]
        if b:
            order += [("t2", b - 1, 0)]
        order += [("qkv", b, j) for j in range(2)]
    b = B - 1
    order += [("kf", b, j) for j in range(4)] + [("lg", 0, 0)]
    order += [("qf", b, j) for j in range(4)] + [("tlg", 0, 0)]
    order += [("kv", b, j) for j in range(2)] + [("tkv", b, j) for j in range(2)]
    order += [("wo", b - 1, 0), ("pos", 0, 0)]
    order += [("qkv", b, j) for j in range(2)]
    bank = [n % 8 for n in range(len(order))]
    order += [("t2", B - 2, 0), ("wo", B - 1, 0), ("lg", 1, 0), ("tlg", 1, 0), ("t2", B - 1, 0),
              ("pos", 1, 0), ("lg", 2, 0), ("tlg", 2, 0), ("pos", 2, 0)]
    bank += [5, 6, 7, 5, 6, 7, 5, 6, 7]
    return order, bank


def build_program(nc, x, ctx, attw, wch, adw, gw, bcol_d, bexp_d, brow_d, cst_d, dest_d, pre_d, xbuf, ybuf, out):
    ORDER, BANK = attention_groups()
    AT = {g: n for n, g in enumerate(ORDER)}

    with ExitStack() as stack:
        def sb(name, shape, dt, on=stack):
            return on.enter_context(nc.sbuf_tensor(name, shape, dt))

        def sem(name):
            return stack.enter_context(nc.semaphore(name))

        ps = [stack.enter_context(nc.psum_tensor(f"bank{i}", [P, 512], F32)) for i in range(8)]

        cst = sb("cst", [P, CCOLS], F32)
        ident = cst[:, C_ID:C_ID + P]
        tri_ones = sb("tri_ones", [P, 2 * P], BF16)
        ones = sb("ones", [P, FD], F32)
        bcol = sb("bcol", [P, BCOLS], F32)
        brow = sb("brow", [P, 3, D], F32)
        dest = sb("dest", [P, NT, 2], I32)
        gate_raw = sb("gate_raw", [P, KD, GP], F32)
        gate_hi = sb("gate_hi", [P, KD, GP], F32R)
        gate_lo = sb("gate_lo", [P, KD, GP], F32R)
        res = sb("res", [P, NT, D], F32)
        rows = sb("rows", [P, NT, ROW], F32)
        xt_hi = sb("xt_hi", [P, KD, T], F32R)
        xt_lo = sb("xt_lo", [P, KD, T], F32R)
        raw = [sb(f"raw{q}", [P, CH], F32) for q in range(4)]
        raw_ad = sb("raw_ad", [P, AD], F32)
        sw_hi = [sb(f"sw_hi{q}", [P, CH], F32R) for q in range(4)]
        sw_lo = [sb(f"sw_lo{q}", [P, CH], F32R) for q in range(4)]
        sdn_hi = sb("sdn_hi", [P, KD, 3, RANK], F32R)
        sdn_lo = sb("sdn_lo", [P, KD, 3, RANK], F32R)
        sup = sb("sup", [AP3, D], F32R)
        lgt = sb("lgt", [E, 2 * S], F32)
        lg = sb("lg", [P, NT, E], F32)
        z = sb("z", [P, NT, E], F32)
        hot = sb("hot", [P, NT, 2, E], BF16)
        queue_place = sb("queue_place", [P, NT, 2, E], F32)
        top = sb("top", [P, NT, E], F32)
        top_i = sb("top_i", [P, NT, E], mybir.dt.uint32)
        expert_no = sb("expert_no", [P, NT, 2], F32)
        place = sb("place", [P, NT, 2], F32)
        slot = sb("slot", [P, NT, 2], F32)
        slot_i = sb("slot_i", [P, NT, 2], I32)
        pre = sb("pre", [P, ROW], F32)
        tmp_exp = sb("tmp_exp", [P, NT, E], F32)
        esum = sb("esum", [P, NT], F32)
        prob = sb("prob", [P, 2, NT], F32)
        stats2 = sb("stats2", [P, TT, 6], F32)
        mv2 = sb("mv2", [P, TT, 2], F32)
        warm = sb("warm", [P, 1], F32)
        minus_half = sb("minus_half", [P, TT], F32)
        sd2 = sb("sd2", [P, TT], F32)
        rstd2 = sb("rstd2", [P, TT], F32)
        nmr2 = sb("nmr2", [P, TT], F32)

        att = ExitStack()
        num = [sb(f"num{j}", [P, S], F32, att) for j in range(2)]
        den = [sb(f"den{j}", [P, S], F32, att) for j in range(2)]
        rden = [sb(f"rden{j}", [P, S], F32, att) for j in range(2)]
        o32 = sb("o32", [P, KD, S], F32, att)
        o_hi, o_lo = sb("o_hi", [P, KD, S], F32R, att), sb("o_lo", [P, KD, S], F32R, att)
        wo_hi, wo_lo = sb("wo_hi", [P, CH // 2], F32R, att), sb("wo_lo", [P, CH // 2], F32R, att)
        aw_hi = [sb(f"aw_hi{i}", [P, CH // 2], F32R, att) for i in range(5)] + [wo_hi]
        aw_lo = [sb(f"aw_lo{i}", [P, CH // 2], F32R, att) for i in range(5)] + [wo_lo]
        ctx_sb = sb("ctx_sb", [P, TT, D], F32, att)
        xn = sb("xn", [P, TT, D], F32, att)
        stats = sb("stats", [P, TT, 6], F32, att)
        mv = [sb(f"mv{i}", [P, TT, 2], F32, att) for i in range(2)]
        sd = [sb(f"sd{i}", [P, TT], F32, att) for i in range(2)]
        rstd = [sb(f"rstd{i}", [P, TT], F32, att) for i in range(2)]
        nmr = [sb(f"nmr{i}", [P, TT], F32, att) for i in range(2)]
        mask_hi = sb("mask_hi", [P, NT], F32R, att)
        mask_lo = sb("mask_lo", [P, NT], F32, att)
        ct_hi, ct_lo = sb("ct_hi", [P, KD, S], F32R, att), sb("ct_lo", [P, KD, S], F32R, att)
        nt_hi, nt_lo = sb("nt_hi", [P, KD, S], F32R, att), sb("nt_lo", [P, KD, S], F32R, att)
        k_hi, k_lo = sb("k_hi", [P, KD, S], F32R, att), sb("k_lo", [P, KD, S], F32R, att)
        q_hi, q_lo = sb("q_hi", [P, KD, S], F32R, att), sb("q_lo", [P, KD, S], F32R, att)
        v32 = sb("v32", [P, TT, D], F32, att)
        v_hi = sb("v_hi", [P, TT, 4, P], F32R, att)
        v_lo = sb("v_lo", [P, TT, 4, P], F32R, att)
        kf_hi, kf_lo = sb("kf_hi", [P, TT, 2, 512], F32R, att), sb("kf_lo", [P, TT, 2, 512], F32R, att)
        qf_hi, qf_lo = sb("qf_hi", [P, 8, S], F32R, att), sb("qf_lo", [P, 8, S], F32R, att)
        kvm = sb("kvm", [P, 4, S], F32, att)
        kvt_hi, kvt_lo = sb("kvt_hi", [P, 8, P], F32R, att), sb("kvt_lo", [P, 8, P], F32R, att)
        att.close()

        ffn = ExitStack()
        yk = sb("yk", [P, 2, NT, D], F32, ffn)
        yw = [sb(f"yw{i}", [SP, ST, D], F32, ffn) for i in range(2)]
        h_hi, h_lo = sb("h_hi", [P, MH, SLOTS], F32R, ffn), sb("h_lo", [P, MH, SLOTS], F32R, ffn)
        h32 = [sb(f"h32_{i}", [P, SLOTS], F32, ffn) for i in range(3)]
        a_st = sb("a_st", [AP3, SLOTS], F32R, ffn)
        ew_hi = [sb(f"ew_hi{q}", [P, CH], F32R, ffn) for q in range(4)]
        ew_lo = [sb(f"ew_lo{q}", [P, CH], F32R, ffn) for q in range(4)]
        dn_hi = sb("dn_hi", [P, KD, 3, RANK], F32R, ffn)
        dn_lo = sb("dn_lo", [P, KD, 3, RANK], F32R, ffn)
        up = sb("up", [AP3, D], F32R, ffn)
        bexp = [sb(f"bexp{i}", [P, NB], F32, ffn) for i in range(2)]
        xg = [sb(f"xg{i}", [SP, ST, D], F32, ffn) for i in range(2)]
        meta = [sb(f"meta{i}", [SP, ST, META], F32, ffn) for i in range(2)]
        xe_hi, xe_lo = sb("xe_hi", [P, KD, SLOTS], F32R, ffn), sb("xe_lo", [P, KD, SLOTS], F32R, ffn)
        ye = sb("ye", [P, KD, SLOTS], F32, ffn)
        ffn.close()

        ident_ld, cst_ld, bcol_ld, brow_ld = sem("ident_ld"), sem("cst_ld"), sem("bcol_ld"), sem("brow_ld")
        misc_ld = sem("misc_ld")
        pre_ld = sem("pre_ld")
        x_in = [sem(f"x_in{b}") for b in range(B)]
        ctx_in = [sem(f"ctx_in{b}") for b in range(B)]
        aw_ld = [sem(f"aw_ld{i}") for i in range(6)]
        aw_hi_done, aw_lo_done = sem("aw_hi_done"), sem("aw_lo_done")
        prefilled = sem("prefilled")
        const_ready = sem("const_ready")
        gate_hi_done = sem("gate_hi_done")
        mask_hi_done = sem("mask_hi_done")
        pool_const, kvt_zeroed = sem("pool_const"), sem("kvt_zeroed")
        sb2_scaled = sem("sb2_scaled")
        att_full, att_evac, att_hi = sem("att_full"), sem("att_evac"), sem("att_hi")
        ln1_mv, ln1_sd, ln1_rs, ln1_out = sem("ln1_mv"), sem("ln1_sd"), sem("ln1_rs"), sem("ln1_out")
        ln2_mv, ln2_sd, ln2_rs, ln2_out = sem("ln2_mv"), sem("ln2_sd"), sem("ln2_rs"), sem("ln2_out")
        vmask = sem("vmask")
        bo_added, sb2_added = sem("bo_added"), sem("sb2_added")
        qkv_copied = sem("qkv_copied")
        inverted, divided, o_high, o_split = sem("inverted"), sem("divided"), sem("o_high"), sem("o_split")
        v_high, v_masked, v_split = sem("v_high"), sem("v_masked"), sem("v_split")
        kv_copied, lg_copied = sem("kv_copied"), sem("lg_copied")
        step = sem("step")
        z_ready, exp_done = sem("z_ready"), sem("exp_done")
        meta_ids = sem("meta_ids")
        hot_ready = sem("hot_ready")
        slots_ready = sem("slots_ready")
        dispatched = sem("dispatched")
        w_ld = [sem(f"w_ld{q}") for q in range(4)]
        w_hi = [sem(f"w_hi{q}") for q in range(4)]
        w_lo = [sem(f"w_lo{q}") for q in range(4)]
        ad_ld, ad_hi, ad_lo = sem("ad_ld"), sem("ad_hi"), sem("ad_lo")
        bias_ld = [sem(f"bias_ld{i}") for i in range(2)]
        g1_full, gelu_done, h_hi_done, h_split = sem("g1_full"), sem("gelu_done"), sem("h_hi_done"), sem("h_split")
        sh_full, sh_evac = sem("sh_full"), sem("sh_evac")
        y_full, y_evac = sem("y_full"), sem("y_evac")
        xg_ld = [sem(f"xg_ld{i}") for i in range(2)]
        meta_ld = [sem(f"meta_ld{i}") for i in range(2)]
        tin_full, tin_hi, tin_evac = sem("tin_full"), sem("tin_hi"), sem("tin_evac")
        tout_full, tout_evac = sem("tout_full"), sem("tout_evac")
        y_sent = [sem(f"y_sent{i}") for i in range(2)]
        yk_ld = [sem(f"yk_ld{i}") for i in range(2)]
        prob_ready = sem("prob_ready")
        rows_weighted = sem("rows_weighted")
        rows_summed = sem("rows_summed")
        combined = sem("combined")
        stored = sem("stored")

        LAST_ATT = AT[("qkv", B - 1, 1)] + 1

        def split3(w_h, w_l, m_h, m_l):
            return ((w_h, m_h), (w_h, m_l), (w_l, m_h))

        def lgt_column(n):
            return S if n == 2 else 0

        def kv_blocks(dst, b, j, i):
            c = HD * (2 * j + i)
            half = slice(FD * i, FD * i + FD)
            kept = lambda ap: ap.rearrange("p g (s x) -> p g s x", s=2)[:, :, :, c:c + HD]
            return (kept(dst[half, j::2, :]),
                    kept(ps[BANK[AT[("tkv", b, j)]]][half, :].rearrange("p (g x) -> p g x", g=4)))

        def down_copies():
            return (raw_ad[:, 0:KD * RANK].rearrange("p (k r) -> p k r", k=KD).unsqueeze(2)
                    .to_broadcast([P, KD, 3, RANK]))

        def raw_aw(i):
            return raw[1 + i // 2][:, (i % 2) * (CH // 2):(i % 2 + 1) * (CH // 2)]

        def xtok(b):
            return x[b].rearrange("(t p) d -> p t d", p=P)

        EVAC = {g: sum(other[0] not in ("kv", "qkv", "lg") for other in ORDER[:n + 1]) for g, n in AT.items()}

        def wait_finished(eng, group):
            if group[0] == "kv":
                eng.wait_ge(kv_copied, 2 * group[1] + group[2] + 1)
            elif group[0] == "lg":
                eng.wait_ge(lg_copied, group[1] + 1)
            elif group[0] == "qkv":
                eng.wait_ge(qkv_copied, 4 * (2 * group[1] + group[2] + 1))
            else:
                eng.wait_ge(att_evac, EVAC[group])

        def wait_bank(eng, bank):
            wait_finished(eng, [ORDER[n] for n in range(LAST_ATT) if BANK[n] == bank][-1])

        block = stack.enter_context(nc.Block())

        @block.sync
        def _(eng):
            def load_raw(u, q):
                eng.dma_start(raw[q][:, :], wch[u, q]).then_inc(w_ld[q], 16)

            def load_adapter(u):
                eng.dma_start(raw_ad[:, :], adw[u]).then_inc(ad_ld, 16)

            def load_rows(e, par):
                eng.dma_start(xg[par][:, :, :],
                              xbuf[bass.ds(e * SLOTS, SLOTS), 0:D].rearrange("(j p) c -> p j c", p=SP)
                              ).then_inc(xg_ld[par], 16)

            def load_meta(e, par):
                eng.dma_start(meta[par][:, :, :],
                              xbuf[bass.ds(e * SLOTS, SLOTS), D:ROW].rearrange("(j p) c -> p j c", p=SP)
                              ).then_inc(meta_ld[par], 16)

            def load_context(b):
                eng.wait_ge(att_full, AT[("tc", b - 1, 0)] + 1)
                eng.dma_start(ctx_sb[:, :, :],
                              ctx[b].rearrange("(t p) d -> p t d", p=P)).then_inc(ctx_in[b], 16)

            eng.dma_start(res[:, 0:TT, :], xtok(0)).then_inc(x_in[0], 16)
            eng.dma_start(cst[:, 0:P], cst_d[:, 0:P]).then_inc(ident_ld, 16)
            for i in range(3):
                eng.dma_start(raw_aw(i), attw[i]).then_inc(aw_ld[i], 16)
            eng.dma_start(brow[:, :, :], brow_d.partition_broadcast(P)).then_inc(brow_ld, 16)
            for i in range(3, 6):
                eng.dma_start(raw_aw(i), attw[i]).then_inc(aw_ld[i], 16)
            eng.dma_start(res[:, TT:2 * TT, :], xtok(1)).then_inc(x_in[1], 16)
            eng.dma_start(cst[:, P:CCOLS], cst_d[:, P:CCOLS]).then_inc(cst_ld, 16)
            for b in range(2, B):
                eng.dma_start(res[:, TT * b:TT * b + TT, :], xtok(b)).then_inc(x_in[b], 16)
            eng.dma_start(dest[:, :, :], dest_d).then_inc(misc_ld, 16)
            eng.dma_start(gate_raw[:, :, :], gw).then_inc(misc_ld, 16)
            eng.dma_start(pre[:, :], pre_d).then_inc(pre_ld, 16)
            load_raw(0, 0)
            load_adapter(0)
            load_context(1)
            for q in range(1, 4):
                eng.wait_ge(aw_lo_done, 2 * q)
                load_raw(0, q)
            for b in range(2, B):
                load_context(b)
            eng.wait_ge(pre_ld, 16)
            eng.dma_start(xbuf.rearrange("(a p) c -> p a c", p=P),
                          pre[:, :].unsqueeze(1).to_broadcast([P, E * SLOTS // P, ROW])).then_inc(prefilled, 16)
            eng.dma_start(ybuf.rearrange("(a p) c -> p a c", p=P),
                          pre[:, 0:D].unsqueeze(1).to_broadcast([P, 2 * NT, D])).then_inc(prefilled, 16)

            def load_expert_weights(e):
                for q in range(4):
                    eng.wait_ge(w_lo[q], e + 1)
                    load_raw(e + 1, q)
                    if q == 1:
                        eng.wait_ge(ad_lo, 2 * e + 2)
                        load_adapter(e + 1)

            load_expert_weights(0)
            eng.wait_ge(dispatched, 16 * 2 * NT)
            load_rows(0, 0)

            def load_bias(e, par):
                eng.dma_start(bexp[par][:, :], bexp_d[e]).then_inc(bias_ld[par], 16)

            def step_loads(e, par, sent=None):
                if sent is not None:
                    eng.wait_ge(tin_full, 2 * e)
                load_rows(e + 1, 1 - par)
                load_expert_weights(e + 1)
                if sent is not None:
                    eng.wait_ge(y_evac, 2 * e)
                load_bias(e + 1, 1 - par)
                if sent is not None and not (isinstance(e, int) and e == 1):
                    eng.wait_ge(y_sent[par], sent)
                load_meta(e, par)

            load_bias(0, 0)
            step_loads(0, 0)
            step_loads(1, 1, 0)
            step_loads(2, 0, 64)
            with eng.Fori(1, 3) as i:
                step_loads(2 * i + 1, 1, 64 * i)
                step_loads(2 * i + 2, 0, 64 * i + 64)
            eng.wait_ge(y_sent[1], 64 * (E // 2 - 1))
            load_meta(E - 1, 1)

            for i in range(2):
                eng.wait_ge(y_sent[i], 64 * (E // 2))
            yview = ybuf.rearrange("(k t p) d -> p k t d", k=2, p=P)
            for part in range(2):
                for k in range(2):
                    tiles = slice(part * NT // 2, (part + 1) * NT // 2)
                    eng.dma_start(yk[:, k, tiles, :], yview[:, k, tiles]).then_inc(yk_ld[part], 16)
            oview = out.rearrange("b (t p) d -> p (b t) d", p=P)
            for tiles, added, shared in ((slice(0, 4), 2, 4), (slice(4, 6), 4, 6), (slice(6, 7), 5, 7), (slice(7, 8), 6, 8)):
                eng.wait_ge(combined, added)
                eng.wait_ge(sh_evac, shared)
                eng.dma_start(oview[:, tiles], res[:, tiles, :]).then_inc(stored, 16)
            eng.wait_ge(stored, 4 * 16)

        @block.gpsimd
        def _(eng):
            g = nc.gpsimd
            last_slot, last_row = eng.to_reg(E * SLOTS - 1), eng.to_reg(2 * T - 1)
            g.memset(ones[:, :], 1.0).then_inc(pool_const, 1)
            g.memset(minus_half[:, :], -0.5).then_inc(pool_const, 1)

            def mask_columns(b):
                if b:
                    eng.wait_ge(att_full, AT[("kv", b - 1, 1)] + 1)
                for tt in range(TT):
                    for dst, m in ((v_hi, bcol[:, MK + TT * b + tt:MK + TT * b + tt + 1]),
                                   (v_lo, mask_lo[:, TT * b + tt:TT * b + tt + 1])):
                        g.tensor_scalar(dst[:, tt, :, FD:P], ones[:, :].unsqueeze(1).to_broadcast([P, 4, FD]),
                                        m, None, ALU.mult).then_inc(vmask, 1)

            def add_row(b, i, done):
                tok = res[:, TT * b:TT * b + TT, :]
                g.tensor_tensor(tok, tok, brow[:, i, :].unsqueeze(1).to_broadcast([P, TT, D]),
                                ALU.add).then_inc(done, 1)

            def values_low(b):
                eng.wait_ge(v_high, TT * b + TT)
                for tt in range(TT):
                    m = bcol[:, MK + TT * b + tt:MK + TT * b + tt + 1]
                    g.tensor_scalar(v32[:, tt, :], v32[:, tt, :], m, None, ALU.mult).then_inc(v_masked, 1)
                eng.wait_ge(v_masked, TT * b + TT)
                for tt in range(TT):
                    g.tensor_tensor(v_lo[:, tt, :, 0:FD], v32[:, tt, :].rearrange("p (g c) -> p g c", g=4),
                                    v_hi[:, tt, :, 0:FD], ALU.subtract).then_inc(v_split, 1)

            def low_half(dst, src, hi):
                return g.tensor_tensor(dst[:, :], src[:, :], hi[:, :], ALU.subtract)

            for t in (kvt_hi, kvt_lo):
                g.memset(t[:, :, :].bitcast(F32), 0.0).then_inc(kvt_zeroed, 1)
            eng.wait_ge(pool_const, 2)
            eng.wait_ge(const_ready, 1)
            mask_columns(0)
            values_low(0)
            eng.wait_ge(brow_ld, 16)
            g.tensor_scalar(brow[:, 2, :], brow[:, 2, :], 0.2, None, ALU.mult).then_inc(sb2_scaled, 1)
            eng.wait_ge(misc_ld, 32)
            for k in range(2):
                g.tensor_copy(rows[:, :, D + k].bitcast(I32), dest[:, :, k]).then_inc(meta_ids, 1)

            def divide(b):
                for j in range(2):
                    n = 2 * b + j
                    eng.wait_ge(qkv_copied, 4 * n + 4)
                    eng.wait_ge(inverted, n + 1)
                    g.tensor_tensor(o32[:, j, :], num[j][:, :], rden[j][:, :], ALU.mult).then_inc(divided, 1)
                    eng.wait_ge(o_high, n + 1)
                    g.tensor_tensor(o_lo[:, j, :], o32[:, j, :], o_hi[:, j, :], ALU.subtract).then_inc(o_split, 1)

            def add_bo(b):
                eng.wait_ge(ln1_out, TT * b + TT)
                add_row(b, 1, bo_added)

            def add_sb2(b):
                eng.wait_ge(ln2_out, TT * b + TT)
                add_row(b, 2, sb2_added)

            def shared_low(q):
                eng.wait_ge(w_hi[q], 1)
                low_half(sw_lo[q], raw[q], sw_hi[q]).then_inc(w_lo[q], 1)

            def dispatch(n, lo, hi):
                eng.wait_ge(slots_ready, n + 1)
                for t in range(lo, hi):
                    for k in range(2):
                        g.indirect_dma_start(out=xbuf, out_offset=bass.IndirectOffsetOnAxis(ap=slot_i[:, t, k:k + 1], axis=0),
                                             in_=rows[:, t, :], in_offset=None,
                                             bounds_check=last_slot, oob_is_err=False).then_inc(dispatched, 16)

            eng.wait_ge(sb2_scaled, 1)
            def invert_deviation(b):
                eng.wait_ge(ln2_mv, TT * b + TT)
                g.tensor_scalar(sd2[:, :], mv2[:, :, 1], LN_EPS, None, ALU.add).then_inc(ln2_sd, 1)
                eng.wait_ge(ln2_sd, b + 1)
                g.tensor_tensor(rstd2[:, :], sd2[:, :], minus_half[:, :], ALU.pow).then_inc(ln2_rs, 1)

            for b in range(B):
                if b:
                    divide(b - 1)
                add_bo(b)
                if b > 1:
                    add_sb2(b - 2)
                if b + 1 < B:
                    mask_columns(b + 1)
                    values_low(b + 1)
                shared_low(b)
            invert_deviation(B - 2)
            eng.wait_ge(prefilled, 32)
            eng.wait_ge(meta_ids, 2)
            dispatch(0, 0, 3)
            invert_deviation(B - 1)
            dispatch(0, 3, 4)
            add_sb2(B - 2)
            dispatch(1, *ROUNDS[1])
            dispatch(2, *ROUNDS[2])
            add_sb2(B - 1)

            def expert_low(e, q):
                eng.wait_ge(w_hi[q], e + 2)
                low_half(ew_lo[q], raw[q], ew_hi[q]).then_inc(w_lo[q], 1)

            expert_low(0, 1)

            def send_rows(par):
                for j in range(ST):
                    choice = j // (ST // 2)
                    idx = meta[par][:, j, choice:choice + 1].bitcast(I32)
                    g.indirect_dma_start(out=ybuf, out_offset=bass.IndirectOffsetOnAxis(ap=idx, axis=0),
                                         in_=yw[par][:, j, :], in_offset=None,
                                         bounds_check=last_row, oob_is_err=False).then_inc(y_sent[par], 16)

            def expert(e, par, seen):
                expert_low(e, 2)
                expert_low(e, 3)
                eng.wait_ge(tout_evac, 2 * e)
                eng.wait_ge(meta_ld[1 - par], seen)
                expert_low(e + 1, 1)
                send_rows(1 - par)

            expert_low(0, 2)
            expert_low(0, 3)
            expert_low(1, 1)
            with eng.Fori(0, 3) as i:
                expert(2 * i + 1, 1, 16 * i + 16)
                expert(2 * i + 2, 0, 16 * i + 16)
            expert_low(E - 1, 2)
            expert_low(E - 1, 3)
            for par in range(2):
                eng.wait_ge(meta_ld[par], 16 * E // 2)
            eng.wait_ge(tout_evac, 2 * E - 2)
            send_rows(0)
            eng.wait_ge(tout_evac, 2 * E)
            send_rows(1)
            for n, t in enumerate(range(NT // 2, NT)):
                eng.wait_ge(rows_weighted, 2 * n + 2)
                g.tensor_tensor(yk[:, 0, t, :], yk[:, 0, t, :], yk[:, 1, t, :], ALU.add).then_inc(rows_summed, 1)

        @block.scalar
        def _(eng):
            a = nc.scalar
            eng.dma_start(ctx_sb[:, :, :], ctx[0].rearrange("(t p) d -> p t d", p=P)).then_inc(ctx_in[0], 16)
            eng.dma_start(bcol[:, :], bcol_d).then_inc(bcol_ld, 16)

            def full(stage, b, j=0):
                eng.wait_ge(att_full, AT[(stage, b, j)] + 1)

            def hi_done(ins):
                ins.then_inc(att_hi, 1)

            def chunk_hi(i):
                eng.wait_ge(aw_ld[i], 16)
                a.activation(aw_hi[i][:, :], raw_aw(i), ACT.Copy).then_inc(aw_hi_done, 1)

            def ln_sqrt(mvt, sdt, s_mv, s_sd, b):
                eng.wait_ge(s_mv, TT * b + TT)
                a.activation(sdt[:, :], mvt[:, :, 1], ACT.Sqrt, bias=LN_EPS).then_inc(s_sd, 1)

            def ln_apply(dst, rs, nm, s_rs, s_out, b):
                eng.wait_ge(s_rs, 2 * b + 2)
                for tt in range(TT):
                    a.activation(dst(tt), res[:, TT * b + tt, :], ACT.Identity,
                                 scale=rs[:, tt:tt + 1], bias=nm[:, tt:tt + 1]).then_inc(s_out, 1)

            def ln1_sqrt(b):
                ln_sqrt(mv[b % 2], sd[b % 2], ln1_mv, ln1_sd, b)

            def ln1_apply(b):
                if b:
                    full("tx", b - 1)
                ln_apply(lambda tt: xn[:, tt, :], rstd[b % 2], nmr[b % 2], ln1_rs, ln1_out, b)

            def ln2_apply(b):
                ln_apply(lambda tt: rows[:, TT * b + tt, 0:D], rstd2, nmr2, ln2_rs, ln2_out, b)

            def turned_hi(stage, dst, b):
                full(stage, b)
                hi_done(a.activation(dst[:, :, :], ps[BANK[AT[(stage, b, 0)]]][:, :], ACT.Copy))

            def biased_hi(stage, dst, c, b):
                full(stage, b)
                bank = ps[BANK[AT[(stage, b, 0)]]]
                for m in range(KD):
                    hi_done(a.activation(dst[:, m, :], bank[:, S * m:S * m + S], ACT.Identity,
                                         bias=bcol[:, c + m:c + m + 1]))

            def values_hi(b):
                wait_finished(eng, ("v", b, 0))
                for tt in range(TT):
                    a.activation(v_hi[:, tt, :, 0:FD], v32[:, tt, :].rearrange("p (g c) -> p g c", g=4), ACT.Copy,
                                 scale=bcol[:, MK + TT * b + tt:MK + TT * b + tt + 1]).then_inc(v_high, 1)

            def features_hi(stage, dst, b, js):
                for j in js:
                    full(stage, b, j)
                    hi_done(a.activation(dst(j), ps[BANK[AT[(stage, b, j)]]][:, :], ACT.Relu))

            def shared_weights_hi(q):
                eng.wait_ge(w_ld[q], 16)
                a.activation(sw_hi[q][:, :], raw[q][:, :], ACT.Copy).then_inc(w_hi[q], 1)

            def normed_hi(b):
                full("t2", b)
                hi_done(a.activation(xt_hi[:, :, S * b:S * b + S],
                                     ps[BANK[AT[("t2", b, 0)]]][:, :].rearrange("p (k n) -> p k n", k=KD), ACT.Copy))

            ln1_sqrt(0)
            chunk_hi(0)
            ln1_apply(0)
            turned_hi("tc", ct_hi, 0)
            chunk_hi(1)
            turned_hi("tx", nt_hi, 0)
            chunk_hi(2)
            chunk_hi(3)
            eng.wait_ge(bcol_ld, 16)
            a.activation(mask_hi[:, :], bcol[:, MK:MK + NT], ACT.Copy).then_inc(mask_hi_done, 1)
            biased_hi("k", k_hi, BK, 0)
            values_hi(0)
            biased_hi("q", q_hi, BQ, 0)
            chunk_hi(4)
            chunk_hi(5)
            eng.wait_ge(misc_ld, 32)
            a.activation(gate_hi[:, :, :], gate_raw[:, :, :], ACT.Copy).then_inc(gate_hi_done, 1)

            def quotients(b, js):
                for j in js:
                    full("qkv", b, j)
                    bank = ps[BANK[AT[("qkv", b, j)]]]
                    for i in range(2):
                        a.activation(den[j][FD * i:FD * i + FD, :], bank[FD:P, S * i:S * i + S], ACT.Identity,
                                     bias=DEN_EPS).then_inc(qkv_copied, 1)
                    for i in range(2):
                        a.activation(num[j][FD * i:FD * i + FD, :], bank[0:FD, S * i:S * i + S],
                                     ACT.Copy).then_inc(qkv_copied, 1)

            def logits_copy(n):
                full("lg", n)
                lo, hi = ROUNDS[n]
                c = lgt_column(n)
                a.activation(lgt[:, c:c + (hi - lo) * P], ps[BANK[AT[("lg", n, 0)]]][0:E, 0:(hi - lo) * P],
                             ACT.Copy).then_inc(lg_copied, 1)

            def quotients_hi(b, j):
                eng.wait_ge(divided, 2 * b + j + 1)
                a.activation(o_hi[:, j, :], o32[:, j, :], ACT.Copy).then_inc(o_high, 1)

            def gelu_groups(body, ms, n, bias):
                for m in ms:
                    g0 = body * NG + m
                    eng.wait_ge(g1_full, g0 + 1)
                    if not isinstance(body, int) or g0 >= 3:
                        eng.wait_ge(h_split, g0 - 2)
                    if m < MH:
                        a.activation(h32[m % 3][:, 0:n], ps[m % 3][:, 0:n], ACT.Gelu,
                                     bias=bias[:, m:m + 1]).then_inc(gelu_done, 1)
                    else:
                        a.activation(h32[m % 3][0:AP3, 0:n], ps[m % 3][0:AP3, 0:n], ACT.Gelu).then_inc(gelu_done, 1)

            shared_bias = bcol[:, 0:NB]

            queries = lambda j: qf_hi[:, 2 * j:2 * j + 2, :]
            for b in range(B):
                last = b == B - 1
                features_hi("kf", lambda j: kf_hi[:, j // 2, j % 2, :], b, range(4))
                if b and not last:
                    ln1_apply(b + 1)
                if last:
                    logits_copy(0)
                features_hi("qf", queries, b, range(2))
                if b:
                    quotients_hi(b - 1, 0)
                else:
                    ln1_sqrt(1)
                features_hi("qf", queries, b, range(2, 4))
                if b:
                    quotients_hi(b - 1, 1)
                if not last:
                    turned_hi("tc", ct_hi, b + 1)
                for j in range(2):
                    full("kv", b, j)
                    a.activation(kvm[:, 2 * j:2 * j + 2, :], ps[BANK[AT[("kv", b, j)]]][:, :], ACT.Copy).then_inc(kv_copied, 1)
                if b == 0:
                    ln1_apply(1)
                if b + 2 < B:
                    ln1_sqrt(b + 2)
                for j in range(2):
                    full("tkv", b, j)
                    for i in range(2):
                        dst, src = kv_blocks(kvt_hi, b, j, i)
                        hi_done(a.activation(dst, src, ACT.Copy))
                if last:
                    break
                if b:
                    ln_sqrt(mv2, sd2, ln2_mv, ln2_sd, b - 1)
                turned_hi("tx", nt_hi, b + 1)
                biased_hi("k", k_hi, BK, b + 1)
                if b:
                    ln2_apply(b - 1)
                shared_weights_hi(b)
                values_hi(b + 1)
                biased_hi("q", q_hi, BQ, b + 1)
                if b:
                    normed_hi(b - 1)
                if b == 1:
                    eng.wait_ge(ad_ld, 16)
                    a.activation(sdn_hi[:, :, :, :], down_copies(), ACT.Copy).then_inc(ad_hi, 1)
                    a.activation(sup[:, :], raw_ad[0:AP3, KD * RANK:AD], ACT.Copy).then_inc(ad_hi, 1)
                quotients(b, range(2))
            shared_weights_hi(B - 1)
            a.activation(warm[:, :], bcol[:, 0:1], ACT.Gelu)
            quotients(B - 1, [0])
            quotients(B - 1, [1])
            gelu_groups(0, range(2), S, shared_bias)
            ln2_apply(B - 2)
            gelu_groups(0, range(2, 3), S, shared_bias)
            normed_hi(B - 2)
            quotients_hi(B - 1, 0)
            quotients_hi(B - 1, 1)
            logits_copy(1)

            def expert_hi(e, q):
                if isinstance(e, int) and e == 0:
                    eng.wait_ge(att_full, LAST_ATT)
                elif q < 2:
                    eng.wait_ge(g1_full, (e - 1 + FIRST) * NG + 4 * q + 4)
                else:
                    eng.wait_ge(y_full, 2 * e)
                eng.wait_ge(w_ld[q], 16 * e + 32)
                a.activation(ew_hi[q][:, :], raw[q][:, :], ACT.Copy).then_inc(w_hi[q], 1)

            def down_hi(e):
                if not (isinstance(e, int) and e == 0):
                    eng.wait_ge(g1_full, (e - 1 + FIRST) * NG + NG)
                eng.wait_ge(ad_ld, 16 * e + 32)
                a.activation(dn_hi[:, :, :, :], down_copies(), ACT.Copy).then_inc(ad_hi, 1)

            def up_hi(e):
                a.activation(up[:, :], raw_ad[0:AP3, KD * RANK:AD], ACT.Copy).then_inc(ad_hi, 1)

            def rows_hi(e, par):
                for k in range(KD):
                    eng.wait_ge(tin_full, 2 * e + 1 + k)
                    a.activation(xe_hi[:, k, :], ps[5 + k][:, 0:SLOTS], ACT.Copy).then_inc(tin_hi, 1)

            gelu_groups(0, range(3, 5), S, shared_bias)
            ln2_apply(B - 1)
            gelu_groups(0, range(5, 6), S, shared_bias)
            normed_hi(B - 1)
            gelu_groups(0, range(6, NG), S, shared_bias)
            logits_copy(2)
            expert_hi(0, 0)
            expert_hi(0, 1)
            gelu_groups(1, range(NG), S, shared_bias)
            down_hi(0)
            eng.wait_ge(z_ready, 2)
            a.activation(tmp_exp[:, :, :], z[:, :, :], ACT.Exp).then_inc(exp_done, 1)
            a.activation(prob[:, 1, :], prob[:, 0, :], ACT.Exp).then_inc(exp_done, 1)
            a.activation(warm[:, :], bcol[:, 0:1], ACT.Gelu)
            rows_hi(0, 0)

            def expert(e, par, bias_seen, last=False):
                body = e + FIRST
                eng.wait_ge(bias_ld[par], bias_seen)
                gelu_groups(body, range(2), SLOTS, bexp[par])
                expert_hi(e, 2)
                gelu_groups(body, range(2, 4), SLOTS, bexp[par])
                expert_hi(e, 3)
                gelu_groups(body, range(4, 6), SLOTS, bexp[par])
                up_hi(e)
                gelu_groups(body, range(6, NG), SLOTS, bexp[par])
                if not last:
                    expert_hi(e + 1, 0)
                    expert_hi(e + 1, 1)
                    down_hi(e + 1)
                    rows_hi(e + 1, 1 - par)
                for d in range(KD):
                    eng.wait_ge(y_full, 2 * e + 1 + d)
                    a.activation(ye[:, d, :], ps[3 + d][:, 0:SLOTS], ACT.Identity,
                                 bias=bexp[par][:, MH + d:MH + d + 1]).then_inc(y_evac, 1)

            expert(0, 0, 16)
            with eng.Fori(0, 3) as i:
                expert(2 * i + 1, 1, 16 * i + 16)
                expert(2 * i + 2, 0, 16 * i + 32)
            expert(E - 1, 1, 64, last=True)
            for body in (TAIL, TAIL + 1):
                gelu_groups(body, range(NG), S, shared_bias)
            eng.wait_ge(prob_ready, 1)
            eng.wait_ge(yk_ld[1], 32)
            for t in range(NT // 2, NT):
                for k in range(2):
                    a.activation(yk[:, k, t, :], yk[:, k, t, :], ACT.Copy,
                                 scale=prob[:, k, t:t + 1]).then_inc(rows_weighted, 1)

        @block.tensor
        def _(eng):
            pe = nc.tensor

            def mm(dst, pairs, last_inc=None, start=True, stop=True):
                for n, (w, m) in enumerate(pairs):
                    ins = pe.matmul(dst, w, m, start=start and n == 0, stop=stop and n == len(pairs) - 1)
                return ins

            def bank_of(g):
                n = AT[g]
                before = [ORDER[i] for i in range(n) if BANK[i] == BANK[n]]
                if before:
                    wait_finished(eng, before[-1])
                return ps[BANK[n]]

            def done(stage, b, j=0):
                wait_finished(eng, (stage, b, j))

            def full(ins):
                ins.then_inc(att_full, 1)

            def turn(g, src):
                bank = bank_of(g)
                for k in range(KD):
                    for tt in range(TT):
                        ins = pe.transpose(bank[:, k * S + tt * P:k * S + tt * P + P],
                                           src(tt)[:, k * P:k * P + P], ident)
                full(ins)

            def aw(i, c, n):
                return aw_hi[i][:, c:c + n], aw_lo[i][:, c:c + n]

            def project(stage, b, i, src_hi, src_lo):
                bank = bank_of((stage, b, 0))
                for m in range(KD):
                    pairs = []
                    for k in range(KD):
                        wh, wl = aw(i, k * D + m * P, P)
                        pairs += split3(wh, wl, src_hi[:, k, :], src_lo[:, k, :])
                    ins = mm(bank[:, m * S:m * S + S], pairs)
                full(ins)

            def project_rows(g, i, src_hi, src_lo):
                bank = bank_of(g)
                for tt in range(TT):
                    pairs = []
                    for k in range(KD):
                        mh, ml = aw(i, k * D, D)
                        pairs += split3(src_hi[:, k, tt * P:tt * P + P], src_lo[:, k, tt * P:tt * P + P], mh, ml)
                    ins = mm(bank[:, tt * D:tt * D + D], pairs)
                full(ins)

            def turn_context(b):
                eng.wait_ge(ctx_in[b], 16)
                turn(("tc", b, 0), lambda tt: ctx_sb[:, tt, :])

            def turn_queries(b):
                eng.wait_ge(ln1_out, TT * b + TT)
                turn(("tx", b, 0), lambda tt: xn[:, tt, :])

            def project_keys(b):
                if b == 0:
                    eng.wait_ge(aw_lo_done, 1)
                done("tc", b)
                project("k", b, 0, ct_hi, ct_lo)

            def project_values(b):
                if b == 0:
                    eng.wait_ge(aw_lo_done, 2)
                project_rows(("v", b, 0), 1, ct_hi, ct_lo)

            def project_queries(b):
                if b == 0:
                    eng.wait_ge(aw_lo_done, 3)
                done("tx", b)
                project("q", b, 2, nt_hi, nt_lo)

            def key_features(b):
                done("k", b)
                if b == 0:
                    eng.wait_ge(aw_lo_done, 4)
                for j in range(4):
                    tt, k = j // 2, j % 2
                    bank = bank_of(("kf", b, j))
                    full(mm(bank[:, :], split3(k_hi[:, k, tt * P:tt * P + P], k_lo[:, k, tt * P:tt * P + P], *aw(3, 0, 512))))

            def query_features(b):
                done("q", b)
                if b == 0:
                    eng.wait_ge(aw_lo_done, 5)
                for j in range(4):
                    bank = bank_of(("qf", b, j))
                    for i in range(2):
                        m = 2 * j + i
                        wh, wl = aw(4, (m % 4) * P, P)
                        ins = mm(bank[:, i * S:i * S + S], split3(wh, wl, q_hi[:, m // 4, :], q_lo[:, m // 4, :]))
                    full(ins)

            def attention_out(b):
                eng.wait_ge(o_split, 2 * b + 2)
                if b == 0:
                    eng.wait_ge(aw_lo_done, 6)
                project_rows(("wo", b, 0), 5, o_hi, o_lo)

            def turn_normed(b):
                eng.wait_ge(ln2_out, TT * b + TT)
                turn(("t2", b, 0), lambda tt: rows[:, TT * b + tt, 0:D])

            def key_values(b):
                eng.wait_ge(v_split, TT * b + TT)
                eng.wait_ge(vmask, 4 * b + 4)
                for j in range(2):
                    bank = bank_of(("kv", b, j))
                    for i in range(2):
                        g = 2 * j + i
                        pairs = []
                        for tt in range(TT):
                            done("kf", b, 2 * tt + g // 2)
                            c = (g % 2) * S
                            pairs += split3(v_hi[:, tt, g, :], v_lo[:, tt, g, :],
                                            kf_hi[:, tt, g // 2, c:c + S], kf_lo[:, tt, g // 2, c:c + S])
                        ins = mm(bank[:, i * S:i * S + S], pairs)
                    full(ins)

            def turn_key_values(b):
                for part in range(2):
                    done("kv", b, part)
                    for j in range(2):
                        bank = bank_of(("tkv", b, j))
                        for g in (2 * part, 2 * part + 1):
                            ins = pe.transpose(bank[:, g * P:g * P + P], kvm[:, g, j * P:j * P + P], ident)
                        if part:
                            full(ins)

            def attend(b):
                done("tkv", b, 1)
                if b == 0:
                    eng.wait_ge(kvt_zeroed, 2)
                for j in range(2):
                    bank = bank_of(("qkv", b, j))
                    for i in range(2):
                        g = 2 * j + i
                        done("qf", b, g)
                        pairs = []
                        for c in range(2):
                            pairs += split3(kvt_hi[:, 2 * g + c, :], kvt_lo[:, 2 * g + c, :],
                                            qf_hi[:, 2 * g + c, :], qf_lo[:, 2 * g + c, :])
                        ins = mm(bank[:, i * S:i * S + S], pairs)
                    full(ins)

            def spin(n):
                for _ in range(n):
                    pe.matmul(ps[7][0:FD, 0:FD], ones[:, :], ones[:, :], start=True, stop=True)

            eng.wait_ge(pool_const, 1)
            spin(14)
            eng.wait_ge(ident_ld, 16)
            turn_context(0)
            spin(6)
            turn_queries(0)
            spin(3)
            project_keys(0)
            project_values(0)
            project_queries(0)

            def logits(n):
                lo, hi = ROUNDS[n]
                done("t2", TT * hi // 4 - 1)
                if n == 0:
                    eng.wait_ge(const_ready, 3)
                bank = bank_of(("lg", n, 0))
                pairs = []
                for k in range(KD):
                    pairs += split3(gate_hi[:, k, :], gate_lo[:, k, :], xt_hi[:, k, lo * P:hi * P], xt_lo[:, k, lo * P:hi * P])
                full(mm(bank[0:GP, 0:(hi - lo) * P], pairs))

            def turn_logits(n):
                lo, hi = ROUNDS[n]
                done("lg", n)
                bank = bank_of(("tlg", n, 0))
                for t in range(hi - lo):
                    c = lgt_column(n) + P * t
                    ins = pe.transpose(bank[:, E * t:E * t + E], lgt[:, c:c + P], ident[0:E, 0:E])
                full(ins)

            def places(n):
                lo, hi = ROUNDS[n]
                eng.wait_ge(hot_ready, n + 1)
                bank = bank_of(("pos", n, 0))
                tri, one = tri_ones[:, 0:P], tri_ones[:, P:2 * P]
                width = 2 * E
                pe.matmul(bank[:, 0:(hi - lo) * width], tri, hot[:, lo:hi, :, :], start=True, stop=False)
                for t in range(hi - 1):
                    to = max(t + 1, lo)
                    ins = pe.matmul(bank[:, (to - lo) * width:(hi - lo) * width], one,
                                    hot[:, t, :, :].rearrange("p k e -> p (k e)").unsqueeze(1).to_broadcast([P, hi - to, width]),
                                    start=False, stop=t == hi - 2)
                full(ins)

            for b in range(B - 1):
                key_features(b)
                query_features(b)
                turn_context(b + 1)
                key_values(b)
                if b:
                    attention_out(b - 1)
                turn_key_values(b)
                turn_queries(b + 1)
                project_keys(b + 1)
                project_values(b + 1)
                project_queries(b + 1)
                if b:
                    turn_normed(b - 1)
                attend(b)
            b = B - 1
            key_features(b)
            logits(0)
            query_features(b)
            turn_logits(0)
            key_values(b)
            turn_key_values(b)
            attention_out(b - 1)
            places(0)
            attend(b)

            def hidden(body, ms, n, wh, wl, dh, dl, mh, ml):
                for m in ms:
                    g0 = body * NG + m
                    if isinstance(body, int) and g0 < 3:
                        wait_bank(eng, m)
                    else:
                        eng.wait_ge(gelu_done, g0 - 2)
                    pairs = []
                    for k in range(KD):
                        if m < MH:
                            c = k * 512 + (m % 4) * P
                            st = (wh[m // 4][:, c:c + P], wl[m // 4][:, c:c + P])
                        else:
                            st = (dh[:, k, :, :].rearrange("p a r -> p (a r)"), dl[:, k, :, :].rearrange("p a r -> p (a r)"))
                        pairs += split3(*st, mh(k), ml(k))
                    rowsn = P if m < MH else AP3
                    mm(ps[m % 3][0:rowsn, 0:n], pairs).then_inc(g1_full, 1)

            def shared_hidden(body, c, ms):
                hidden(body, ms, S, sw_hi, sw_lo, sdn_hi, sdn_lo,
                       lambda k: xt_hi[:, k, S * c:S * c + S], lambda k: xt_lo[:, k, S * c:S * c + S])

            def shared_out(body, n, tt, half):
                tok = slice(tt * P, tt * P + P)
                if half == 0:
                    if n:
                        eng.wait_ge(sh_evac, TT * (n - 1) + tt + 1)
                    else:
                        wait_bank(eng, 3 + tt)
                    if body == TAIL:
                        eng.wait_ge(y_evac, 2 * E)
                for m in range(half * MH // 2, (half + 1) * MH // 2):
                    if tt == 0:
                        eng.wait_ge(h_split, body * NG + m + 1)
                    c = (m % 4) * D
                    mm(ps[3 + tt][:, 0:D], split3(h_hi[:, m, tok], h_lo[:, m, tok],
                                                  sw_hi[2 + m // 4][:, c:c + D], sw_lo[2 + m // 4][:, c:c + D]),
                       start=m == 0, stop=False)
                if half:
                    eng.wait_ge(h_split, body * NG + NG)
                    pe.matmul(ps[3 + tt][:, 0:D], a_st[:, tok], sup[:, :], start=False, stop=True).then_inc(sh_full, 1)

            eng.wait_ge(w_lo[0], 1)
            shared_hidden(0, 0, range(4))
            eng.wait_ge(w_lo[1], 1)
            shared_hidden(0, 0, range(4, 5))
            turn_normed(B - 2)
            shared_hidden(0, 0, range(5, 6))
            attention_out(B - 1)
            logits(1)
            turn_logits(1)
            shared_hidden(0, 0, range(6, 8))

            for q in range(2, 4):
                eng.wait_ge(w_lo[q], 1)
            shared_out(0, 0, 0, 0)
            turn_normed(B - 1)
            places(1)
            eng.wait_ge(ad_lo, 2)
            shared_hidden(0, 0, range(8, NG))
            logits(2)
            shared_out(0, 0, 1, 0)
            turn_logits(2)
            shared_out(0, 0, 0, 1)
            shared_out(0, 0, 1, 1)
            places(2)
            shared_hidden(1, 1, range(NG))

            def rows_in(e, par, seen):
                eng.wait_ge(xg_ld[par], seen)
                if isinstance(e, int) and e == 0:
                    done("pos", 2)
                elif not (isinstance(e, int) and e == 1):
                    eng.wait_ge(tout_evac, 2 * e - 2)
                for k in range(KD):
                    for j in range(ST):
                        ins = pe.transpose(ps[5 + k][:, j * SP:j * SP + SP],
                                           xg[par][:, j, k * P:k * P + P], ident[0:SP, 0:SP])
                    ins.then_inc(tin_full, 1)

            def rows_out(e):
                eng.wait_ge(y_evac, 2 * e + 2)
                if not (isinstance(e, int) and e == 0):
                    eng.wait_ge(tout_evac, 2 * e)
                for j in range(ST):
                    bank = ps[7] if j < 2 else ps[5]
                    for d in range(KD):
                        c = (j % 2) * D + d * P
                        ins = pe.transpose(bank[0:SP, c:c + P], ye[:, d, j * SP:j * SP + SP], ident)
                    if j % 2:
                        ins.then_inc(tout_full, 1)

            for tt, half in ((0, 0), (0, 1), (1, 0)):
                shared_out(1, 1, tt, half)
            rows_in(0, 0, 16)
            shared_out(1, 1, 1, 1)

            def expert(e, par, seen, first=False, last=False):
                body = e + FIRST
                half = lambda ms: hidden(body, ms, SLOTS, ew_hi, ew_lo, dn_hi, dn_lo,
                                         lambda k: xe_hi[:, k, :], lambda k: xe_lo[:, k, :])
                eng.wait_ge(tin_evac, 2 * e + 2)
                eng.wait_ge(w_lo[0], e + 2)
                half(range(4))
                eng.wait_ge(w_lo[1], e + 2)
                half(range(4, MH))
                eng.wait_ge(ad_lo, 2 * e + 3)
                half([MH])
                if not first:
                    rows_out(e - 1)
                if first:
                    eng.wait_ge(sh_evac, FIRST * TT)
                else:
                    eng.wait_ge(y_evac, 2 * e)
                for m in range(MH):
                    eng.wait_ge(h_split, body * NG + m + 1)
                    if m % 4 == 0:
                        eng.wait_ge(w_lo[2 + m // 4], e + 2)
                    if m == 5 and not last:
                        rows_in(e + 1, 1 - par, seen)
                    for d in range(KD):
                        c = (m % 4) * D + d * P
                        ins = mm(ps[3 + d][:, 0:SLOTS], split3(ew_hi[2 + m // 4][:, c:c + P], ew_lo[2 + m // 4][:, c:c + P],
                                                               h_hi[:, m, :], h_lo[:, m, :]), start=m == 0, stop=False)
                eng.wait_ge(h_split, body * NG + NG)
                eng.wait_ge(ad_lo, 2 * e + 4)
                for d in range(KD):
                    pe.matmul(ps[3 + d][:, 0:SLOTS], up[:, d * P:d * P + P], a_st[:, :],
                              start=False, stop=True).then_inc(y_full, 1)

            expert(0, 0, 16, first=True)
            with eng.Fori(0, 3) as i:
                expert(2 * i + 1, 1, 16 * i + 32)
                expert(2 * i + 2, 0, 16 * i + 32)
            expert(E - 1, 1, None, last=True)
            shared_hidden(TAIL, 2, range(2))
            rows_out(E - 1)
            shared_hidden(TAIL, 2, range(2, NG))
            for tt, half in ((0, 0), (0, 1), (1, 0), (1, 1)):
                shared_out(TAIL, 2, tt, half)
            shared_hidden(TAIL + 1, 3, range(NG))
            for tt, half in ((0, 0), (1, 0), (0, 1), (1, 1)):
                shared_out(TAIL + 1, 3, tt, half)

        @block.vector
        def _(eng):
            v = nc.vector
            steps = [0]

            def own(ins):
                steps[0] += 1
                ins.then_inc(step, 1)
                eng.wait_ge(step, steps[0])

            def full(stage, b, j=0):
                eng.wait_ge(att_full, AT[(stage, b, j)] + 1)
                return ps[BANK[AT[(stage, b, j)]]]

            def evac(ins):
                ins.then_inc(att_evac, 1)

            hi_seen = [0]

            def after_hi(n=1):
                hi_seen[0] += n
                eng.wait_ge(att_hi, hi_seen[0])

            def low(dst, src, hi):
                return v.tensor_tensor(dst, src, hi, ALU.subtract)

            def statistics(b, st, mvt, s_mv):
                for tt in range(TT):
                    ins = v.bn_stats(st[:, tt, :], res[:, TT * b + tt, :])
                own(ins)
                for tt in range(TT):
                    v.bn_aggr(mvt[:, tt, :], st[:, tt, :]).then_inc(s_mv, 1)

            def factors(b, mvt, sdt, rs, nm, s_sd, s_rs):
                if sdt is not None:
                    eng.wait_ge(s_sd, b + 1)
                    v.reciprocal(rs[:, :], sdt[:, :]).then_inc(s_rs, 1)
                eng.wait_ge(s_rs, 2 * b + 1)
                v.scalar_tensor_tensor(nm[:, :], mvt[:, :, 0], -1.0, rs[:, :], ALU.mult, ALU.mult).then_inc(s_rs, 1)

            def turned_low(stage, lo, hi, b):
                bank = full(stage, b)
                after_hi()
                evac(low(lo[:, :, :], bank[:, :], hi[:, :, :]))

            def biased_low(stage, lo, hi, c, b):
                bank = full(stage, b)
                after_hi(KD)
                for m in range(KD):
                    ins = v.scalar_tensor_tensor(lo[:, m, :], bank[:, S * m:S * m + S], bcol[:, c + m:c + m + 1],
                                                 hi[:, m, :], ALU.add, ALU.subtract)
                evac(ins)

            def values(b):
                bank = full("v", b)
                evac(v.tensor_tensor(v32[:, :, :], bank[:, :].rearrange("p (t d) -> p t d", t=TT),
                                     brow[:, 0, :].unsqueeze(1).to_broadcast([P, TT, D]), ALU.add))

            def relu_low(dst, bank, hi):
                return v.scalar_tensor_tensor(dst, bank[:, :], 0.0, hi, ALU.max, ALU.subtract)

            def ln2_factors(b):
                factors(b, mv2, sd2 if b < B - 2 else None, rstd2, nmr2, ln2_sd, ln2_rs)

            def ln1_factors(b):
                factors(b, mv[b % 2], sd[b % 2], rstd[b % 2], nmr[b % 2], ln1_sd, ln1_rs)

            def chunk_low(i):
                eng.wait_ge(aw_hi_done, i + 1)
                low(aw_lo[i][:, :], raw_aw(i), aw_hi[i][:, :]).then_inc(aw_lo_done, 1)

            eng.wait_ge(x_in[0], 16)
            statistics(0, stats, mv[0], ln1_mv)
            ln1_factors(0)
            chunk_low(0)
            turned_low("tc", ct_lo, ct_hi, 0)
            chunk_low(1)
            turned_low("tx", nt_lo, nt_hi, 0)
            chunk_low(2)
            chunk_low(3)
            eng.wait_ge(mask_hi_done, 1)
            v.tensor_tensor(mask_lo[:, :], bcol[:, MK:MK + NT], mask_hi[:, :], ALU.subtract).then_inc(const_ready, 1)
            biased_low("k", k_lo, k_hi, BK, 0)
            eng.wait_ge(brow_ld, 16)
            values(0)
            biased_low("q", q_lo, q_hi, BQ, 0)
            chunk_low(4)

            def attention_sum(b):
                bank = full("wo", b)
                eng.wait_ge(bo_added, b + 1)
                tok = res[:, TT * b:TT * b + TT, :]
                evac(v.tensor_tensor(tok, bank[:, :].rearrange("p (t d) -> p t d", t=TT), tok, ALU.add))
                wait_finished(eng, ("wo", b, 0))
                statistics(b, stats2, mv2, ln2_mv)

            def keys_low(b, j):
                bank = full("kf", b, j)
                after_hi()
                evac(relu_low(kf_lo[:, j // 2, j % 2, :], bank, kf_hi[:, j // 2, j % 2, :]))

            def queries_low(b, j):
                bank = full("qf", b, j)
                after_hi()
                evac(relu_low(qf_lo[:, 2 * j:2 * j + 2, :], bank, qf_hi[:, 2 * j:2 * j + 2, :]))

            def normed_low(b):
                bank = full("t2", b)
                after_hi()
                evac(low(xt_lo[:, :, S * b:S * b + S], bank[:, :].rearrange("p (k n) -> p k n", k=KD),
                         xt_hi[:, :, S * b:S * b + S]))

            def choose(n):
                lo, hi = ROUNDS[n]
                m = hi - lo
                t = slice(lo, hi)
                bank = full("tlg", n)
                evac(v.tensor_copy(lg[:, t, :], bank[:, 0:m * E].rearrange("p (t e) -> p t e", e=E)))
                wait_finished(eng, ("tlg", n, 0))
                for i in range(lo, hi):
                    ins = v.max(top[:, i, :], lg[:, i, :])
                own(ins)
                for i in range(lo, hi):
                    ins = v.max_index(top_i[:, i, :], top[:, i, :], lg[:, i, :])
                own(ins)
                own(v.tensor_copy(expert_no[:, t, :], top_i[:, t, 0:2]))
                v.tensor_tensor(hot[:, t, :, :], cst[:, C_EXP:C_EXP + E].unsqueeze(1).unsqueeze(1).to_broadcast([P, m, 2, E]),
                                expert_no[:, t, :].unsqueeze(3).to_broadcast([P, m, 2, E]), ALU.is_equal).then_inc(hot_ready, 1)
                own(v.scalar_tensor_tensor(slot[:, t, :], expert_no[:, t, :], float(SLOTS),
                                           cst[:, C_BASE:C_BASE + 2 * m].rearrange("p (t k) -> p t k", k=2), ALU.mult, ALU.add))

            def slots(n):
                lo, hi = ROUNDS[n]
                t = slice(lo, hi)
                bank = full("pos", n)
                eng.wait_ge(hot_ready, n + 1)
                evac(v.tensor_tensor(queue_place[:, t, :, :], hot[:, t, :, :],
                                     bank[:, 0:(hi - lo) * 2 * E].rearrange("p (t k e) -> p t k e", k=2, e=E), ALU.mult))
                wait_finished(eng, ("pos", n, 0))
                own(v.tensor_reduce(place[:, t, :], queue_place[:, t, :, :], AX_X, ALU.add))
                own(v.tensor_tensor(slot[:, t, :], slot[:, t, :], place[:, t, :], ALU.add))
                own(v.tensor_scalar(place[:, t, :], place[:, t, :], float(CAP), float(NOWHERE), ALU.is_ge, ALU.mult))
                own(v.tensor_tensor(slot[:, t, :], slot[:, t, :], place[:, t, :], ALU.add))
                v.tensor_copy(slot_i[:, t, :], slot[:, t, :]).then_inc(slots_ready, 1)

            def invert(b, j):
                eng.wait_ge(qkv_copied, 4 * (2 * b + j) + 2)
                v.reciprocal(rden[j][:, :], den[j][:, :]).then_inc(inverted, 1)

            def key_values_low(b):
                for j in range(2):
                    full("tkv", b, j)
                    after_hi(2)
                    for i in range(2):
                        dst, src = kv_blocks(kvt_lo, b, j, i)
                        ins = low(dst, src, kv_blocks(kvt_hi, b, j, i)[0])
                    evac(ins)

            for b in range(B - 1):
                if b:
                    invert(b - 1, 0)
                for j in range(4):
                    keys_low(b, j)
                if b:
                    invert(b - 1, 1)
                else:
                    eng.wait_ge(x_in[1], 16)
                    statistics(1, stats, mv[1], ln1_mv)
                for j in range(4):
                    queries_low(b, j)
                if b == 0:
                    ln1_factors(1)
                turned_low("tc", ct_lo, ct_hi, b + 1)
                if b + 2 < B:
                    eng.wait_ge(x_in[b + 2], 16)
                    statistics(b + 2, stats, mv[b % 2], ln1_mv)
                if b:
                    attention_sum(b - 1)
                key_values_low(b)
                if b + 2 < B:
                    ln1_factors(b + 2)
                if b:
                    ln2_factors(b - 1)
                turned_low("tx", nt_lo, nt_hi, b + 1)
                biased_low("k", k_lo, k_hi, BK, b + 1)
                values(b + 1)
                biased_low("q", q_lo, q_hi, BQ, b + 1)
                if b:
                    normed_low(b - 1)
                if b == 0:
                    chunk_low(5)
                    eng.wait_ge(cst_ld, 16)
                    v.tensor_copy(tri_ones[:, :], cst[:, C_TRI:C_TRI + 2 * P]).then_inc(const_ready, 1)
                    eng.wait_ge(gate_hi_done, 1)
                    low(gate_lo[:, :, :], gate_raw[:, :, :], gate_hi[:, :, :]).then_inc(const_ready, 1)
                if b == 1:
                    eng.wait_ge(ad_hi, 2)
                    low(sdn_lo[:, :, :, :], down_copies(), sdn_hi[:, :, :, :]).then_inc(ad_lo, 1)
                    v.tensor_tensor(sup[2 * RANK:AP3, :], raw_ad[2 * RANK:AP3, KD * RANK:AD], sup[2 * RANK:AP3, :],
                                    ALU.subtract).then_inc(ad_lo, 1)
            b = B - 1
            invert(b - 1, 0)
            for j in range(4):
                keys_low(b, j)
            invert(b - 1, 1)
            for j in range(4):
                queries_low(b, j)
            choose(0)
            key_values_low(b)
            attention_sum(b - 1)
            slots(0)
            for j in range(2):
                invert(b, j)
                if j == 0:
                    ln2_factors(b - 1)
                eng.wait_ge(inverted, 2 * b + j + 1)
                eng.wait_ge(qkv_copied, 4 * (2 * b + j) + 4)
                v.tensor_tensor(o32[:, j, :], num[j][:, :], rden[j][:, :], ALU.mult).then_inc(divided, 1)
            for j in range(2):
                eng.wait_ge(o_high, 2 * b + j + 1)
                low(o_lo[:, j, :], o32[:, j, :], o_hi[:, j, :]).then_inc(o_split, 1)

            def split_groups(body, ms, n):
                for m in ms:
                    g0 = body * NG + m
                    eng.wait_ge(gelu_done, g0 + 1)
                    src = h32[m % 3]
                    if m < MH:
                        v.tensor_copy(h_hi[:, m, 0:n], src[:, 0:n]).then_inc(h_hi_done, 1)
                        eng.wait_ge(h_hi_done, g0 + 1)
                        low(h_lo[:, m, 0:n], src[:, 0:n], h_hi[:, m, 0:n]).then_inc(h_split, 1)
                    else:
                        v.tensor_copy(a_st[:, 0:n], src[0:AP3, 0:n]).then_inc(h_hi_done, 1)
                        eng.wait_ge(h_hi_done, g0 + 1)
                        mid = slice(RANK, 2 * RANK)
                        low(a_st[mid, 0:n], src[mid, 0:n], a_st[mid, 0:n]).then_inc(h_split, 1)

            def add_shared(c, n, tts):
                for tt in tts:
                    eng.wait_ge(sh_full, TT * n + tt + 1)
                    if tt == 0:
                        eng.wait_ge(sb2_added, c + 1)
                    tok = res[:, TT * c + tt, :]
                    v.scalar_tensor_tensor(tok, ps[3 + tt][:, 0:D], 0.2, tok, ALU.mult, ALU.add).then_inc(sh_evac, 1)

            normed_low(B - 2)
            split_groups(0, range(2), S)
            attention_sum(B - 1)
            split_groups(0, range(2, 4), S)
            ln2_factors(B - 1)
            split_groups(0, range(4, 5), S)
            choose(1)
            split_groups(0, range(5, 6), S)
            normed_low(B - 1)
            slots(1)
            split_groups(0, range(6, NG), S)
            choose(2)
            add_shared(0, 0, [0])
            slots(2)
            add_shared(0, 0, [1])
            v.tensor_tensor(z[:, :, :], lg[:, :, :], top[:, :, 0:1].to_broadcast([P, NT, E]), ALU.subtract).then_inc(z_ready, 1)
            v.tensor_tensor(prob[:, 0, :], top[:, :, 1], top[:, :, 0], ALU.subtract).then_inc(z_ready, 1)
            split_groups(1, range(NG), S)

            def rows_low(e):
                for k in range(KD):
                    eng.wait_ge(tin_hi, 2 * e + 1 + k)
                    low(xe_lo[:, k, :], ps[5 + k][:, 0:SLOTS], xe_hi[:, k, :]).then_inc(tin_evac, 1)

            def results(e, par, sent):
                if sent is not None:
                    eng.wait_ge(y_sent[par], sent)
                for j in range(ST):
                    if j % 2 == 0:
                        eng.wait_ge(tout_full, 2 * e + 1 + j // 2)
                        bank = ps[7] if j == 0 else ps[5]
                        v.tensor_copy(yw[par][:, j:j + 2, :], bank[0:SP, :].rearrange("p (j d) -> p j d", j=2)
                                      ).then_inc(tout_evac, 1)

            def first_low(e):
                eng.wait_ge(w_hi[0], e + 2)
                low(ew_lo[0][:, :], raw[0][:, :], ew_hi[0][:, :]).then_inc(w_lo[0], 1)

            def down_low(e):
                eng.wait_ge(ad_hi, 2 * e + 3)
                low(dn_lo[:, :, :, :], down_copies(), dn_hi[:, :, :, :]).then_inc(ad_lo, 1)

            def up_low(e):
                eng.wait_ge(ad_hi, 2 * e + 4)
                v.tensor_tensor(up[2 * RANK:AP3, :], raw_ad[2 * RANK:AP3, KD * RANK:AD], up[2 * RANK:AP3, :],
                                ALU.subtract).then_inc(ad_lo, 1)

            first_low(0)
            down_low(0)
            add_shared(1, 1, [0])
            rows_low(0)
            add_shared(1, 1, [1])
            eng.wait_ge(exp_done, 2)
            own(v.tensor_reduce(esum[:, :], tmp_exp[:, :, :], AX_X, ALU.add))
            own(v.reciprocal(prob[:, 0, :], esum[:, :]))
            v.tensor_tensor(prob[:, 1, :], prob[:, 1, :], prob[:, 0, :], ALU.mult).then_inc(prob_ready, 1)
            eng.wait_ge(prob_ready, 1)

            def expert(e, par, sent=None, first=False, last=False):
                body = e + FIRST
                split_groups(body, range(6), SLOTS)
                up_low(e)
                split_groups(body, range(6, NG), SLOTS)
                if not first:
                    results(e - 1, 1 - par, sent)
                if not last:
                    first_low(e + 1)
                    down_low(e + 1)
                    rows_low(e + 1)

            expert(0, 0, first=True)
            expert(1, 1)
            expert(2, 0)
            with eng.Fori(1, 3) as i:
                expert(2 * i + 1, 1, sent=64 * i)
                expert(2 * i + 2, 0, sent=64 * i)
            expert(E - 1, 1, sent=64 * 3, last=True)

            def combine(k):
                eng.wait_ge(yk_ld[0], 32)
                for t in range(NT // 2):
                    tok = res[:, t, :]
                    ins = v.scalar_tensor_tensor(tok, yk[:, k, t, :], prob[:, k, t:t + 1], tok, ALU.mult, ALU.add)
                ins.then_inc(combined, 1)
                eng.wait_ge(combined, k + 1)

            split_groups(TAIL, range(2), S)
            results(E - 1, 1, 64 * 3)
            split_groups(TAIL, range(2, NG), S)
            add_shared(2, 2, range(TT))
            eng.wait_ge(sh_evac, 3 * TT)
            split_groups(TAIL + 1, range(3), S)
            combine(0)
            split_groups(TAIL + 1, range(3, NG), S)
            combine(1)
            for n, t in enumerate(range(NT // 2, NT)):
                eng.wait_ge(rows_summed, n + 1)
                v.tensor_tensor(res[:, t, :], yk[:, 0, t, :], res[:, t, :], ALU.add).then_inc(combined, 1)
            eng.wait_ge(combined, 2 + NT // 2)
            add_shared(3, 3, range(TT))


def kernel(x, ctx_2048, mask_BxS2_ff1, **w):
    import concourse.bacc as bacc
    from concourse.bass_utils import run_bass_kernel_spmd

    def f(name):
        return np.asarray(w[name])

    def tiles(m):
        return np.asarray(m).reshape(-1, P, m.shape[-1]).transpose(1, 0, 2)

    def cols(m):
        return tiles(m).reshape(P, -1)

    feat = np.zeros((P, 2, 8 * FD), np.float32)
    for h in range(8):
        for i, name in enumerate(("L0_xattn_Wkf", "L0_xattn_Wqf")):
            feat[HD * h:HD * h + HD, i, FD * h:FD * h + FD] = f(name).T
    attw = np.stack([cols(f("L0_xattn_Wk").T), cols(f("L0_xattn_Wv").T), cols(f("L0_xattn_Wq").T),
                     feat[:, 0], feat[:, 1], cols(f("L0_xattn_Wo").T)])

    def chunks(w1, w2):
        one, two = tiles(w1), tiles(w2)
        return np.stack([one[:, :, 0:512].reshape(P, CH), one[:, :, 512:1024].reshape(P, CH),
                         two[:, 0:4].reshape(P, CH), two[:, 4:8].reshape(P, CH)])

    def adapter(wd, wu):
        side = np.zeros((P, D), np.float32)
        side[0:AP3] = np.concatenate([wu, wu, wu], 0)
        return np.concatenate([cols(wd), side], 1)

    w1, w2, wd, wu = (f("L0_ffn_" + n) for n in ("w1", "w2", "wd", "wu"))
    wch = np.stack([chunks(f("L0_ffn_sw1"), f("L0_ffn_sw2"))] + [chunks(w1[e], w2[e]) for e in range(E)])
    adw = np.stack([adapter(f("L0_ffn_swd"), f("L0_ffn_swu"))] + [adapter(wd[e], wu[e]) for e in range(E)])
    gate = np.zeros((D, GP), np.float32)
    gate[:, 0:E] = f("L0_ffn_gate_w")
    vec = lambda m: np.asarray(m).reshape(-1, P).T
    bexp = np.stack([np.concatenate([vec(f("L0_ffn_b1")[e]), vec(f("L0_ffn_b2")[e])], 1) for e in range(E)])
    bias = [vec(f("L0_ffn_sb1")), np.zeros((P, 2), np.float32), vec(f("L0_xattn_bq")), vec(f("L0_xattn_bk")), vec(mask_BxS2_ff1)]
    bcol = np.concatenate(bias, 1)
    brow = np.stack([f("L0_xattn_bv"), f("L0_xattn_bo"), f("L0_ffn_sb2")])

    r = np.arange(P)
    cst = np.zeros((P, CCOLS), np.float32)
    cst[:, C_ID:C_ID + P] = np.eye(P)
    cst[:, C_TRI:C_TRI + P] = r[:, None] < r[None, :]
    cst[:, C_ONE:C_ONE + P] = 1.0
    cst[:, C_EXP:C_EXP + E] = np.arange(E)
    cst[:, C_BASE:C_BASE + 2 * NT] = np.tile([0, CAP], NT)
    dest = (np.arange(NT)[None, :, None] * P + r[:, None, None] + T * np.arange(2)[None, None, :]).astype(np.int32)
    pre = np.zeros((P, ROW), np.int32)
    pre[:, D:] = NOWHERE + r[:, None]

    nc = bacc.Bacc("TRN2", target_bir_lowering=False, num_devices=1)
    arrays, args = {}, []
    for name, arr in (("x", x), ("ctx", ctx_2048), ("attw", attw), ("wch", wch), ("adw", adw), ("gate", tiles(gate)),
                      ("bcol", bcol), ("bexp", bexp), ("brow", brow), ("cst", cst), ("dest", dest), ("pre", pre.view(np.float32))):
        arrays["in_" + name] = np.ascontiguousarray(arr)
        args.append(nc.dram_tensor("in_" + name, arr.shape, mybir.dt.from_np(arrays["in_" + name].dtype),
                                   kind="ExternalInput").ap())
    args.append(nc.dram_tensor("xbuf", (E * SLOTS, ROW), F32, kind="Internal").ap())
    args.append(nc.dram_tensor("ybuf", (2 * T, D), F32, kind="Internal").ap())
    args.append(nc.dram_tensor("out", (B, S, D), F32, kind="ExternalOutput").ap())
    build_program(nc, *args)
    r = run_bass_kernel_spmd(nc, [arrays], core_ids=[0])
    return r.results[0]["out"]
```
